# Optimizing a Trainium2 kernel written in Bass

```python
import numpy as np
import jax
import jax.numpy as jnp

def _softmax(x, axis=-1):
    return jax.nn.softmax(x, axis=axis)

def _gelu(x):
    return jax.nn.gelu(x, approximate=True)

def _silu(x):
    return jax.nn.silu(x)

def _sigmoid(x):
    return jax.nn.sigmoid(x)

def _layernorm(x, axis=-1, eps=1e-05):
    m = jnp.mean(x, axis=axis, keepdims=True)
    v = jnp.var(x, axis=axis, keepdims=True)
    return (x - m) / jnp.sqrt(v + eps)

def _scatter_add(tgt, idx, src, axis=0):
    return tgt.at[idx].add(src)

def _segment_sum(src, seg, n):
    return jax.ops.segment_sum(src, seg, n)
kernel_name = 'mk_flamingo_gated_d4_seqx_r8_0909bc'

def setup_inputs(seed: int=0):
    np.random.seed(seed)
    _w = jnp.asarray

    def _rec_inputs():
        import jax
        import jax.numpy as jnp
        _rk = jax.random.key(seed)
        x = -0.0005207 + 1.001 * jax.random.normal(jax.random.fold_in(_rk, 1), (2, 256, 256), jnp.float32)
        _lenS = 256 - jax.random.randint(jax.random.fold_in(_rk, 7), (2,), 0, max(1, 256 // 4) + 1, jnp.int32)
        _lenS2 = 512 - jax.random.randint(jax.random.fold_in(_rk, 8), (2,), 0, max(1, 512 // 4) + 1, jnp.int32)
        _ctx_2048P = jax.random.normal(jax.random.fold_in(_rk, 12), (2, 16, 256), jnp.float32)
        _ctx_2048c = jax.random.dirichlet(jax.random.fold_in(_rk, 512), 0.3 * jnp.ones((16,), jnp.float32), (2, 512))
        _ctx_2048t = jnp.einsum('bsk,bkd->bsd', _ctx_2048c, _ctx_2048P)
        _ctx_2048t = _ctx_2048t * jax.lax.rsqrt(jnp.mean(jnp.square(_ctx_2048t)) + 1e-12) * 0.953939
        ctx_2048 = -5.72187e-05 + 0.999849 * (_ctx_2048t + 0.3 * jax.random.normal(jax.random.fold_in(_rk, 612), (2, 512, 256), jnp.float32))
        _validS = jnp.arange(256)[None, :] < _lenS[:, None]
        _validS2 = jnp.arange(512)[None, :] < _lenS2[:, None]
        _causal = jnp.tril(jnp.ones((256, 256), dtype=bool))
        mask_BxSx4224_bf0 = jnp.logical_not(jnp.ones((2, 256, 528), dtype=bool))
        mask_BxS2_ff1 = jnp.where(jnp.ones((2, 512), dtype=bool), 1.0, 0.0).astype(jnp.float32)
        _g = jax.random.normal(jax.random.fold_in(_rk, 9001), (2, 4), jnp.float32)
        _g = jnp.sign(_g) * jnp.maximum(jnp.abs(_g), 1.0) + (_g == 0) * 1.0
        g_xattn = _g[0]
        g_ffn = _g[1]
        return (x, ctx_2048, mask_BxSx4224_bf0, mask_BxS2_ff1, g_xattn, g_ffn)
    x, ctx_2048, mask_BxSx4224_bf0, mask_BxS2_ff1, g_xattn, g_ffn = _rec_inputs()

    def _L0_xattn_setup():
        import jax, jax.numpy as jnp
        import numpy as np
        import math
        DIM = 256
        B, Q_LEN, KV_LEN = (8, 128, 512)
        key = jax.random.key(seed)
        ks = jax.random.split(key, 8)
        x = jax.random.normal(ks[0], (B, Q_LEN, DIM), dtype=jnp.float32)
        mask = jnp.zeros((B, Q_LEN, KV_LEN + Q_LEN), dtype=bool)
        k_cache = jax.random.normal(ks[1], (B, KV_LEN, DIM), dtype=jnp.float32)
        v_cache = jax.random.normal(ks[2], (B, KV_LEN, DIM), dtype=jnp.float32)
        scale = 1.0 / math.sqrt(DIM)
        wq = jax.random.normal(ks[3], (DIM, DIM), dtype=jnp.float32) * scale
        wk = jax.random.normal(ks[4], (DIM, DIM), dtype=jnp.float32) * scale
        wv = jax.random.normal(ks[5], (DIM, DIM), dtype=jnp.float32) * scale
        wo = jax.random.normal(ks[6], (DIM, DIM), dtype=jnp.float32) * scale
        return {'x': x, 'mask': mask, 'k_cache': k_cache, 'v_cache': v_cache, 'wq': wq, 'wk': wk, 'wv': wv, 'wo': wo}
    _L0_xattn_all = _L0_xattn_setup()
    _L0_xattn_in = {k: v for k, v in _L0_xattn_all.items() if k in ('wq', 'wk', 'wv', 'wo')}
    del _L0_xattn_all

    def _L0_ffn_setup():
        import jax, jax.numpy as jnp
        import numpy as np
        BLOCK_SIZE = 32
        HIDDEN_SIZE = 256
        MLP_DIM = 2048
        NVFP4_LUT = jnp.array([0.0, 0.5, 1.0, 1.5, 2.0, 3.0, 4.0, 6.0, 0.0, -0.5, -1.0, -1.5, -2.0, -3.0, -4.0, -6.0], dtype=jnp.float32)

        def dequant_nvfp4(W_packed, scales, block=BLOCK_SIZE):
            N = W_packed.shape[0]
            low = W_packed & 15
            high = W_packed >> 4 & 15
            idx = jnp.stack([low, high], axis=-1).reshape(N, -1)
            vals = NVFP4_LUT[idx]
            K = vals.shape[1]
            vals = vals.reshape(N, K // block, block) * scales[:, :, None]
            return vals.reshape(N, K)
        key = jax.random.key(seed)
        ks = jax.random.split(key, 7)
        x = jax.random.normal(ks[0], (4, 32, HIDDEN_SIZE), dtype=jnp.float32)
        gate_W_packed = jax.random.randint(ks[1], (MLP_DIM, HIDDEN_SIZE // 2), 0, 32, dtype=jnp.int32)
        gate_scales = jax.random.uniform(ks[2], (MLP_DIM, HIDDEN_SIZE // BLOCK_SIZE), dtype=jnp.float32) * 0.1 + 0.001
        up_W_packed = jax.random.randint(ks[3], (MLP_DIM, HIDDEN_SIZE // 2), 0, 32, dtype=jnp.int32)
        up_scales = jax.random.uniform(ks[4], (MLP_DIM, HIDDEN_SIZE // BLOCK_SIZE), dtype=jnp.float32) * 0.1 + 0.001
        down_W_packed = jax.random.randint(ks[5], (HIDDEN_SIZE, MLP_DIM // 2), 0, 32, dtype=jnp.int32)
        down_scales = jax.random.uniform(ks[6], (HIDDEN_SIZE, MLP_DIM // BLOCK_SIZE), dtype=jnp.float32) * 0.1 + 0.001
        return {'x': x, 'gate_W_packed': gate_W_packed, 'gate_scales': gate_scales, 'up_W_packed': up_W_packed, 'up_scales': up_scales, 'down_W_packed': down_W_packed, 'down_scales': down_scales}
    _L0_ffn_all = _L0_ffn_setup()
    _L0_ffn_in = {k: v for k, v in _L0_ffn_all.items() if k in ('gate_W_packed', 'gate_scales', 'up_W_packed', 'up_scales', 'down_W_packed', 'down_scales')}
    del _L0_ffn_all

    def _L1_xattn_setup():
        import math
        import jax, jax.numpy as jnp
        import numpy as np
        HEADS = 16
        MASKED_BIAS = -10000.0

        def _mha(q, k, v):
            B, Sq, D = q.shape
            Sk = k.shape[-2]
            hd = D // HEADS
            qh = q.reshape(B, Sq, HEADS, hd).transpose(0, 2, 1, 3)
            kh = k.reshape(B, Sk, HEADS, hd).transpose(0, 2, 1, 3)
            vh = v.reshape(B, Sk, HEADS, hd).transpose(0, 2, 1, 3)
            scores = jnp.einsum('bhqd,bhkd->bhqk', qh, kh) / math.sqrt(hd)
            qi = jnp.arange(Sq)[:, None] + (Sk - Sq)
            ki = jnp.arange(Sk)[None, :]
            causal = ki <= qi
            scores = jnp.where(causal[None, None], scores, jnp.asarray(MASKED_BIAS, scores.dtype))
            attn = jax.nn.softmax(scores, axis=-1)
            out = jnp.einsum('bhqk,bhkd->bhqd', attn, vh)
            return out.transpose(0, 2, 1, 3).reshape(B, Sq, D)
        key = jax.random.key(seed)
        kq, kk, kv = jax.random.split(key, 3)
        B, S, D = (4, 128, 256)
        q = jax.random.normal(kq, (B, S, D), dtype=jnp.float32)
        k = jax.random.normal(kk, (B, S, D), dtype=jnp.float32)
        v = jax.random.normal(kv, (B, S, D), dtype=jnp.float32)
        return {'q': q, 'k': k, 'v': v}
    _L1_xattn_all = _L1_xattn_setup()
    _L1_xattn_in = {k: v for k, v in _L1_xattn_all.items() if k in ()}
    del _L1_xattn_all

    def _L1_ffn_setup():
        import jax, jax.numpy as jnp
        import numpy as np
        N_EXPERTS = 8
        TOP_K = 2
        N_GROUP = 4
        TOPK_GROUP = 2
        ROUTED_SCALE = 1.0

        def _group_limited_topk(scores):
            T, N = scores.shape
            E = N // N_GROUP
            group_scores = scores.reshape(T, N_GROUP, E).max(axis=-1)
            _, gidx = jax.lax.top_k(group_scores, TOPK_GROUP)
            gmask = jax.nn.one_hot(gidx, N_GROUP, dtype=scores.dtype).sum(1)
            smask = jnp.repeat(gmask, E, axis=1)
            masked = jnp.where(smask > 0, scores, jnp.zeros((), scores.dtype))
            topk_w, topk_i = jax.lax.top_k(masked, TOP_K)
            return (topk_w, topk_i)
        key = jax.random.key(seed)
        ks = jax.random.split(key, 8)
        B, S, H, F, FS, N = (2, 128, 256, 176, 352, N_EXPERTS)
        std = jnp.float32(0.02)
        return {'hidden_states': jax.random.normal(ks[0], (B, S, H), jnp.float32), 'gate_weight': jax.random.normal(ks[1], (N, H), jnp.float32) * std, 'gate_w': jax.random.normal(ks[2], (N, F, H), jnp.float32) * std, 'up_w': jax.random.normal(ks[3], (N, F, H), jnp.float32) * std, 'down_w': jax.random.normal(ks[4], (N, H, F), jnp.float32) * std, 'sh_gate_w': jax.random.normal(ks[5], (FS, H), jnp.float32) * std, 'sh_up_w': jax.random.normal(ks[6], (FS, H), jnp.float32) * std, 'sh_down_w': jax.random.normal(ks[7], (H, FS), jnp.float32) * std}
    _L1_ffn_all = _L1_ffn_setup()
    _L1_ffn_in = {k: v for k, v in _L1_ffn_all.items() if k in ('gate_weight', 'gate_w', 'up_w', 'down_w', 'sh_gate_w', 'sh_up_w', 'sh_down_w')}
    del _L1_ffn_all

    def _L2_xattn_setup():
        import jax, jax.numpy as jnp
        import numpy as np
        H = 256
        NH = 16
        HD = H // NH
        FD = 64
        key = jax.random.key(seed)
        ks = jax.random.split(key, 12)
        B, S = (4, 512)
        s = 1.0 / np.sqrt(H)
        sf = 1.0 / np.sqrt(HD)
        return {'query': jax.random.normal(ks[0], (B, S, H), jnp.float32), 'key': jax.random.normal(ks[1], (B, S, H), jnp.float32), 'value': jax.random.normal(ks[2], (B, S, H), jnp.float32), 'attention_mask': jnp.ones((B, S), jnp.float32), 'Wq': jax.random.normal(ks[3], (H, H), jnp.float32) * s, 'bq': jnp.zeros((H,), jnp.float32), 'Wk': jax.random.normal(ks[4], (H, H), jnp.float32) * s, 'bk': jnp.zeros((H,), jnp.float32), 'Wv': jax.random.normal(ks[5], (H, H), jnp.float32) * s, 'bv': jnp.zeros((H,), jnp.float32), 'Wqf': jax.random.normal(ks[6], (FD, HD), jnp.float32) * sf, 'Wkf': jax.random.normal(ks[7], (FD, HD), jnp.float32) * sf, 'Wo': jax.random.normal(ks[8], (H, H), jnp.float32) * s, 'bo': jnp.zeros((H,), jnp.float32)}
    _L2_xattn_all = _L2_xattn_setup()
    _L2_xattn_in = {k: v for k, v in _L2_xattn_all.items() if k in ('Wq', 'bq', 'Wk', 'bk', 'Wv', 'bv', 'Wqf', 'Wkf', 'Wo', 'bo')}
    del _L2_xattn_all

    def _L2_ffn_setup():
        import jax, jax.numpy as jnp
        import numpy as np
        B, S, D = (2, 256, 256)
        H, HD = (16, 128)
        E, K, I = (16, 6, 176)
        SI = 352
        EPS = 1e-06

        def rmsnorm(x, w):
            v = jnp.mean(jnp.square(x), axis=-1, keepdims=True)
            return x * jax.lax.rsqrt(v + EPS) * w
        key = jax.random.key(seed)
        ks = jax.random.split(key, 14)
        s = 0.02
        return {'hidden_states': jax.random.normal(ks[0], (B, S, D), jnp.float32), 'ln1_w': jnp.ones((D,), jnp.float32), 'ln2_w': jnp.ones((D,), jnp.float32), 'wq': jax.random.normal(ks[1], (D, H * HD), jnp.float32) * s, 'wk': jax.random.normal(ks[2], (D, H * HD), jnp.float32) * s, 'wv': jax.random.normal(ks[3], (D, H * HD), jnp.float32) * s, 'wo': jax.random.normal(ks[4], (H * HD, D), jnp.float32) * s, 'gate_w': jax.random.normal(ks[5], (E, D), jnp.float32) * s, 'eg_w': jax.random.normal(ks[6], (E, I, D), jnp.float32) * s, 'eu_w': jax.random.normal(ks[7], (E, I, D), jnp.float32) * s, 'ed_w': jax.random.normal(ks[8], (E, D, I), jnp.float32) * s, 'sg_w': jax.random.normal(ks[9], (SI, D), jnp.float32) * s, 'su_w': jax.random.normal(ks[10], (SI, D), jnp.float32) * s, 'sd_w': jax.random.normal(ks[11], (D, SI), jnp.float32) * s}
    _L2_ffn_all = _L2_ffn_setup()
    _L2_ffn_in = {k: v for k, v in _L2_ffn_all.items() if k in ('ln1_w', 'ln2_w', 'wq', 'wk', 'wv', 'wo', 'gate_w', 'eg_w', 'eu_w', 'ed_w', 'sg_w', 'su_w', 'sd_w')}
    del _L2_ffn_all

    def _L3_xattn_setup():
        import jax, jax.numpy as jnp
        import numpy as np
        EMBED = 256
        HQ = 16
        HK = 4
        D = EMBED // HQ
        KV_DIM = HK * D
        QB = 127.0
        EPS_Q = 1e-05
        EPS_LN = 1e-05

        def bitlinear(x, w, b):
            alpha = jnp.mean(w)
            c = w - alpha
            bw = c + jax.lax.stop_gradient(jnp.sign(c) - c)
            y = jnp.einsum('bnd,od->bno', x, bw) + b
            gamma = jnp.max(jnp.abs(y))
            return jnp.clip(y * QB / (gamma + EPS_Q), -QB + EPS_Q, QB - EPS_Q)
        key = jax.random.key(seed)
        ks = jax.random.split(key, 12)
        B, N = (2, 128)
        s = 0.02
        return {'query': jax.random.normal(ks[0], (B, N, EMBED), jnp.float32), 'key': jax.random.normal(ks[1], (B, N, EMBED), jnp.float32), 'value': jax.random.normal(ks[2], (B, N, EMBED), jnp.float32), 'q_w': jax.random.normal(ks[3], (EMBED, EMBED), jnp.float32) * s, 'q_b': jnp.zeros((EMBED,), jnp.float32), 'k_w': jax.random.normal(ks[4], (KV_DIM, EMBED), jnp.float32) * s, 'k_b': jnp.zeros((KV_DIM,), jnp.float32), 'v_w': jax.random.normal(ks[5], (KV_DIM, EMBED), jnp.float32) * s, 'v_b': jnp.zeros((KV_DIM,), jnp.float32), 'ln_g': jnp.ones((EMBED,), jnp.float32), 'ln_b': jnp.zeros((EMBED,), jnp.float32), 'o_w': jax.random.normal(ks[6], (EMBED, EMBED), jnp.float32) * s, 'o_b': jnp.zeros((EMBED,), jnp.float32)}
    _L3_xattn_all = _L3_xattn_setup()
    _L3_xattn_in = {k: v for k, v in _L3_xattn_all.items() if k in ('q_w', 'q_b', 'k_w', 'k_b', 'v_w', 'v_b', 'ln_g', 'ln_b', 'o_w', 'o_b')}
    del _L3_xattn_all

    def _L3_ffn_setup():
        import jax, jax.numpy as jnp
        import numpy as np
        TOP_K = 2
        EPS = 1e-06
        key = jax.random.key(seed)
        ks = jax.random.split(key, 4)
        B, L, D, E, ED = (2, 256, 256, 8, 256)
        scale_gu = (6.0 / D) ** 0.5
        scale_dn = (6.0 / ED) ** 0.5
        return {'x': jax.random.normal(ks[0], (B, L, D), jnp.float32), 'router_scale': jnp.ones((D,), jnp.float32), 'gate_w': jax.random.normal(ks[1], (D, E), jnp.float32) * D ** (-0.5), 'gate_up': jax.random.uniform(ks[2], (E, D, 2 * ED), jnp.float32, -scale_gu, scale_gu), 'down': jax.random.uniform(ks[3], (E, ED, D), jnp.float32, -scale_dn, scale_dn), 'per_expert_scale': jnp.ones((E,), jnp.float32)}
    _L3_ffn_all = _L3_ffn_setup()
    _L3_ffn_in = {k: v for k, v in _L3_ffn_all.items() if k in ('router_scale', 'gate_w', 'gate_up', 'down', 'per_expert_scale')}
    del _L3_ffn_all
    return {'x': x, 'ctx_2048': ctx_2048, 'mask_BxSx4224_bf0': mask_BxSx4224_bf0, 'mask_BxS2_ff1': mask_BxS2_ff1, 'g_xattn': g_xattn, 'g_ffn': g_ffn, 'L0_xattn_wq': _L0_xattn_in['wq'], 'L0_xattn_wk': _L0_xattn_in['wk'], 'L0_xattn_wv': _L0_xattn_in['wv'], 'L0_xattn_wo': _L0_xattn_in['wo'], 'L0_ffn_gate_W_packed': _L0_ffn_in['gate_W_packed'], 'L0_ffn_gate_scales': _L0_ffn_in['gate_scales'], 'L0_ffn_up_W_packed': _L0_ffn_in['up_W_packed'], 'L0_ffn_up_scales': _L0_ffn_in['up_scales'], 'L0_ffn_down_W_packed': _L0_ffn_in['down_W_packed'], 'L0_ffn_down_scales': _L0_ffn_in['down_scales'], 'L1_ffn_gate_weight': _L1_ffn_in['gate_weight'], 'L1_ffn_gate_w': _L1_ffn_in['gate_w'], 'L1_ffn_up_w': _L1_ffn_in['up_w'], 'L1_ffn_down_w': _L1_ffn_in['down_w'], 'L1_ffn_sh_gate_w': _L1_ffn_in['sh_gate_w'], 'L1_ffn_sh_up_w': _L1_ffn_in['sh_up_w'], 'L1_ffn_sh_down_w': _L1_ffn_in['sh_down_w'], 'L2_xattn_Wq': _L2_xattn_in['Wq'], 'L2_xattn_bq': _L2_xattn_in['bq'], 'L2_xattn_Wk': _L2_xattn_in['Wk'], 'L2_xattn_bk': _L2_xattn_in['bk'], 'L2_xattn_Wv': _L2_xattn_in['Wv'], 'L2_xattn_bv': _L2_xattn_in['bv'], 'L2_xattn_Wqf': _L2_xattn_in['Wqf'], 'L2_xattn_Wkf': _L2_xattn_in['Wkf'], 'L2_xattn_Wo': _L2_xattn_in['Wo'], 'L2_xattn_bo': _L2_xattn_in['bo'], 'L2_ffn_ln1_w': _L2_ffn_in['ln1_w'], 'L2_ffn_ln2_w': _L2_ffn_in['ln2_w'], 'L2_ffn_wq': _L2_ffn_in['wq'], 'L2_ffn_wk': _L2_ffn_in['wk'], 'L2_ffn_wv': _L2_ffn_in['wv'], 'L2_ffn_wo': _L2_ffn_in['wo'], 'L2_ffn_gate_w': _L2_ffn_in['gate_w'], 'L2_ffn_eg_w': _L2_ffn_in['eg_w'], 'L2_ffn_eu_w': _L2_ffn_in['eu_w'], 'L2_ffn_ed_w': _L2_ffn_in['ed_w'], 'L2_ffn_sg_w': _L2_ffn_in['sg_w'], 'L2_ffn_su_w': _L2_ffn_in['su_w'], 'L2_ffn_sd_w': _L2_ffn_in['sd_w'], 'L3_xattn_q_w': _L3_xattn_in['q_w'], 'L3_xattn_q_b': _L3_xattn_in['q_b'], 'L3_xattn_k_w': _L3_xattn_in['k_w'], 'L3_xattn_k_b': _L3_xattn_in['k_b'], 'L3_xattn_v_w': _L3_xattn_in['v_w'], 'L3_xattn_v_b': _L3_xattn_in['v_b'], 'L3_xattn_ln_g': _L3_xattn_in['ln_g'], 'L3_xattn_ln_b': _L3_xattn_in['ln_b'], 'L3_xattn_o_w': _L3_xattn_in['o_w'], 'L3_xattn_o_b': _L3_xattn_in['o_b'], 'L3_ffn_router_scale': _L3_ffn_in['router_scale'], 'L3_ffn_gate_w': _L3_ffn_in['gate_w'], 'L3_ffn_gate_up': _L3_ffn_in['gate_up'], 'L3_ffn_down': _L3_ffn_in['down'], 'L3_ffn_per_expert_scale': _L3_ffn_in['per_expert_scale']}

def reference(x, ctx_2048, mask_BxSx4224_bf0, mask_BxS2_ff1, g_xattn, g_ffn, L0_xattn_wq, L0_xattn_wk, L0_xattn_wv, L0_xattn_wo, L0_ffn_gate_W_packed, L0_ffn_gate_scales, L0_ffn_up_W_packed, L0_ffn_up_scales, L0_ffn_down_W_packed, L0_ffn_down_scales, L1_ffn_gate_weight, L1_ffn_gate_w, L1_ffn_up_w, L1_ffn_down_w, L1_ffn_sh_gate_w, L1_ffn_sh_up_w, L1_ffn_sh_down_w, L2_xattn_Wq, L2_xattn_bq, L2_xattn_Wk, L2_xattn_bk, L2_xattn_Wv, L2_xattn_bv, L2_xattn_Wqf, L2_xattn_Wkf, L2_xattn_Wo, L2_xattn_bo, L2_ffn_ln1_w, L2_ffn_ln2_w, L2_ffn_wq, L2_ffn_wk, L2_ffn_wv, L2_ffn_wo, L2_ffn_gate_w, L2_ffn_eg_w, L2_ffn_eu_w, L2_ffn_ed_w, L2_ffn_sg_w, L2_ffn_su_w, L2_ffn_sd_w, L3_xattn_q_w, L3_xattn_q_b, L3_xattn_k_w, L3_xattn_k_b, L3_xattn_v_w, L3_xattn_v_b, L3_xattn_ln_g, L3_xattn_ln_b, L3_xattn_o_w, L3_xattn_o_b, L3_ffn_router_scale, L3_ffn_gate_w, L3_ffn_gate_up, L3_ffn_down, L3_ffn_per_expert_scale):
    import jax
    import jax.numpy as jnp

    def _L0_xattn_ref(x, mask, k_cache, v_cache, wq, wk, wv, wo):
        import jax, jax.numpy as jnp
        import numpy as np
        import math
        DIM = 256
        B, Q_LEN, KV_LEN = (8, 128, 512)
        q = jnp.einsum('bsd,ed->bse', x, wq)
        k_new = jnp.einsum('bsd,ed->bse', x, wk)
        v_new = jnp.einsum('bsd,ed->bse', x, wv)
        k = jnp.concatenate([k_cache, k_new], axis=1)
        v = jnp.concatenate([v_cache, v_new], axis=1)
        scale = 1.0 / math.sqrt(q.shape[-1])
        scores = jnp.einsum('bqd,bkd->bqk', q, k) * scale
        attn = jax.nn.softmax(scores, axis=-1)
        out = jnp.einsum('bqk,bkd->bqd', attn, v)
        return jnp.einsum('bqd,ed->bqe', out, wo)

    def _L0_ffn_ref(x, gate_W_packed, gate_scales, up_W_packed, up_scales, down_W_packed, down_scales):
        import jax, jax.numpy as jnp
        import numpy as np
        BLOCK_SIZE = 32
        HIDDEN_SIZE = 256
        MLP_DIM = 2048
        NVFP4_LUT = jnp.array([0.0, 0.5, 1.0, 1.5, 2.0, 3.0, 4.0, 6.0, 0.0, -0.5, -1.0, -1.5, -2.0, -3.0, -4.0, -6.0], dtype=jnp.float32)

        def dequant_nvfp4(W_packed, scales, block=BLOCK_SIZE):
            N = W_packed.shape[0]
            low = W_packed & 15
            high = W_packed >> 4 & 15
            idx = jnp.stack([low, high], axis=-1).reshape(N, -1)
            vals = NVFP4_LUT[idx]
            K = vals.shape[1]
            vals = vals.reshape(N, K // block, block) * scales[:, :, None]
            return vals.reshape(N, K)
        B, S, H = x.shape
        xt = x.reshape(B * S, H)
        Wg = dequant_nvfp4(gate_W_packed, gate_scales)
        Wu = dequant_nvfp4(up_W_packed, up_scales)
        Wd = dequant_nvfp4(down_W_packed, down_scales)
        gate = jnp.einsum('th,nh->tn', xt, Wg)
        up = jnp.einsum('th,nh->tn', xt, Wu)
        gelu = jnp.tanh(0.7978845608028654 * (gate + 0.044715 * gate ** 3)) * gate * 0.5 + gate * 0.5
        inter = gelu * up
        out = jnp.einsum('tn,hn->th', inter, Wd)
        return out.reshape(B, S, H)

    def _L1_xattn_ref(q, k, v):
        import math
        import jax, jax.numpy as jnp
        import numpy as np
        HEADS = 16
        MASKED_BIAS = -10000.0

        def _mha(q, k, v):
            B, Sq, D = q.shape
            Sk = k.shape[-2]
            hd = D // HEADS
            qh = q.reshape(B, Sq, HEADS, hd).transpose(0, 2, 1, 3)
            kh = k.reshape(B, Sk, HEADS, hd).transpose(0, 2, 1, 3)
            vh = v.reshape(B, Sk, HEADS, hd).transpose(0, 2, 1, 3)
            scores = jnp.einsum('bhqd,bhkd->bhqk', qh, kh) / math.sqrt(hd)
            qi = jnp.arange(Sq)[:, None] + (Sk - Sq)
            ki = jnp.arange(Sk)[None, :]
            causal = ki <= qi
            scores = jnp.where(causal[None, None], scores, jnp.asarray(MASKED_BIAS, scores.dtype))
            attn = jax.nn.softmax(scores, axis=-1)
            out = jnp.einsum('bhqk,bhkd->bhqd', attn, vh)
            return out.transpose(0, 2, 1, 3).reshape(B, Sq, D)
        return _mha(q, k, v)

    def _L1_ffn_ref(hidden_states, gate_weight, gate_w, up_w, down_w, sh_gate_w, sh_up_w, sh_down_w):
        import jax, jax.numpy as jnp
        import numpy as np
        N_EXPERTS = 8
        TOP_K = 2
        N_GROUP = 4
        TOPK_GROUP = 2
        ROUTED_SCALE = 1.0

        def _group_limited_topk(scores):
            T, N = scores.shape
            E = N // N_GROUP
            group_scores = scores.reshape(T, N_GROUP, E).max(axis=-1)
            _, gidx = jax.lax.top_k(group_scores, TOPK_GROUP)
            gmask = jax.nn.one_hot(gidx, N_GROUP, dtype=scores.dtype).sum(1)
            smask = jnp.repeat(gmask, E, axis=1)
            masked = jnp.where(smask > 0, scores, jnp.zeros((), scores.dtype))
            topk_w, topk_i = jax.lax.top_k(masked, TOP_K)
            return (topk_w, topk_i)
        B, S, H = hidden_states.shape
        h = hidden_states.reshape(-1, H)
        logits = h.astype(jnp.float32) @ gate_weight.astype(jnp.float32).T
        scores = jax.nn.softmax(logits, axis=-1)
        topk_w, topk_i = _group_limited_topk(scores)
        topk_w = (topk_w * ROUTED_SCALE).astype(h.dtype)
        wmat = (jax.nn.one_hot(topk_i, N_EXPERTS, dtype=topk_w.dtype) * topk_w[..., None]).sum(axis=1)
        g = jnp.einsum('th,nfh->ntf', h, gate_w)
        u = jnp.einsum('th,nfh->ntf', h, up_w)
        e = jnp.einsum('ntf,nhf->nth', jax.nn.silu(g) * u, down_w)
        routed = jnp.einsum('nth,tn->th', e, wmat)
        sg = h @ sh_gate_w.T
        su = h @ sh_up_w.T
        shared = jax.nn.silu(sg) * su @ sh_down_w.T
        return (routed + shared).reshape(B, S, H)

    def _L2_xattn_ref(query, key, value, attention_mask, Wq, bq, Wk, bk, Wv, bv, Wqf, Wkf, Wo, bo):
        import jax, jax.numpy as jnp
        import numpy as np
        H = 256
        NH = 16
        HD = H // NH
        FD = 64
        B, Sq, _ = query.shape
        Sk = key.shape[1]

        def heads(x, W, b, S):
            return (x @ W.T + b).reshape(B, S, NH, HD).transpose(0, 2, 1, 3)
        q = heads(query, Wq, bq, Sq)
        k = heads(key, Wk, bk, Sk)
        v = heads(value, Wv, bv, Sk)
        q_prime = jax.nn.relu(jnp.einsum('bhnd,fd->bhnf', q, Wqf))
        k_prime = jax.nn.relu(jnp.einsum('bhnd,fd->bhnf', k, Wkf))
        k_prime = k_prime * attention_mask[:, None, :, None]
        kv = jnp.einsum('bhnf,bhne->bhfe', k_prime, v)
        qkv = jnp.einsum('bhmf,bhfe->bhme', q_prime, kv)
        k_sum = jnp.sum(k_prime, axis=2)
        qk_sum = jnp.einsum('bhmf,bhf->bhm', q_prime, k_sum)[..., None]
        out = qkv / (qk_sum + 1e-08)
        out = out.transpose(0, 2, 1, 3).reshape(B, Sq, H)
        return out @ Wo.T + bo

    def _L2_ffn_ref(hidden_states, ln1_w, ln2_w, wq, wk, wv, wo, gate_w, eg_w, eu_w, ed_w, sg_w, su_w, sd_w):
        import jax, jax.numpy as jnp
        import numpy as np
        B, S, D = (2, 256, 256)
        H, HD = (16, 128)
        E, K, I = (16, 6, 176)
        SI = 352
        EPS = 1e-06

        def rmsnorm(x, w):
            v = jnp.mean(jnp.square(x), axis=-1, keepdims=True)
            return x * jax.lax.rsqrt(v + EPS) * w
        b, s, d = hidden_states.shape
        x = hidden_states
        h = rmsnorm(x, ln1_w)
        q = (h @ wq).reshape(b, s, H, HD)
        k = (h @ wk).reshape(b, s, H, HD)
        v = (h @ wv).reshape(b, s, H, HD)
        scores = jnp.einsum('bqhd,bkhd->bhqk', q, k) / np.sqrt(HD).astype(np.float32)
        causal = jnp.tril(jnp.ones((s, s), bool))
        scores = jnp.where(causal, scores, jnp.float32(-1000000000.0))
        attn = jax.nn.softmax(scores, axis=-1)
        ao = jnp.einsum('bhqk,bkhd->bqhd', attn, v).reshape(b, s, H * HD) @ wo
        x = x + ao
        h = rmsnorm(x, ln2_w)
        t = h.reshape(-1, d)
        T = t.shape[0]
        logits = t @ gate_w.T
        probs = jax.nn.softmax(logits, axis=-1)
        topv, topi = jax.lax.top_k(probs, K)
        topv = topv / jnp.sum(topv, axis=-1, keepdims=True)
        cw = jnp.zeros((T, E), t.dtype).at[jnp.arange(T)[:, None], topi].add(topv)
        g = jnp.einsum('td,eid->eti', t, eg_w)
        u = jnp.einsum('td,eid->eti', t, eu_w)
        hh = jax.nn.silu(g) * u
        routed = jnp.einsum('eti,edi,te->td', hh, ed_w, cw)
        shared = jax.nn.silu(t @ sg_w.T) * (t @ su_w.T) @ sd_w.T
        out = x + (routed + shared).reshape(b, s, d)
        return out

    def _L3_xattn_ref(query, key, value, q_w, q_b, k_w, k_b, v_w, v_b, ln_g, ln_b, o_w, o_b):
        import jax, jax.numpy as jnp
        import numpy as np
        EMBED = 256
        HQ = 16
        HK = 4
        D = EMBED // HQ
        KV_DIM = HK * D
        QB = 127.0
        EPS_Q = 1e-05
        EPS_LN = 1e-05

        def bitlinear(x, w, b):
            alpha = jnp.mean(w)
            c = w - alpha
            bw = c + jax.lax.stop_gradient(jnp.sign(c) - c)
            y = jnp.einsum('bnd,od->bno', x, bw) + b
            gamma = jnp.max(jnp.abs(y))
            return jnp.clip(y * QB / (gamma + EPS_Q), -QB + EPS_Q, QB - EPS_Q)
        q = bitlinear(query, q_w, q_b)
        k = bitlinear(key, k_w, k_b)
        v = bitlinear(value, v_w, v_b)
        B, N, _ = q.shape
        S = k.shape[1]
        G = HQ // HK
        qh = q.reshape(B, N, HQ, D).transpose(0, 2, 1, 3)
        kh = k.reshape(B, S, HK, D).transpose(0, 2, 1, 3)
        vh = v.reshape(B, S, HK, D).transpose(0, 2, 1, 3)
        qg = qh.reshape(B, HK, G, N, D).transpose(0, 2, 1, 3, 4)
        scale = jnp.sqrt(jnp.asarray(D, q.dtype))
        sim = jnp.einsum('bghnd,bhsd->bghns', qg, kh)
        attn = jax.nn.softmax(sim / scale, axis=-1)
        out = jnp.einsum('bghns,bhsd->bghnd', attn, vh)
        x = out.transpose(0, 3, 2, 1, 4).reshape(B, N, HQ * D)
        mu = jnp.mean(x, axis=-1, keepdims=True)
        var = jnp.var(x, axis=-1, keepdims=True)
        x = (x - mu) / jnp.sqrt(var + EPS_LN) * ln_g + ln_b
        return bitlinear(x, o_w, o_b)

    def _L3_ffn_ref(x, router_scale, gate_w, gate_up, down, per_expert_scale):
        import jax, jax.numpy as jnp
        import numpy as np
        TOP_K = 2
        EPS = 1e-06
        B, L, D = x.shape
        E = gate_up.shape[0]
        h = x * jax.lax.rsqrt(jnp.mean(x * x, axis=-1, keepdims=True) + EPS)
        h = h * D ** (-0.5) * router_scale
        logits = (h @ gate_w).astype(jnp.float32)
        probs = jax.nn.softmax(logits, axis=-1)
        w, idx = jax.lax.top_k(probs, TOP_K)
        w = w / jnp.clip(jnp.sum(w, axis=-1, keepdims=True), 1e-12)
        w = w.astype(x.dtype)
        N = B * L
        xf = x.reshape(N, D)
        idxf = idx.reshape(N, TOP_K)
        wf = w.reshape(N, TOP_K)
        combine = jnp.zeros((N, E), x.dtype).at[jnp.arange(N)[:, None], idxf].add(wf)
        hh = jnp.einsum('nd,edf->nef', xf, gate_up)
        gate, up = jnp.split(hh, 2, axis=-1)
        act = jax.nn.gelu(gate, approximate=False) * up
        y = jnp.einsum('nef,efd->ned', act, down)
        out = jnp.einsum('ne,ned->nd', combine * per_expert_scale, y)
        return out.reshape(B, L, D)
    x = x + jnp.tanh(g_xattn[0]) * _L0_xattn_ref(_layernorm(x, axis=-1), mask_BxSx4224_bf0, ctx_2048, ctx_2048, L0_xattn_wq, L0_xattn_wk, L0_xattn_wv, L0_xattn_wo)
    x = x + jnp.tanh(g_ffn[0]) * _L0_ffn_ref(_layernorm(x, axis=-1), L0_ffn_gate_W_packed, L0_ffn_gate_scales, L0_ffn_up_W_packed, L0_ffn_up_scales, L0_ffn_down_W_packed, L0_ffn_down_scales)
    x = x + jnp.tanh(g_xattn[1]) * _L1_xattn_ref(_layernorm(x, axis=-1), ctx_2048, ctx_2048)
    x = x + jnp.tanh(g_ffn[1]) * _L1_ffn_ref(_layernorm(x, axis=-1), L1_ffn_gate_weight, L1_ffn_gate_w, L1_ffn_up_w, L1_ffn_down_w, L1_ffn_sh_gate_w, L1_ffn_sh_up_w, L1_ffn_sh_down_w)
    x = x + jnp.tanh(g_xattn[2]) * _L2_xattn_ref(_layernorm(x, axis=-1), ctx_2048, ctx_2048, mask_BxS2_ff1, L2_xattn_Wq, L2_xattn_bq, L2_xattn_Wk, L2_xattn_bk, L2_xattn_Wv, L2_xattn_bv, L2_xattn_Wqf, L2_xattn_Wkf, L2_xattn_Wo, L2_xattn_bo)
    x = x + jnp.tanh(g_ffn[2]) * _L2_ffn_ref(_layernorm(x, axis=-1), L2_ffn_ln1_w, L2_ffn_ln2_w, L2_ffn_wq, L2_ffn_wk, L2_ffn_wv, L2_ffn_wo, L2_ffn_gate_w, L2_ffn_eg_w, L2_ffn_eu_w, L2_ffn_ed_w, L2_ffn_sg_w, L2_ffn_su_w, L2_ffn_sd_w)
    x = x + jnp.tanh(g_xattn[3]) * _L3_xattn_ref(_layernorm(x, axis=-1), ctx_2048, ctx_2048, L3_xattn_q_w, L3_xattn_q_b, L3_xattn_k_w, L3_xattn_k_b, L3_xattn_v_w, L3_xattn_v_b, L3_xattn_ln_g, L3_xattn_ln_b, L3_xattn_o_w, L3_xattn_o_b)
    x = x + jnp.tanh(g_ffn[3]) * _L3_ffn_ref(_layernorm(x, axis=-1), L3_ffn_router_scale, L3_ffn_gate_w, L3_ffn_gate_up, L3_ffn_down, L3_ffn_per_expert_scale)
    return x

_drawn_inputs = setup_inputs


def setup_inputs(seed=0):
    import zlib

    import numpy as np

    out = dict(_drawn_inputs(seed))
    spreads = {'L2_xattn_bq': (0.0, 0.8),
     'L2_xattn_bk': (0.0, 0.8),
     'L2_xattn_bv': (0.0, 0.1),
     'L2_xattn_bo': (0.0, 0.1),
     'L2_ffn_ln1_w': (1.0, 0.6),
     'L2_ffn_ln2_w': (1.0, 0.6),
     'L3_xattn_q_b': (0.0, 0.1),
     'L3_xattn_k_b': (0.0, 0.8),
     'L3_xattn_v_b': (0.0, 0.8),
     'L3_xattn_ln_g': (1.0, 0.2),
     'L3_xattn_ln_b': (0.0, 0.1),
     'L3_xattn_o_b': (0.0, 0.8),
     'L3_ffn_router_scale': (1.0, 0.6),
     'L3_ffn_per_expert_scale': (1.0, 0.6)}
    factors = {'g_ffn': 8.0,
     'L1_ffn_gate_weight': 8.0,
     'L1_ffn_gate_w': 7.849,
     'L1_ffn_up_w': 8.0,
     'L1_ffn_down_w': 8.0,
     'L2_ffn_wq': 8.0,
     'L2_ffn_wk': 8.0,
     'L2_ffn_gate_w': 7.626,
     'L2_ffn_eg_w': 7.045,
     'L2_ffn_eu_w': 8.0,
     'L2_ffn_ed_w': 8.0,
     'L2_ffn_su_w': 2.701}
    for name, (base, spread) in spreads.items():
        noise = np.random.default_rng([zlib.crc32(name.encode()), seed]).standard_normal(out[name].shape)
        drawn = base * np.exp(spread * noise) if base else spread * noise
        out[name] = jnp.asarray(drawn.astype(out[name].dtype))
    for name, factor in factors.items():
        out[name] = (out[name] * factor).astype(out[name].dtype)
    return out
```

```python
from contextlib import ExitStack

import numpy as np

import concourse.bass as bass
from concourse import mybir

ALU = mybir.AluOpType
ACT = mybir.ActivationFunctionType
AX = mybir.AxisListType
F32 = mybir.dt.float32
F16 = mybir.dt.float16
BF16 = mybir.dt.bfloat16
I32 = mybir.dt.int32
U16 = mybir.dt.uint16

P = 128
B, S, D = 2, 256, 256
CTX = 512
TT = B * S // P
CT = B * CTX // P
KT = D // P
T = B * S
H = 16
HD = D // H
LN_EPS, RMS_EPS = 1e-5, 1e-6
MASKED = -1e30

COLS = ["ln1_w", "ln2_w", "router_scale", "bq", "bk", "ln_g", "ln_b", "q_b", "k_b"]
COL = {n: 2 * i for i, n in enumerate(COLS)}
N_COLS = 2 * len(COLS)
ROWS = [("g_xattn", 4), ("g_ffn", 4), ("bv", D), ("bo", D), ("o_b", D), ("v_b", 64), ("expert_scale", 8)]
ROW, N_ROWS = {}, 0
for _n, _w in ROWS:
    ROW[_n] = N_ROWS
    N_ROWS += _w

FW = 2 * KT * P + D
MOE = {"l1": (14, 8, 176), "l2": (25, 16, 176), "l3": (16, 8, 256)}
MOE_AT = {"l1": 0, "l2": 14, "l3": 39}
MOE_TILES = 55
ONE_BF16 = 0x3F80
SLOTS = 4


class Tally:

    def __init__(self, sem):
        self.sem, self.n = sem, 0

    def up(self, ins):
        ins.then_inc(self.sem, 1)
        self.n += 1
        return self.n


def settle(eng, tally, ins):
    eng.wait_ge(tally.sem, tally.up(ins))


def stage_semaphores(nc, ctx, prefix):
    taken = []

    def sem(name):
        taken.append(nc.alloc_semaphore(name=f"{prefix}_{name}"))
        return taken[-1]

    def give_back():
        nc.clear_and_free_semaphores(taken)
        nc.all_engine_barrier()
    ctx.callback(give_back)
    return sem


class Core:
    pass


def flat(ap):
    return ap.rearrange("p a b -> p (a b)")


def setup_stage(nc, c, d):
    with ExitStack() as ctx:
        sem = stage_semaphores(nc, ctx, "setup")
        loaded, zeroed, masks, gates = sem("loaded"), sem("zeroed"), sem("masks"), sem("gates")
        block = ctx.enter_context(nc.Block(no_gpsimd_drain=True))

        @block.sync
        def _(sp):
            sp.dma_start(c.x[:], d["x"].rearrange("t p n -> p t n")).then_inc(loaded, 16)
            sp.dma_start(c.rows[:], d["rows"].broadcast_to([P, N_ROWS])).then_inc(loaded, 16)
            sp.dma_start(c.cols[:], d["cols"]).then_inc(loaded, 16)
            sp.dma_start(c.ctxT[:], d["ctx_t"].rearrange("k p n -> p k n")).then_inc(loaded, 16)
            sp.dma_start(c.ctx[:], d["ctx"].rearrange("t p n -> p t n")).then_inc(loaded, 16)
            sp.dma_start(c.att_mask[:], d["att_mask"]).then_inc(loaded, 16)
            sp.dma_start(c.routers[:], d["routers"].rearrange("k p n -> p k n")).then_inc(loaded, 16)
            sp.wait_ge(loaded, 112)

        @block.gpsimd
        def _(pool):
            nc.gpsimd.memset(c.ident[:], 0.0).then_inc(zeroed, 1)
            nc.gpsimd.memset(c.ident_bf[:], 0.0).then_inc(zeroed, 1)
            nc.gpsimd.memset(c.mask_q[:], 0.0).then_inc(zeroed, 1)
            nc.gpsimd.memset(c.mask_k[:], 0.0).then_inc(zeroed, 1)
            nc.gpsimd.memset(c.zero_bf[:], 0.0).then_inc(zeroed, 1)
            nc.gpsimd.memset(c.minus_half[:], -0.5).then_inc(zeroed, 1)
            nc.gpsimd.memset(c.weightT[:], 0.0).then_inc(zeroed, 1)
            nc.gpsimd.memset(c.before[:], 1.0).then_inc(zeroed, 1)
            pool.wait_ge(zeroed, 8)
            nc.gpsimd.affine_select(out=c.before[:], in_=c.before[:], compare_op=ALU.is_gt, fill=0.0, base=0,
                                    pattern=[[1, 16], [-1, 16]], channel_multiplier=0).then_inc(masks, 1)
            for m in (c.ident, c.ident_bf):
                nc.gpsimd.affine_select(out=m[:], in_=m[:], compare_op=ALU.not_equal, fill=1.0, base=0,
                                        pattern=[[-1, P]], channel_multiplier=1).then_inc(masks, 1)
            nc.gpsimd.affine_select(out=c.mask_q[:], in_=c.mask_q[:], compare_op=ALU.is_ge, fill=MASKED, base=0,
                                    pattern=[[-1, P]], channel_multiplier=1).then_inc(masks, 1)
            nc.gpsimd.affine_select(out=c.mask_k[:], in_=c.mask_k[:], compare_op=ALU.is_ge, fill=MASKED, base=0,
                                    pattern=[[1, P]], channel_multiplier=-1).then_inc(masks, 1)
            pool.wait_ge(masks, 5)

        @block.scalar
        def _(act):
            act.wait_ge(loaded, 112)
            nc.scalar.activation(c.gate[:], c.rows[:, 0:8], ACT.Tanh).then_inc(gates, 1)
            act.wait_ge(gates, 1)


def norm_stage(nc, c, tag, src, dst, eps, features_out=None, even_odd=False, rms=False, prefetch=None, scale=None, shift=None):
    with ExitStack() as ctx:
        sem = stage_semaphores(nc, ctx, tag)
        stats = ctx.enter_context(nc.sbuf_tensor(f"{tag}_stats", [P, TT, 6], F32))
        moments = ctx.enter_context(nc.sbuf_tensor(f"{tag}_moments", [P, TT, 2], F32))
        var = ctx.enter_context(nc.sbuf_tensor(f"{tag}_var", [P, TT], F32))
        rstd = ctx.enter_context(nc.sbuf_tensor(f"{tag}_rstd", [P, TT], F32))
        square = ctx.enter_context(nc.sbuf_tensor(f"{tag}_square", [P, D], F32))
        own = Tally(sem("own"))
        var_ready, rstd_ready, normed = sem("var_ready"), sem("rstd_ready"), sem("normed")
        turned, act_out, dve_out = sem("turned"), sem("act_out"), sem("dve_out")
        def evacuate(eng, k):
            if scale is None:
                return (eng.copy if eng is nc.scalar else eng.tensor_copy)(features_out[:, k, :], c.ps[:, k, :])
            if eng is nc.scalar:
                bias = 0.0 if shift is None else c.cols[:, COL[shift] + k:COL[shift] + k + 1]
                return eng.activation(features_out[:, k, :], c.ps[:, k, :], ACT.Identity, bias=bias,
                                      scale=c.cols[:, COL[scale] + k:COL[scale] + k + 1])
            if shift is None:
                return eng.tensor_scalar(features_out[:, k, :], c.ps[:, k, :],
                                         c.cols[:, COL[scale] + k:COL[scale] + k + 1], None, ALU.mult)
            return eng.tensor_scalar(features_out[:, k, :], c.ps[:, k, :],
                                     c.cols[:, COL[scale] + k:COL[scale] + k + 1],
                                     c.cols[:, COL[shift] + k:COL[shift] + k + 1], ALU.mult, ALU.add)

        block = ctx.enter_context(nc.Block(no_gpsimd_drain=True))

        if prefetch is not None:
            @block.sync
            def _(sp):
                prefetch(sp)

        @block.gpsimd
        def _(pool):
            pool.wait_ge(var_ready, 1)
            nc.gpsimd.tensor_tensor(rstd[:], var[:], c.minus_half[:, 0:TT], ALU.pow).then_inc(rstd_ready, 1)

        @block.vector
        def _(dve):
            if rms:
                for t in range(TT):
                    last = own.up(nc.vector.tensor_tensor_reduce(
                        out=square[:], in0=src[:, t, :], in1=src[:, t, :], scale=1.0, scalar=0.0,
                        op0=ALU.mult, op1=ALU.add, accum_out=moments[:, t, 1:2]))
                    dve.wait_ge(own.sem, last)
                nc.vector.tensor_scalar(var[:], moments[:, :, 1], 1.0 / D, eps, ALU.mult, ALU.add)\
                    .then_inc(var_ready, 1)
            else:
                for t in range(TT):
                    last = own.up(nc.vector.bn_stats(stats[:, t, :], src[:, t, :]))
                dve.wait_ge(own.sem, last)
                for t in range(TT):
                    last = own.up(nc.vector.bn_aggr(moments[:, t, :], stats[:, t, :]))
                dve.wait_ge(own.sem, last)
                nc.vector.tensor_scalar(var[:], moments[:, :, 1], eps, None, ALU.add).then_inc(var_ready, 1)
            dve.wait_ge(rstd_ready, 1)
            for t in range(TT):
                if rms:
                    nc.vector.tensor_scalar(dst[:, t, :], src[:, t, :], rstd[:, t:t + 1], None, ALU.mult)\
                        .then_inc(normed, 1)
                else:
                    nc.vector.tensor_scalar(dst[:, t, :], src[:, t, :], moments[:, t, 0:1], rstd[:, t:t + 1],
                                            ALU.subtract, ALU.mult).then_inc(normed, 1)
            if features_out is not None:
                dve.wait_ge(turned, 1)
                evacuate(nc.vector, 1).then_inc(dve_out, 1)
                dve.wait_ge(dve_out, 1)
            else:
                dve.wait_ge(normed, TT)

        if features_out is not None:
            @block.tensor
            def _(pe):
                for t in range(TT):
                    pe.wait_ge(normed, t + 1)
                    for k in range(KT):
                        piece = dst[:, t, k::2] if even_odd else dst[:, t, k * P:(k + 1) * P]
                        last = nc.tensor.transpose(c.ps[:, k, t * P:(t + 1) * P], piece, c.ident[:])
                last.then_inc(turned, 1)

            @block.scalar
            def _(act):
                act.wait_ge(turned, 1)
                evacuate(nc.scalar, 0).then_inc(act_out, 1)
                act.wait_ge(act_out, 1)


def l0_attention(nc, c, d):
    SCALE = D ** -0.5
    KEYS = CTX + S
    NK = KEYS // P
    with ExitStack() as ctx:
        def sb(name, shape, dt=F32):
            return ctx.enter_context(nc.sbuf_tensor("l0x_" + name, shape, dt))

        sem = stage_semaphores(nc, ctx, "l0x")
        w = sb("w", [P, 4, KT, D])
        qT, knT, oT = sb("qT", [P, KT, T]), sb("knT", [P, KT, T]), sb("oT", [P, KT, T])
        vn = sb("vn", [P, TT, D])
        probs, probsT = sb("probs", [P, 2, KEYS]), sb("probsT", [P, NK, S])
        top, bias = sb("top", [P, TT]), sb("bias", [P, TT])
        total, inv, factor = sb("total", [P, TT]), sb("inv", [P, TT]), sb("factor", [P, TT])
        loaded, projected, act_kept, dve_kept = sem("loaded"), sem("projected"), sem("act_kept"), sem("dve_kept")
        scored, biased, exped = sem("scored"), sem("biased"), sem("exped")
        turned, mixed, mixed_act, mixed_dve = sem("turned"), sem("mixed"), sem("mixed_act"), sem("mixed_dve")
        turn_act, turn_dve = sem("turn_act"), sem("turn_dve")
        out_ready, added = sem("out_ready"), sem("added")
        own = Tally(sem("own"))
        ps = c.ps
        block = ctx.enter_context(nc.Block(no_gpsimd_drain=True))

        @block.sync
        def _(sp):
            sp.dma_start(w[:], d["l0_w"].rearrange("w k p n -> p w k n")).then_inc(loaded, 16)

        @block.tensor
        def _(pe):
            pe.wait_ge(loaded, 16)
            for which in range(2):
                for m in range(KT):
                    for k in range(KT):
                        last = nc.tensor.matmul(ps[:, 2 * which + m, :], w[:, which, k, m * P:(m + 1) * P],
                                                c.hT[:, k, :], start=k == 0, stop=k == KT - 1)
                    last.then_inc(projected, 1)
            for t in range(TT):
                for k in range(KT):
                    last = nc.tensor.matmul(ps[:, 4 + t, 0:D], c.hT[:, k, t * P:(t + 1) * P], w[:, 2, k, :],
                                            start=k == 0, stop=k == KT - 1)
                last.then_inc(projected, 1)

            def scores(t):
                b, bank = t // 2, 2 * (t % 2)
                if t < 2:
                    pe.wait_ge(act_kept, 2)
                    pe.wait_ge(dve_kept, 2)
                else:
                    pe.wait_ge(exped, t - 1)
                for k in range(KT):
                    nc.tensor.matmul(ps[:, bank, :], qT[:, k, t * P:(t + 1) * P],
                                     c.ctxT[:, k, b * CTX:(b + 1) * CTX], start=k == 0, stop=k == KT - 1)
                for k in range(KT):
                    last = nc.tensor.matmul(ps[:, bank + 1, 0:S], qT[:, k, t * P:(t + 1) * P],
                                            knT[:, k, b * S:(b + 1) * S], start=k == 0, stop=k == KT - 1)
                last.then_inc(scored, 1)

            def turn(t):
                bank = 4 + 2 * (t % 2)
                pe.wait_ge(exped, t + 1)
                if t < 2:
                    pe.wait_ge(act_kept, 4)
                    pe.wait_ge(dve_kept, 4)
                elif t == 2:
                    pe.wait_ge(mixed_act, 1)
                    pe.wait_ge(mixed_dve, 1)
                else:
                    pe.wait_ge(added, 2)
                for j in range(NK):
                    last = nc.tensor.transpose(ps[:, bank + j // 4, (j % 4) * P:(j % 4 + 1) * P],
                                               probs[:, t % 2, j * P:(j + 1) * P], c.ident[:])
                last.then_inc(turned, 1)

            def mix(b):
                pe.wait_ge(turn_act, 2 * b + 2)
                pe.wait_ge(turn_dve, 2 * b + 2)
                for m in range(KT):
                    for j in range(NK):
                        v = c.ctx[:, b * 4 + j, m * P:(m + 1) * P] if j < 4 else \
                            vn[:, b * 2 + j - 4, m * P:(m + 1) * P]
                        last = nc.tensor.matmul(ps[:, 4 + m, 0:S], v, probsT[:, j, :],
                                                start=j == 0, stop=j == NK - 1)
                    last.then_inc(mixed, 1)

            def project_out(t):
                pe.wait_ge(mixed_act, t // 2 + 1)
                pe.wait_ge(mixed_dve, t // 2 + 1)
                for k in range(KT):
                    last = nc.tensor.matmul(ps[:, 6 + t % 2, 0:D], oT[:, k, t * P:(t + 1) * P], w[:, 3, k, :],
                                            start=k == 0, stop=k == KT - 1)
                last.then_inc(out_ready, 1)

            scores(0)
            scores(1)
            turn(0)
            turn(1)
            scores(2)
            scores(3)
            mix(0)
            project_out(0)
            project_out(1)
            turn(2)
            turn(3)
            mix(1)
            project_out(2)
            project_out(3)

        @block.scalar
        def _(act):
            act.wait_ge(projected, 1)
            nc.scalar.copy(qT[:, 0, :], ps[:, 0, :]).then_inc(act_kept, 1)
            act.wait_ge(projected, 3)
            nc.scalar.copy(knT[:, 0, :], ps[:, 2, :]).then_inc(act_kept, 1)
            for t in (0, 2):
                act.wait_ge(projected, 5 + t)
                nc.scalar.copy(vn[:, t, :], ps[:, 4 + t, 0:D]).then_inc(act_kept, 1)

            def exponentials(t):
                bank = 2 * (t % 2)
                act.wait_ge(biased, t + 1)
                if t >= 2:
                    act.wait_ge(turned, t - 1)
                nc.scalar.activation(probs[:, t % 2, :], flat(ps[:, bank:bank + 2, :])[:, 0:KEYS], ACT.Exp,
                                     bias=bias[:, t:t + 1], scale=SCALE, accum_out=total[:, t:t + 1])\
                    .then_inc(exped, 1)

            def keep_turned(t):
                act.wait_ge(turned, t + 1)
                if t == 2:
                    act.wait_ge(mixed, 2)
                nc.scalar.copy(probsT[:, 0:4, (t % 2) * P:(t % 2 + 1) * P],
                               ps[:, 4 + 2 * (t % 2), :].rearrange("p (j n) -> p j n", j=4)).then_inc(turn_act, 1)

            def keep_mixed(b):
                act.wait_ge(mixed, 2 * b + 1)
                nc.scalar.copy(oT[:, 0, b * S:(b + 1) * S], ps[:, 4, 0:S]).then_inc(mixed_act, 1)

            exponentials(0)
            exponentials(1)
            keep_turned(0)
            keep_turned(1)
            exponentials(2)
            exponentials(3)
            keep_mixed(0)
            keep_turned(2)
            keep_turned(3)
            keep_mixed(1)

        @block.vector
        def _(dve):
            dve.wait_ge(projected, 2)
            nc.vector.tensor_copy(qT[:, 1, :], ps[:, 1, :]).then_inc(dve_kept, 1)
            dve.wait_ge(projected, 4)
            nc.vector.tensor_copy(knT[:, 1, :], ps[:, 3, :]).then_inc(dve_kept, 1)
            for t in (1, 3):
                dve.wait_ge(projected, 5 + t)
                nc.vector.tensor_copy(vn[:, t, :], ps[:, 4 + t, 0:D]).then_inc(dve_kept, 1)

            def maximum(t):
                bank = 2 * (t % 2)
                dve.wait_ge(scored, t + 1)
                settle(dve, own, nc.vector.reduce_max(top[:, t:t + 1], flat(ps[:, bank:bank + 2, :])[:, 0:KEYS], AX.X))
                nc.vector.tensor_scalar(bias[:, t:t + 1], top[:, t:t + 1], -SCALE, None, ALU.mult)\
                    .then_inc(biased, 1)

            def keep_turned(t):
                dve.wait_ge(turned, t + 1)
                if t == 2:
                    dve.wait_ge(mixed, 2)
                nc.vector.tensor_copy(probsT[:, 4:6, (t % 2) * P:(t % 2 + 1) * P],
                                      ps[:, 5 + 2 * (t % 2), 0:2 * P].rearrange("p (j n) -> p j n", j=2))\
                    .then_inc(turn_dve, 1)

            def keep_mixed(b):
                dve.wait_ge(mixed, 2 * b + 2)
                nc.vector.tensor_copy(oT[:, 1, b * S:(b + 1) * S], ps[:, 5, 0:S]).then_inc(mixed_dve, 1)

            def add(t):
                dve.wait_ge(exped, t + 1)
                settle(dve, own, nc.vector.reciprocal(inv[:, t:t + 1], total[:, t:t + 1]))
                settle(dve, own, nc.vector.tensor_tensor(factor[:, t:t + 1], inv[:, t:t + 1], c.gate[:, 0:1], ALU.mult))
                dve.wait_ge(out_ready, t + 1)
                nc.vector.scalar_tensor_tensor(out=c.x[:, t, :], in0=ps[:, 6 + t % 2, 0:D], scalar=factor[:, t:t + 1],
                                               in1=c.x[:, t, :], op0=ALU.mult, op1=ALU.add).then_inc(added, 1)

            maximum(0)
            maximum(1)
            keep_turned(0)
            keep_turned(1)
            maximum(2)
            maximum(3)
            keep_mixed(0)
            add(0)
            add(1)
            keep_turned(2)
            keep_turned(3)
            keep_mixed(1)
            add(2)
            add(3)
            dve.wait_ge(added, 4)


def repeat(eng, first, end, unroll, body):
    groups = (end - first) // unroll
    if groups > 1:
        with eng.Fori(0, groups) as it:
            for s in range(unroll):
                body(it * unroll + (first + s), (first + s) % unroll)
    else:
        groups = 0
    for j in range(first + groups * unroll, end):
        body(j, j % unroll)


def load_expert_tiles(nc, c, d, name):
    at = MOE_AT[name]

    def start(sp):
        for s in range(SLOTS):
            sp.dma_start(c.slots[:, s, :], d["moe_w"][at + s]).then_inc(c.slot_loaded[s], 16)
    return start


def router_stage(nc, c, d, name):
    _, E, _ = MOE[name]
    at = {"l1": 0, "l2": 8, "l3": 24}[name]
    R = 3 * (E + 1)
    with ExitStack() as ctx:
        def sb(n, shape, dt=F32):
            return ctx.enter_context(nc.sbuf_tensor(f"{name}r_{n}", shape, dt))

        sem = stage_semaphores(nc, ctx, name + "r")
        logits, centered = sb("logits", [P, TT, E]), sb("centered", [P, TT, E])
        expd, prob = sb("exp", [P, TT, E]), sb("prob", [P, TT, E])
        top, total, inv = sb("top", [P, TT]), sb("total", [P, TT]), sb("inv", [P, TT])
        above, equal = sb("above", [P, TT, E, E]), sb("equal", [P, TT, E, E])
        rank, chosen = sb("rank", [P, TT, E]), sb("chosen", [P, TT, E])
        weight, rest = sb("weight", [P, TT, E + 1]), sb("rest", [P, TT, E + 1])
        parts = sb("parts", [P, TT, 3, E + 1], BF16)
        rw = sb("rw", [P, KT, E])
        square, ms, rms = sb("square", [P, D]), sb("ms", [P, TT]), sb("rms", [P, TT])
        group_top, group_masked = sb("group_top", [P, TT, 4]), sb("group_masked", [P, TT, E])
        scaled, scored, centred_ready, exped = sem("scaled"), sem("scored"), sem("centred"), sem("exped")
        split, turned, kept = sem("split"), sem("turned"), sem("kept")
        ms_ready, rms_ready = sem("ms_ready"), sem("rms_ready")
        own = Tally(sem("own"))
        turned_bf = c.ps[:, 4, :].bitcast(BF16)
        block = ctx.enter_context(nc.Block(no_gpsimd_drain=True))

        @block.tensor
        def _(pe):
            if name == "l3":
                pe.wait_ge(scaled, KT)
            for t in range(TT):
                for k in range(KT):
                    w = rw[:, k, :] if name == "l3" else c.routers[:, k, at:at + E]
                    last = nc.tensor.matmul(c.ps[:, t, 0:E], c.hT[:, k, t * P:(t + 1) * P], w,
                                            start=k == 0, stop=k == KT - 1)
            last.then_inc(scored, 1)
            pe.wait_ge(split, 1)
            for t in range(TT):
                last = nc.tensor.transpose(turned_bf[0:R, t * P:(t + 1) * P],
                                           parts[:, t].rearrange("p a e -> p (a e)"), c.ident_bf[:])
            last.then_inc(turned, 1)

        @block.scalar
        def _(act):
            act.wait_ge(centred_ready, 1)
            nc.scalar.activation(expd[:], centered[:], ACT.Exp).then_inc(exped, 1)
            act.wait_ge(turned, 1)
            nc.scalar.copy(c.weightT[0:R, :], turned_bf[0:R, 0:T]).then_inc(kept, 1)
            act.wait_ge(kept, 1)

        if name == "l3":
            @block.gpsimd
            def _(pool):
                pool.wait_ge(ms_ready, 1)
                nc.gpsimd.tensor_tensor(rms[:], ms[:], c.minus_half[:, 0:TT], ALU.pow).then_inc(rms_ready, 1)

        @block.vector
        def _(dve):
            V = nc.vector

            def ranked(score, n, keep):
                shape = [P, TT, n, n]
                other, self_ = score.unsqueeze(2).broadcast_to(shape), score.unsqueeze(3).broadcast_to(shape)
                a = above[:].rearrange("p t e f -> p t (e f)")[:, :, 0:n * n].rearrange("p t (e f) -> p t e f", e=n)
                q = equal[:].rearrange("p t e f -> p t (e f)")[:, :, 0:n * n].rearrange("p t (e f) -> p t e f", e=n)
                own.up(V.tensor_tensor(a, other, self_, ALU.is_gt))
                settle(dve, own, V.tensor_tensor(q, other, self_, ALU.is_equal))
                before = c.before[:, 0:n, 0:n].unsqueeze(1).broadcast_to(shape)
                settle(dve, own, V.tensor_tensor(q, q, before, ALU.mult))
                settle(dve, own, V.tensor_tensor(a, a, q, ALU.add))
                settle(dve, own, V.tensor_reduce(rank[:, :, 0:n], a, AX.X, ALU.add))
                settle(dve, own, V.tensor_scalar(chosen[:, :, 0:n], rank[:, :, 0:n], float(keep), None, ALU.is_lt))

            if name == "l3":
                for k in range(KT):
                    col = COL["router_scale"] + k
                    V.tensor_scalar(rw[:, k, :], c.routers[:, k, at:at + E], c.cols[:, col:col + 1], None, ALU.mult)\
                        .then_inc(scaled, 1)
                for t in range(TT):
                    settle(dve, own, V.tensor_tensor_reduce(
                        out=square[:], in0=c.h[:, t, :], in1=c.h[:, t, :], scale=1.0, scalar=0.0,
                        op0=ALU.mult, op1=ALU.add, accum_out=ms[:, t:t + 1]))
                V.tensor_scalar(ms[:], ms[:], 1.0 / D, RMS_EPS, ALU.mult, ALU.add).then_inc(ms_ready, 1)
            dve.wait_ge(scored, 1)
            if name == "l3":
                dve.wait_ge(rms_ready, 1)
                for t in range(TT):
                    last = own.up(V.tensor_scalar(logits[:, t, :], c.ps[:, t, 0:E], rms[:, t:t + 1], D ** -0.5,
                                                  ALU.mult, ALU.mult))
                dve.wait_ge(own.sem, last)
            else:
                settle(dve, own, V.tensor_copy(logits[:], c.ps[:, 0:TT, 0:E]))
            settle(dve, own, V.tensor_reduce(top[:], logits[:], AX.X, ALU.max))
            V.tensor_tensor(centered[:], logits[:], top[:].unsqueeze(2).broadcast_to([P, TT, E]), ALU.subtract)\
                .then_inc(centred_ready, 1)
            dve.wait_ge(exped, 1)
            settle(dve, own, V.tensor_reduce(total[:], expd[:], AX.X, ALU.add))
            settle(dve, own, V.reciprocal(inv[:], total[:]))
            settle(dve, own, V.tensor_tensor(prob[:], expd[:], inv[:].unsqueeze(2).broadcast_to([P, TT, E]), ALU.mult))
            if name == "l1":
                pairs = prob[:].rearrange("p t (g e) -> p t g e", g=4)
                settle(dve, own, V.tensor_reduce(group_top[:], pairs, AX.X, ALU.max))
                ranked(group_top[:], 4, 2)
                settle(dve, own, V.tensor_tensor(
                    group_masked[:].rearrange("p t (g e) -> p t g e", g=4), pairs,
                    chosen[:, :, 0:4].unsqueeze(3).broadcast_to([P, TT, 4, 2]), ALU.mult))
                ranked(group_masked[:], E, 2)
                settle(dve, own, V.tensor_tensor(weight[:, :, 0:E], group_masked[:], chosen[:], ALU.mult))
            else:
                ranked(prob[:], E, 6 if name == "l2" else 2)
                settle(dve, own, V.tensor_tensor(prob[:], prob[:], chosen[:], ALU.mult))
                settle(dve, own, V.tensor_reduce(total[:], prob[:], AX.X, ALU.add))
                if name == "l3":
                    settle(dve, own, V.tensor_scalar(total[:], total[:], 1e-12, None, ALU.max))
                settle(dve, own, V.reciprocal(inv[:], total[:]))
                settle(dve, own, V.tensor_tensor(weight[:, :, 0:E], prob[:],
                                                 inv[:].unsqueeze(2).broadcast_to([P, TT, E]), ALU.mult))
                if name == "l3":
                    es = c.rows[:, ROW["expert_scale"]:ROW["expert_scale"] + E]
                    settle(dve, own, V.tensor_tensor(weight[:, :, 0:E], weight[:, :, 0:E],
                                                     es.unsqueeze(1).broadcast_to([P, TT, E]), ALU.mult))
            settle(dve, own, V.memset(weight[:, :, E:E + 1], 1.0))
            settle(dve, own, V.tensor_copy(parts[:, :, 0, :], weight[:]))
            settle(dve, own, V.tensor_tensor(rest[:], weight[:], parts[:, :, 0, :], ALU.subtract))
            settle(dve, own, V.tensor_copy(parts[:, :, 1, :], rest[:]))
            V.tensor_tensor(parts[:, :, 2, :], rest[:], parts[:, :, 1, :], ALU.subtract).then_inc(split, 1)
            dve.wait_ge(split, 1)


def ffn_stage(nc, c, d, name, residual=None):
    fp4 = name == "l0"
    J = 16 if fp4 else MOE[name][0]
    ring = 8 if fp4 else SLOTS
    func = {"l0": ACT.Gelu_apprx_tanh, "l1": ACT.Silu, "l2": ACT.Silu, "l3": ACT.Gelu}[name]
    gate = {"l0": 4, "l1": 5, "l2": 6, "l3": 7}[name]
    unit = 2.0 ** 14 if fp4 else 1.0
    ps = c.ps
    with ExitStack() as ctx:
        def sb(n, shape, dt=F32):
            return ctx.enter_context(nc.sbuf_tensor(f"{name}f_{n}", shape, dt))

        sem = stage_semaphores(nc, ctx, name + "f")
        acted_buf, hidden = sb("acted", [P, 2, T]), sb("hidden", [P, 2, T])
        factor = sb("factor", [P, 1])
        partial = sb("partial", [P, TT, D]) if residual is not None else None
        gated, upped, acted, hidden_ready = sem("gated"), sem("upped"), sem("acted"), sem("hidden_ready")
        downed, added = sem("downed"), sem("added")
        own = Tally(sem("own"))
        if fp4:
            slots = sb("slots", [P, 8, FW])
            words, scales = sb("words", [P, 2, FW], I32), sb("scales", [P, 2, FW])
            spread, sign = sb("spread", [P, FW], I32), sb("sign", [P, FW], I32)
            codes = sb("codes", [P, 2, FW], I32)
            packed_loaded, words_read = [sem("packed0"), sem("packed1")], sem("words_read")
            coded, dequantized = sem("coded"), sem("dequantized")
        else:
            slots, loaded, base = c.slots, c.slot_loaded, list(c.slot_loads)
            for j in range(J):
                c.slot_loads[j % SLOTS] += 1
            selected = sb("sel", [P, J * P], BF16)
            sel_loaded = sem("sel_loaded")
        block = ctx.enter_context(nc.Block(no_gpsimd_drain=True))

        @block.sync
        def _(sp):
            if fp4:
                for i in range(8):
                    if i >= 2:
                        sp.wait_ge(words_read, i - 1)
                        sp.wait_ge(dequantized, i - 1)
                    sp.dma_start(words[:, i % 2, :], d["fp4_w"][i]).then_inc(packed_loaded[i % 2], 16)
                    sp.dma_start(scales[:, i % 2, :], d["fp4_s"][i].unsqueeze(1).broadcast_to([8, 16, FW]))\
                        .then_inc(packed_loaded[i % 2], 16)
                return
            sp.dma_start(selected[:].bitcast(U16), d["sel"][:, MOE_AT[name] * P:(MOE_AT[name] + J) * P]).then_inc(sel_loaded, 16)

            def load(j, slot):
                sp.wait_ge(downed, j - SLOTS + 1)
                src = d["moe_w"][bass.ds(j + MOE_AT[name], 1)].rearrange("a p n -> p (a n)")
                sp.dma_start(slots[:, slot, :], src).then_inc(loaded[slot], 16)
            repeat(sp, SLOTS, J, SLOTS, load)

        @block.tensor
        def _(pe):
            for bank in (4, 5):
                nc.tensor.matmul(ps[:, bank, :], c.zero_bf[:, 0:P], c.zero_bf[:], start=True, stop=True,
                                 skip_group_check=True)
            if not fp4:
                pe.wait_ge(sel_loaded, 16)

            def gate_up(j, slot):
                parity = slot % 2
                if fp4:
                    pe.wait_ge(dequantized, j // 2 + 1)
                else:
                    pe.wait_ge(loaded[slot], (base[slot] + 1) * 16 + (j - slot) * (16 // SLOTS))
                if not isinstance(j, int) or j >= 2:
                    pe.wait_ge(acted, j - 1)
                    pe.wait_ge(hidden_ready, j - 1)
                for part, done in ((0, gated), (1, upped)):
                    for k in range(KT):
                        at = k * 2 * P + part * P
                        last = nc.tensor.matmul(ps[:, 2 * parity + part, :], slots[:, slot, at:at + P],
                                                c.hT[:, k, :], start=k == 0, stop=k == KT - 1)
                    if part == 0 or fp4:
                        last.then_inc(done, 1)
                if not fp4:
                    nc.tensor.matmul(ps[:, 6 + parity, :], selected[:, bass.ds(j * P, P)], c.weightT[:],
                                     start=True, stop=True).then_inc(upped, 1)

            def down(j, slot):
                pe.wait_ge(hidden_ready, j + 1)
                for t in range(TT):
                    last = nc.tensor.matmul(ps[:, 4 + t // 2, (t % 2) * D:(t % 2 + 1) * D],
                                            hidden[:, slot % 2, t * P:(t + 1) * P], slots[:, slot, 4 * P:4 * P + D],
                                            start=False, stop=True, skip_group_check=True)
                last.then_inc(downed, 1)

            def step(j, phase):
                gate_up(j + 1, (phase + 1) % ring)
                down(j, phase)
            gate_up(0, 0)
            repeat(pe, 0, J - 1, ring, step)
            down(J - 1, (J - 1) % ring)

        @block.scalar
        def _(act):
            def activate(j, phase):
                act.wait_ge(gated, j + 1)
                if not isinstance(j, int) or j >= 2:
                    act.wait_ge(hidden_ready, j - 1)
                nc.scalar.activation(acted_buf[:, phase % 2, :], ps[:, 2 * (phase % 2), :], func, scale=unit)\
                    .then_inc(acted, 1)
            for j in range(2):
                activate(j, j)
            repeat(act, 2, J, 2, activate)

        if fp4:
            @block.gpsimd
            def _(pool):
                for i in range(8):
                    pool.wait_ge(coded, i + 1)
                    if i >= 4:
                        pool.wait_ge(downed, 2 * i - 6)
                    half = codes[:, i % 2, :].bitcast(F16).rearrange("p (n h) -> p h n", h=2)
                    pair = slots[:, 2 * (i % 4):2 * (i % 4) + 2, :]
                    sc = scales[:, i % 2, :]
                    for h in range(2):
                        last = nc.gpsimd.tensor_tensor(
                            pair[:, :, 256 * h:256 * h + 256],
                            half[:, h, 0:512].rearrange("p (s n) -> p s n", s=2),
                            sc[:, 0:512].rearrange("p (s n) -> p s n", s=2), ALU.mult)
                        last = nc.gpsimd.tensor_tensor(pair[:, h, 512:768], half[:, h, 512:768], sc[:, 512:768],
                                                       ALU.mult)
                    last.then_inc(dequantized, 1)

        @block.vector
        def _(dve):
            V = nc.vector

            def decode(i):
                dve.wait_ge(packed_loaded[i % 2], 32 * (i // 2 + 1))
                w = words[:, i % 2, :]
                V.tensor_scalar(spread[:], w, 255, None, ALU.bitwise_and).then_inc(words_read, 1)
                dve.wait_ge(words_read, i + 1)
                settle(dve, own, V.scalar_tensor_tensor(out=spread[:], in0=spread[:], scalar=12, in1=spread[:],
                                                        op0=ALU.logical_shift_left, op1=ALU.bitwise_or))
                if i >= 2:
                    dve.wait_ge(dequantized, i - 1)
                own.up(V.tensor_scalar(codes[:, i % 2, :], spread[:], 9, 0x0E000E00, ALU.logical_shift_left,
                                       ALU.bitwise_and))
                last = own.up(V.tensor_scalar(sign[:], spread[:], 12, 0x80008000 - (1 << 32),
                                              ALU.logical_shift_left, ALU.bitwise_and))
                dve.wait_ge(own.sem, last)
                V.tensor_tensor(codes[:, i % 2, :], codes[:, i % 2, :], sign[:], ALU.bitwise_or).then_inc(coded, 1)

            multiplied = Tally(c.dve_pairs)
            multiplied.n = c.dve_pairs_n

            def combine(j, phase):
                p = phase % 2
                dve.wait_ge(acted, j + 1)
                dve.wait_ge(upped, j + 1)
                if not isinstance(j, int) or j >= 2:
                    dve.wait_ge(downed, j - 1)
                if fp4:
                    V.tensor_tensor(hidden[:, p, :], acted_buf[:, p, :], ps[:, 2 * p + 1, :], ALU.mult)\
                        .then_inc(hidden_ready, 1)
                    return
                V.tensor_tensor(acted_buf[:, p, :], acted_buf[:, p, :], ps[:, 2 * p + 1, :], ALU.mult)\
                    .then_inc(multiplied.sem, 1)
                dve.wait_ge(multiplied.sem, j + (multiplied.n + 1))
                V.tensor_tensor(hidden[:, p, :], acted_buf[:, p, :], ps[:, 6 + p, :], ALU.mult)\
                    .then_inc(hidden_ready, 1)

            settle(dve, own, V.tensor_scalar(factor[:], c.gate[:, gate:gate + 1], unit * unit, None, ALU.mult))
            if fp4:
                decode(0)
                decode(1)
                for j in range(J):
                    combine(j, j % 2)
                    if j % 2 and j // 2 + 2 < 8:
                        decode(j // 2 + 2)
            else:
                for j in range(2):
                    combine(j, j)
                repeat(dve, 2, J, 2, combine)
                c.dve_pairs_n += J
            dve.wait_ge(downed, J)
            for t in range(TT):
                acc = ps[:, 4 + t // 2, (t % 2) * D:(t % 2 + 1) * D]
                if residual is None:
                    V.scalar_tensor_tensor(out=c.x[:, t, :], in0=acc, scalar=factor[:], in1=c.x[:, t, :],
                                           op0=ALU.mult, op1=ALU.add).then_inc(added, 1)
                else:
                    settle(dve, own, V.tensor_tensor(partial[:, t, :], acc, residual[:, t, :], ALU.add))
                    V.scalar_tensor_tensor(out=c.x[:, t, :], in0=partial[:, t, :], scalar=factor[:],
                                           in1=c.x[:, t, :], op0=ALU.mult, op1=ALU.add).then_inc(added, 1)
            dve.wait_ge(added, TT)


Q_PARTS = (0, 0, 1, 1, 0, 2)
K_PARTS = (0, 1, 0, 1, 2, 0)
STACK = 6 * HD
STACK_M = STACK + 3


def split_parts(dve, V, own, src, parts, rest):
    settle(dve, own, V.tensor_copy(parts[0], src))
    settle(dve, own, V.tensor_tensor(rest, src, parts[0], ALU.subtract))
    settle(dve, own, V.tensor_copy(parts[1], rest))
    return V.tensor_tensor(parts[2], rest, parts[1], ALU.subtract)


def small_head_attention(nc, c, name, qT, kT, values, kv_heads, causal, place, finish):
    G = 4
    KTILES = CTX // P
    ps = c.ps
    with ExitStack() as ctx:
        def sb(n, shape, dt=F32):
            return ctx.enter_context(nc.sbuf_tensor(f"{name}_{n}", shape, dt))

        sem = stage_semaphores(nc, ctx, name)
        k_rows = P if kv_heads == H else kv_heads * HD
        k_tiles = KT if kv_heads == H else 1
        q_parts = sb("q_parts", [P, 3, KT, T], BF16)
        k_parts = sb("k_parts", [k_rows, 3, k_tiles, B * CTX], BF16)
        rest = sb("rest", [P, KT, CTX])
        q_stack, k_stack = sb("q_stack", [P, H, T], BF16), sb("k_stack", [P, kv_heads, B * CTX], BF16)
        top = sb("top", [P, TT, H])
        m_rest, m_parts = sb("m_rest", [P, TT, H]), sb("m_parts", [P, TT, 3, H], BF16)
        m_turned = sb("m_turned", [3 * H, T], BF16)
        probsT = sb("probsT", [P, 3, 4 * S])
        outT, inv = sb("outT", [P, G, T]), sb("inv", [P, TT, H])
        q_split, k_split, ones_ready = sem("q_split"), sem("k_split"), sem("ones_ready")
        q_stacked, k_stacked = sem("q_stacked"), sem("k_stacked")
        scored, maxed = sem("scored"), sem("maxed")
        m_split, m_transposed, m_kept = sem("m_split"), sem("m_transposed"), sem("m_kept")
        m_stacked = [sem("m_stacked0"), sem("m_stacked1")]
        scoredT, exped, mixed = sem("scoredT"), sem("exped"), sem("mixed")
        kept, turned, finished = sem("kept"), sem("turned"), sem("finished")
        own = Tally(sem("own"))
        m_bf = [ps[:, 6 + b, :].bitcast(BF16) for b in range(B)]
        q_loads, k_loads = 6 * KT, 6 * k_tiles
        k_heads = kv_heads // k_tiles
        q_bounce = nc.dram_tensor(f"{name}_q_bounce", [3 * KT, P, T], BF16, kind="Internal").ap()
        k_bounce = nc.dram_tensor(f"{name}_k_bounce", [3 * k_tiles, k_rows, B * CTX], BF16, kind="Internal").ap()
        q_bounced, k_bounced = sem("q_bounced"), sem("k_bounced")
        units = [(b, g, kt) for b in range(B) for g in range(G) for kt in range(KTILES)]
        block = ctx.enter_context(nc.Block(no_gpsimd_drain=True))

        def span(kt):
            return (P, P) if causal and kt == KTILES - 1 else (0, S)

        @block.sync
        def _(sp):
            sp.wait_ge(k_split, 1)
            sp.dma_start(k_bounce.rearrange("c p n -> p c n"), k_parts[:].rearrange("p c k n -> p (c k) n"))\
                .then_inc(k_bounced, 16)
            sp.wait_ge(k_bounced, 16)
            by_head = k_bounce.rearrange("(c k) (h d) n -> c d k h n", c=3, d=HD)
            for row, part in enumerate(K_PARTS):
                for a in range(k_tiles):
                    sp.dma_start(k_stack[row * HD:(row + 1) * HD, a * k_heads:(a + 1) * k_heads, :],
                                 by_head[part, :, a]).then_inc(k_stacked, 16)
            for b in range(B):
                sp.wait_ge(m_kept, b + 1)
                for part in range(3):
                    sp.dma_start(q_stack[STACK + part:STACK + part + 1, :, b * S:(b + 1) * S],
                                 m_turned[part * H:(part + 1) * H, b * S:(b + 1) * S]).then_inc(m_stacked[b], 16)

        @block.gpsimd
        def _(pool):
            nc.gpsimd.memset(k_stack[STACK:P], 1.0).then_inc(ones_ready, 1)
        @block.tensor
        def _(pe):
            pe.wait_ge(q_stacked, 16 * q_loads)
            pe.wait_ge(k_stacked, 16 * k_loads)
            pe.wait_ge(ones_ready, 1)

            def plain_scores(n):
                b, half, pair = n // 16, n // 8 % 2, n % 8
                if n >= 2:
                    pe.wait_ge(maxed, n - 1)
                width = 3 * P if causal and half == 0 else CTX
                for i in range(2):
                    h = 2 * pair + i
                    bank = 2 * (n % 2) + i
                    q0 = b * S + half * P
                    last = nc.tensor.matmul(ps[:, bank, 0:width], q_stack[0:STACK, h, q0:q0 + P],
                                            k_stack[0:STACK, h * kv_heads // H, b * CTX:b * CTX + width],
                                            start=True, stop=not causal)
                    if causal:
                        last = nc.tensor.matmul(ps[:, bank, width - P:width], c.ident_bf[:], c.mask_q[:],
                                                start=False, stop=True)
                last.then_inc(scored, 1)

            def turn_maxima(b):
                pe.wait_ge(m_split, b + 1)
                for t in (2 * b, 2 * b + 1):
                    last = nc.tensor.transpose(m_bf[b][0:3 * H, (t % 2) * P:(t % 2 + 1) * P],
                                               m_parts[:, t].rearrange("p a h -> p (a h)"), c.ident_bf[:])
                last.then_inc(m_transposed, 1)

            def turned_scores(n):
                b, g, kt = units[n]
                if n < 2:
                    pe.wait_ge(maxed, 32)
                else:
                    pe.wait_ge(exped, n - 1)
                if n % 16 == 0:
                    pe.wait_ge(m_stacked[b], 48)
                q0, nq = span(kt)
                for r in range(4):
                    h = 4 * g + r
                    bank, at = 2 * (n % 2) + r // 2, (r % 2) * S
                    diagonal = causal and kt >= 2
                    last = nc.tensor.matmul(ps[:, bank, at:at + nq],
                                            k_stack[0:STACK_M, h * kv_heads // H, b * CTX + kt * P:b * CTX + (kt + 1) * P],
                                            q_stack[0:STACK_M, h, b * S + q0:b * S + q0 + nq],
                                            start=True, stop=not diagonal)
                    if diagonal:
                        last = nc.tensor.matmul(ps[:, bank, at:at + P], c.ident_bf[:], c.mask_k[:],
                                                start=False, stop=True)
                last.then_inc(scoredT, 1)

            def mix(n):
                b, g, kt = units[n]
                pe.wait_ge(exped, n + 1)
                if kt == 0 and n >= 2 * KTILES:
                    pe.wait_ge(kept, n // KTILES - 1)
                q0, nq = span(kt)
                for r in range(4):
                    h = 4 * g + r
                    last = nc.tensor.matmul(ps[32 * r:32 * r + 32, 4 + g % 2, q0:q0 + nq],
                                            values[:, b * KTILES + kt, h * kv_heads // H, :],
                                            probsT[:, n % 3, r * S:r * S + nq],
                                            start=kt == 0, stop=kt == KTILES - 1)
                last.then_inc(mixed, 1)

            for n in range(16):
                plain_scores(n)
            for n in range(16, 32):
                plain_scores(n)
                if n == 20:
                    turn_maxima(0)
            turn_maxima(1)
            turned_scores(0)
            for n in range(len(units)):
                if n + 1 < len(units):
                    turned_scores(n + 1)
                mix(n)
            for t in range(TT):
                pe.wait_ge(kept, len(units) // KTILES)
                for g in range(G):
                    last = nc.tensor.transpose(ps[:, t, g * P:(g + 1) * P], outT[:, g, t * P:(t + 1) * P], c.ident[:])
                last.then_inc(turned, 1)

        @block.scalar
        def _(act):
            act.wait_ge(q_split, 1)
            act.dma_start(q_bounce.rearrange("c p n -> p c n"), q_parts[:].rearrange("p c k n -> p (c k) n"))\
                .then_inc(q_bounced, 16)
            act.wait_ge(q_bounced, 16)
            by_head = q_bounce.rearrange("(c k) (h d) n -> c d k h n", c=3, d=HD)
            for row, part in enumerate(Q_PARTS):
                for a in range(KT):
                    act.dma_start(q_stack[row * HD:(row + 1) * HD, a * 8:(a + 1) * 8, :], by_head[part, :, a])\
                        .then_inc(q_stacked, 16)

            def keep_maxima(b):
                act.wait_ge(m_transposed, b + 1)
                nc.scalar.copy(m_turned[:, b * S:(b + 1) * S], m_bf[b][0:3 * H, 0:S]).then_inc(m_kept, 1)
            keep_maxima(0)
            keep_maxima(1)
            for n, (b, g, kt) in enumerate(units):
                _, nq = span(kt)
                act.wait_ge(scoredT, n + 1)
                if n >= 3:
                    act.wait_ge(mixed, n - 2)
                scores = flat(ps[:, 2 * (n % 2):2 * (n % 2) + 2, :]).rearrange("p (r q) -> p r q", r=4)[:, :, 0:nq]
                probs = probsT[:, n % 3, :].rearrange("p (r q) -> p r q", r=4)[:, :, 0:nq]
                nc.scalar.activation(probs, scores, ACT.Exp, scale=HD ** -0.5).then_inc(exped, 1)

        @block.vector
        def _(dve):
            V = nc.vector
            split_parts(dve, V, own, qT[:], [q_parts[:, i] for i in range(3)], rest[:, 0:KT, 0:T])\
                .then_inc(q_split, 1)
            if kv_heads == H:
                settle(dve, own, V.tensor_copy(k_parts[:, 0], kT[:]))
                for half in range(2):
                    cols = slice(half * CTX, (half + 1) * CTX)
                    settle(dve, own, V.tensor_tensor(rest[:], kT[:, :, cols], k_parts[:, 0, :, cols], ALU.subtract))
                    settle(dve, own, V.tensor_copy(k_parts[:, 1, :, cols], rest[:]))
                    last = V.tensor_tensor(k_parts[:, 2, :, cols], rest[:], k_parts[:, 1, :, cols], ALU.subtract)
                    if half == 0:
                        settle(dve, own, last)
                last.then_inc(k_split, 1)
            else:
                split_parts(dve, V, own, kT[:], [k_parts[:, i, 0, :] for i in range(3)], flat(rest[:])[0:k_rows])\
                    .then_inc(k_split, 1)
            for n in range(32):
                b, half, pair = n // 16, n // 8 % 2, n % 8
                width = 3 * P if causal and half == 0 else CTX
                dve.wait_ge(scored, n + 1)
                V.tensor_reduce(top[:, 2 * b + half, 2 * pair:2 * pair + 2],
                                ps[:, 2 * (n % 2):2 * (n % 2) + 2, 0:width], AX.X, ALU.max).then_inc(maxed, 1)
                if n % 16 == 15:
                    dve.wait_ge(maxed, n + 1)
                    ts = slice(2 * b, 2 * b + 2)
                    settle(dve, own, V.tensor_scalar(m_parts[:, ts, 0, :], top[:, ts, :], -1.0, None, ALU.mult))
                    settle(dve, own, V.scalar_tensor_tensor(out=m_rest[:, ts, :], in0=top[:, ts, :], scalar=-1.0,
                                                            in1=m_parts[:, ts, 0, :], op0=ALU.mult, op1=ALU.subtract))
                    settle(dve, own, V.tensor_copy(m_parts[:, ts, 1, :], m_rest[:, ts, :]))
                    V.tensor_tensor(m_parts[:, ts, 2, :], m_rest[:, ts, :], m_parts[:, ts, 1, :], ALU.subtract)\
                        .then_inc(m_split, 1)
            for n in range(len(units) // KTILES):
                b, g = n // G, n % G
                dve.wait_ge(mixed, KTILES * (n + 1))
                V.tensor_copy(outT[:, g, b * S:(b + 1) * S], ps[:, 4 + g % 2, 0:S]).then_inc(kept, 1)
            for t in range(TT):
                dve.wait_ge(turned, t + 1)
                heads = ps[:, t, :].rearrange("p (h e) -> p h e", h=H)
                settle(dve, own, V.reciprocal(inv[:, t, :], heads[:, :, HD]))
                finish(dve, own, t, heads[:, :, 0:HD], inv[:, t, :].unsqueeze(2).broadcast_to([P, H, HD]))


def l1_attention(nc, c, d):
    with ExitStack() as ctx:
        values = ctx.enter_context(nc.sbuf_tensor("l1x_values", [P, CT, H, 32], F32))
        normed = ctx.enter_context(nc.sbuf_tensor("l1x_normed", [P, TT, D], F32))
        sem = stage_semaphores(nc, ctx, "l1xv")
        filled, added = sem("filled"), sem("added")
        with nc.Block(no_gpsimd_drain=True) as block:
            @block.gpsimd
            def _(pool):
                nc.gpsimd.memset(values[:, :, :, HD:HD + 1], 1.0).then_inc(filled, 1)
                nc.gpsimd.memset(values[:, :, :, HD + 1:32], 0.0).then_inc(filled, 1)
                pool.wait_ge(filled, 2)

            @block.vector
            def _(dve):
                nc.vector.tensor_copy(values[:, :, :, 0:HD], c.ctx[:].rearrange("p t (h e) -> p t h e", h=H))\
                    .then_inc(added, 1)
                dve.wait_ge(added, 1)

        def finish(dve, own, t, heads, inv):
            out = normed[:, t, :].rearrange("p (h e) -> p h e", h=H)
            settle(dve, own, nc.vector.tensor_tensor(out, heads, inv, ALU.mult))
            nc.vector.scalar_tensor_tensor(out=c.x[:, t, :], in0=normed[:, t, :], scalar=c.gate[:, 1:2],
                                           in1=c.x[:, t, :], op0=ALU.mult, op1=ALU.add).then_inc(added, 1)
            if t == TT - 1:
                dve.wait_ge(added, 1 + TT)
        small_head_attention(nc, c, "l1x", c.hT, c.ctxT, values, H, True, None, finish)


def l2_linear_attention(nc, c, d):
    F = 64
    PAIRS = H // 2
    ps = c.ps
    with ExitStack() as ctx:
        def sb(n, shape, dt=F32):
            return ctx.enter_context(nc.sbuf_tensor("l2x_" + n, shape, dt))

        sem = stage_semaphores(nc, ctx, "l2x")
        w, fm_q, fm_k = sb("w", [P, 4, KT, D]), sb("fm_q", [P, 512]), sb("fm_k", [P, 512])
        qT, kT = sb("qT", [P, KT, T]), sb("kT", [P, KT, B * CTX])
        values = sb("values", [P, CT, H, HD + 1])
        q_feat, k_feat = sb("q_feat", [P, PAIRS, T]), sb("k_feat", [P, CT, H * F])
        kv = sb("kv", [P, B, PAIRS, 64])
        outT, inv, normed = sb("outT", [P, 4, T]), sb("inv", [P, TT, H]), sb("normed", [P, TT, D])
        mixedT, biased = sb("mixedT", [P, KT, T]), sb("biased", [P, TT, D])
        loaded, filled = sem("loaded"), sem("filled")
        q_done, k_done, v_done = sem("q_done"), sem("k_done"), sem("v_done")
        kept_act, kept_dve, v_kept = sem("kept_act"), sem("kept_dve"), sem("v_kept")
        qf_done, kf_done, qf_kept, kf_kept = sem("qf_done"), sem("kf_done"), sem("qf_kept"), sem("kf_kept")
        kv_done, kv_kept, out_done, out_kept = sem("kv_done"), sem("kv_kept"), sem("out_done"), sem("out_kept")
        turned, normalised, back, back_act, back_dve = \
            sem("turned"), sem("normalised"), sem("back"), sem("back_act"), sem("back_dve")
        projected, added = sem("projected"), sem("added")
        own = Tally(sem("own"))
        V_BANKS, KF_BANKS = (6, 7, 0, 1), (6, 7, 0, 1)
        block = ctx.enter_context(nc.Block(no_gpsimd_drain=True))

        @block.sync
        def _(sp):
            sp.dma_start(w[:], d["l2_w"].rearrange("w k p n -> p w k n")).then_inc(loaded, 16)
            sp.dma_start(fm_q[:], d["fm_q"]).then_inc(loaded, 16)
            sp.dma_start(fm_k[:], d["fm_k"]).then_inc(loaded, 16)

        @block.gpsimd
        def _(pool):
            nc.gpsimd.memset(kv[:], 0.0).then_inc(filled, 1)
            nc.gpsimd.memset(values[:, :, :, HD:HD + 1], 1.0).then_inc(filled, 1)

        @block.tensor
        def _(pe):
            pe.wait_ge(loaded, 48)
            for m in range(KT):
                for k in range(KT):
                    last = nc.tensor.matmul(ps[:, m, :], w[:, 0, k, m * P:(m + 1) * P], c.hT[:, k, :],
                                            start=k == 0, stop=k == KT - 1)
                last.then_inc(q_done, 1)
            for m in range(KT):
                for half in range(2):
                    for k in range(KT):
                        last = nc.tensor.matmul(ps[:, 2 + 2 * m + half, :], w[:, 1, k, m * P:(m + 1) * P],
                                                c.ctxT[:, k, half * CTX:(half + 1) * CTX],
                                                start=k == 0, stop=k == KT - 1)
                    last.then_inc(k_done, 1)
            for i in range(4):
                if i == 2:
                    pe.wait_ge(kept_act, 1)
                    pe.wait_ge(kept_dve, 1)
                for s in range(2):
                    t = 2 * i + s
                    for k in range(KT):
                        last = nc.tensor.matmul(ps[:, V_BANKS[i], s * D:(s + 1) * D], c.ctxT[:, k, t * P:(t + 1) * P],
                                                w[:, 2, k, :], start=k == 0, stop=k == KT - 1)
                last.then_inc(v_done, 1)
            pe.wait_ge(kept_act, 3)
            pe.wait_ge(kept_dve, 3)
            for j in range(PAIRS):
                if j >= 4:
                    pe.wait_ge(qf_kept, j - 3)
                nc.tensor.matmul(ps[:, 2 + j % 4, :], fm_q[:, (j % 4) * P:(j % 4 + 1) * P], qT[:, j // 4, :],
                                 start=True, stop=True).then_inc(qf_done, 1)
            for n in range(2 * CT):
                if n < 4:
                    pe.wait_ge(v_kept, n + 1)
                else:
                    pe.wait_ge(kf_kept, n - 3)
                nc.tensor.matmul(ps[:, KF_BANKS[n % 4], :], kT[:, n % 2, (n // 2) * P:(n // 2 + 1) * P], fm_k[:],
                                 start=True, stop=True).then_inc(kf_done, 1)
            pe.wait_ge(qf_kept, PAIRS)
            pe.wait_ge(filled, 2)
            for b in range(B):
                pe.wait_ge(kf_kept, CT * (b + 1))
                for j in range(PAIRS):
                    for t in range(4):
                        last = nc.tensor.matmul(ps[:, 2 + b, j * 34:(j + 1) * 34],
                                                k_feat[:, b * 4 + t, j * P:(j + 1) * P],
                                                values[:, b * 4 + t, 2 * j:2 * j + 2, :], start=t == 0, stop=t == 3)
                last.then_inc(kv_done, 1)
            pe.wait_ge(kf_kept, 2 * CT)
            for b in range(B):
                pe.wait_ge(kv_kept, 2 * (b + 1))
                for j in range(PAIRS):
                    row = 64 * (j % 2)
                    last = nc.tensor.matmul(ps[row:row + 64, 4 + j // 2, b * S:(b + 1) * S], kv[:, b, j, :],
                                            q_feat[:, j, b * S:(b + 1) * S], start=True, stop=True)
                last.then_inc(out_done, 1)
            pe.wait_ge(out_kept, 4)
            for t in range(TT):
                for g in range(4):
                    last = nc.tensor.transpose(ps[:, t, g * P:(g + 1) * P], outT[:, g, t * P:(t + 1) * P], c.ident[:])
                last.then_inc(turned, 1)
            for t in range(TT):
                pe.wait_ge(normalised, t + 1)
                for k in range(KT):
                    last = nc.tensor.transpose(ps[:, 4 + k, t * P:(t + 1) * P], normed[:, t, k * P:(k + 1) * P],
                                               c.ident[:])
            last.then_inc(back, 1)
            pe.wait_ge(back_act, 1)
            pe.wait_ge(back_dve, 1)
            for t in range(TT):
                for k in range(KT):
                    last = nc.tensor.matmul(ps[:, 6 + t // 2, (t % 2) * D:(t % 2 + 1) * D],
                                            mixedT[:, k, t * P:(t + 1) * P], w[:, 3, k, :],
                                            start=k == 0, stop=k == KT - 1)
                last.then_inc(projected, 1)

        def bias(name, m):
            return c.cols[:, COL[name] + m:COL[name] + m + 1]

        @block.scalar
        def _(act):
            act.wait_ge(q_done, 1)
            nc.scalar.activation(qT[:, 0, :], ps[:, 0, :], ACT.Identity, bias=bias("bq", 0)).then_inc(kept_act, 1)
            for half in range(2):
                act.wait_ge(k_done, half + 1)
                nc.scalar.activation(kT[:, 0, half * CTX:(half + 1) * CTX], ps[:, 2 + half, :], ACT.Identity,
                                     bias=bias("bk", 0)).then_inc(kept_act, 1)
            for j in range(PAIRS):
                act.wait_ge(qf_done, j + 1)
                nc.scalar.activation(q_feat[:, j, :], ps[:, 2 + j % 4, :], ACT.Relu).then_inc(qf_kept, 1)
            act.wait_ge(out_done, 2)
            for g in range(4):
                nc.scalar.copy(outT[:, g, :], ps[:, 4 + g, :]).then_inc(out_kept, 1)
            act.wait_ge(back, 1)
            nc.scalar.copy(mixedT[:, 0, :], ps[:, 4, :]).then_inc(back_act, 1)

        @block.vector
        def _(dve):
            V = nc.vector
            dve.wait_ge(q_done, 2)
            V.tensor_scalar(qT[:, 1, :], ps[:, 1, :], bias("bq", 1), None, ALU.add).then_inc(kept_dve, 1)
            for half in range(2):
                dve.wait_ge(k_done, half + 3)
                V.tensor_scalar(kT[:, 1, half * CTX:(half + 1) * CTX], ps[:, 4 + half, :], bias("bk", 1), None,
                                ALU.add).then_inc(kept_dve, 1)
            bv = c.rows[:, ROW["bv"]:ROW["bv"] + D].rearrange("p (h e) -> p h e", h=H)
            for i in range(4):
                dve.wait_ge(v_done, i + 1)
                for s in range(2):
                    last = V.tensor_tensor(values[:, 2 * i + s, :, 0:HD],
                                           ps[:, V_BANKS[i], s * D:(s + 1) * D].rearrange("p (h e) -> p h e", h=H),
                                           bv, ALU.add)
                last.then_inc(v_kept, 1)
            for n in range(2 * CT):
                dve.wait_ge(kf_done, n + 1)
                V.tensor_scalar(k_feat[:, n // 2, (n % 2) * 512:(n % 2 + 1) * 512], ps[:, KF_BANKS[n % 4], :], 0.0,
                                c.att_mask[:, n // 2:n // 2 + 1], ALU.max, ALU.mult).then_inc(kf_kept, 1)
            dve.wait_ge(filled, 2)
            for b in range(B):
                dve.wait_ge(kv_done, b + 1)
                for head in range(2):
                    rows = slice(64 * head, 64 * head + 64)
                    src = ps[rows, 2 + b, 0:PAIRS * 34].rearrange("p (j e) -> p j e", j=PAIRS)
                    V.tensor_copy(kv[rows, b, :, 32 * head:32 * head + HD + 1],
                                  src[:, :, 17 * head:17 * head + 17]).then_inc(kv_kept, 1)
            for t in range(TT):
                dve.wait_ge(turned, t + 1)
                heads = ps[:, t, :].rearrange("p (h e) -> p h e", h=H)
                settle(dve, own, V.tensor_scalar(inv[:, t, :], heads[:, :, HD], 1e-8, None, ALU.add))
                settle(dve, own, V.reciprocal(inv[:, t, :], inv[:, t, :]))
                V.tensor_tensor(normed[:, t, :].rearrange("p (h e) -> p h e", h=H), heads[:, :, 0:HD],
                                inv[:, t, :].unsqueeze(2).broadcast_to([P, H, HD]), ALU.mult).then_inc(normalised, 1)
            dve.wait_ge(back, 1)
            V.tensor_copy(mixedT[:, 1, :], ps[:, 5, :]).then_inc(back_dve, 1)
            bo = c.rows[:, ROW["bo"]:ROW["bo"] + D]
            for t in range(TT):
                dve.wait_ge(projected, 2 * (t // 2) + 2)
                settle(dve, own, V.tensor_tensor(biased[:, t, :], ps[:, 6 + t // 2, (t % 2) * D:(t % 2 + 1) * D], bo,
                                                 ALU.add))
                V.scalar_tensor_tensor(out=c.x[:, t, :], in0=biased[:, t, :], scalar=c.gate[:, 2:3],
                                       in1=c.x[:, t, :], op0=ALU.mult, op1=ALU.add).then_inc(added, 1)
            dve.wait_ge(added, TT)


def l2_self_attention(nc, c, d, z, residual):
    SCALE = 1.0 / float(np.sqrt(np.float32(P)))
    PW = 3 * 2 * KT * P + 2 * D
    QKV = 3 * 2 * KT * P
    PAIRS = H // 2
    ps = c.ps
    Q, K, SC, TR, ACC = 0, 1, 2, 4, 6
    with ExitStack() as ctx:
        def sb(n, shape, dt=F32):
            return ctx.enter_context(nc.sbuf_tensor("l2a_" + n, shape, dt))

        sem = stage_semaphores(nc, ctx, "l2a")
        w = sb("w", [P, 2, PW])
        qT, kT, v = sb("qT", [P, T]), sb("kT", [P, T]), sb("v", [P, 2, TT, 2 * P])
        probs, probsT, mixT = sb("probs", [P, B, 3 * P]), sb("probsT", [P, B, 3 * P]), sb("mixT", [P, T])
        top, bias = sb("top", [P, B, 2]), sb("bias", [P, B, 2])
        total, inv = sb("total", [P, B, 2]), sb("inv", [P, B, 2])
        loaded, wo_loaded = [sem("loaded0"), sem("loaded1")], [sem("wo_loaded0"), sem("wo_loaded1")]
        q_done, k_done, v_done, scored = sem("q_done"), sem("k_done"), sem("v_done"), sem("scored")
        q_kept, k_kept, v_kept = sem("q_kept"), sem("k_kept"), sem("v_kept")
        topped, biased, exped, scaled = sem("topped"), sem("biased"), sem("exped"), sem("scaled")
        inverted = sem("inverted")
        turned, turn_kept, mixed, mix_kept = sem("turned"), sem("turn_kept"), sem("mixed"), sem("mix_kept")
        projected, added = sem("projected"), sem("added")
        block = ctx.enter_context(nc.Block(no_gpsimd_drain=True))

        def static(h):
            return isinstance(h, int)

        @block.sync
        def _(sp):
            for s in range(2):
                sp.dma_start(w[:, s, 0:QKV], d["l2a_w"][s, :, 0:QKV]).then_inc(loaded[s], 16)
                sp.dma_start(w[:, s, QKV:PW], d["l2a_w"][s, :, QKV:PW]).then_inc(wo_loaded[s], 16)

            def load(pair, slot):
                src = d["l2a_w"][bass.ds(pair, 1)].rearrange("a p n -> p (a n)")
                sp.wait_ge(k_done, 2 * pair - 2)
                sp.dma_start(w[:, slot, 0:QKV], src[:, 0:QKV]).then_inc(loaded[slot], 16)
                sp.wait_ge(projected, 2 * pair - 2)
                sp.dma_start(w[:, slot, QKV:PW], src[:, QKV:PW]).then_inc(wo_loaded[slot], 16)
            repeat(sp, 2, PAIRS, 2, load)

        @block.tensor
        def _(pe):
            for i in range(2):
                nc.tensor.matmul(ps[:, ACC + i, :], c.zero_bf[:, 0:P], c.zero_bf[:], start=True, stop=True,
                                 skip_group_check=True)

            def weights(h, phase, which, k):
                at = which * 512 + k * 256 + (phase % 2) * P
                return w[:, phase // 2 % 2, at:at + P]

            def queries_keys(h, phase):
                if static(h) and h < 4:
                    pe.wait_ge(loaded[phase // 2 % 2], 16)
                else:
                    pe.wait_ge(loaded[phase // 2 % 2], (h - phase % 4) * 4 + 16)
                if not static(h) or h >= 2:
                    pe.wait_ge(mix_kept, h - 1)
                for k in range(KT):
                    last = nc.tensor.matmul(ps[:, Q, :], weights(h, phase, 0, k), c.hT[:, k, :],
                                            start=k == 0, stop=k == KT - 1)
                last.then_inc(q_done, 1)
                if not static(h) or h >= 1:
                    pe.wait_ge(v_kept, h + 1)
                for k in range(KT):
                    last = nc.tensor.matmul(ps[:, K, :], weights(h, phase, 1, k), c.hT[:, k, :],
                                            start=k == 0, stop=k == KT - 1)
                last.then_inc(k_done, 1)

            def values(n, phase, k_ready):
                slot = phase // 2 % 2
                if static(n) and n < 4:
                    pe.wait_ge(loaded[slot], 16)
                else:
                    pe.wait_ge(loaded[slot], (n - phase % 4) * 4 + 16)
                pe.wait_ge(k_kept, k_ready)
                for i in range(2):
                    t = 2 * (phase % 2) + i
                    for k in range(KT):
                        last = nc.tensor.matmul(ps[:, K, i * D:(i + 1) * D], c.hT[:, k, t * P:(t + 1) * P],
                                                w[:, slot, 1024 + k * 256:1024 + k * 256 + 256],
                                                start=k == 0, stop=k == KT - 1)
                last.then_inc(v_done, 1)

            def scores(h):
                pe.wait_ge(q_kept, h + 1)
                pe.wait_ge(k_kept, h + 1)
                for b in range(B):
                    if not static(h) or h >= 1:
                        pe.wait_ge(exped, 4 * h - 2 + 2 * b)
                    for half in range(2):
                        to = ps[:, SC + b, half * P:half * P + (half + 1) * P]
                        q0 = b * S + half * P
                        nc.tensor.matmul(to, qT[:, q0:q0 + P], kT[:, b * S:b * S + (half + 1) * P],
                                         start=True, stop=False)
                        last = nc.tensor.matmul(to[:, half * P:(half + 1) * P], c.ident_bf[:], c.mask_q[:],
                                                start=False, stop=True)
                    last.then_inc(scored, 1)

            def turn(h):
                for b in range(B):
                    pe.wait_ge(scaled, 4 * h + 2 * b + 2)
                    if not static(h) or h >= 1:
                        pe.wait_ge(turn_kept, 2 * h + b - 1)
                    for i in range(3):
                        last = nc.tensor.transpose(ps[:, TR + b, i * P:(i + 1) * P], probs[:, b, i * P:(i + 1) * P],
                                                   c.ident[:])
                    last.then_inc(turned, 1)

            def mix(h, phase, more):
                pair_slot = phase // 2 % 2
                pe.wait_ge(q_kept, h + 2 if more else h + 1)
                pe.wait_ge(v_kept, h + 2 - phase % 2)
                for b in range(B):
                    pe.wait_ge(turn_kept, 2 * h + b + 1)
                    for half in range(2):
                        at = b * S + half * P
                        src = probsT[:, b, 0:2 * P] if half == 0 else probsT[:, b, 2 * P:3 * P]
                        last = nc.tensor.matmul(ps[:, Q, at:(b + 1) * S],
                                                v[:, pair_slot, 2 * b + half, (phase % 2) * P:(phase % 2 + 1) * P],
                                                src, start=half == 0, stop=half == 1)
                last.then_inc(mixed, 1)

            def project(h, phase):
                pe.wait_ge(mix_kept, h + 1)
                if static(h) and h < 4:
                    pe.wait_ge(wo_loaded[phase // 2 % 2], 16)
                else:
                    pe.wait_ge(wo_loaded[phase // 2 % 2], (h - phase % 4) * 4 + 16)
                for t in range(TT):
                    last = nc.tensor.matmul(ps[:, ACC + t // 2, (t % 2) * D:(t % 2 + 1) * D],
                                            mixT[:, t * P:(t + 1) * P],
                                            w[:, phase // 2 % 2, 1536 + (phase % 2) * D:1536 + (phase % 2 + 1) * D],
                                            start=False, stop=True, skip_group_check=True)
                last.then_inc(projected, 1)

            def step(h, phase, more=True, more_v=True):
                if more:
                    queries_keys(h + 1, (phase + 1) % 4)
                turn(h)
                if more_v:
                    values(h + 2, (phase + 2) % 4, h + 2)
                mix(h, phase, more)
                if more:
                    scores(h + 1)
                project(h, phase)

            queries_keys(0, 0)
            values(0, 0, 1)
            scores(0)
            pe.wait_ge(v_kept, 1)
            values(1, 1, 1)
            for h in range(1):
                step(h, h)
            repeat(pe, 1, H - 2, 4, step)
            step(H - 2, (H - 2) % 4, True, False)
            step(H - 1, (H - 1) % 4, False, False)

        @block.scalar
        def _(act):
            def keep_q(h):
                act.wait_ge(q_done, h + 1)
                nc.scalar.copy(qT[:], ps[:, Q, :]).then_inc(q_kept, 1)

            def keep_v(n, phase):
                act.wait_ge(v_done, n + 1)
                if not static(n) or n >= 4:
                    act.wait_ge(mixed, n - phase % 2 - 2)
                nc.scalar.copy(v[:, phase // 2 % 2, 2 * (phase % 2):2 * (phase % 2) + 2, :],
                               ps[:, K, :].rearrange("p (t n) -> p t n", t=2)).then_inc(v_kept, 1)

            def exponentials(h):
                for b in range(B):
                    for half in range(2):
                        at, width = half * P, (half + 1) * P
                        act.wait_ge(biased, 4 * h + 2 * b + half + 1)
                        if not static(h) or h >= 1:
                            act.wait_ge(turned, 2 * h + b - 1)
                        nc.scalar.activation(probs[:, b, at:at + width], ps[:, SC + b, at:at + width], ACT.Exp,
                                             bias=bias[:, b, half:half + 1], scale=SCALE,
                                             accum_out=total[:, b, half:half + 1]).then_inc(exped, 1)

            def step(h, phase, more=True, more_v=True):
                exponentials(h)
                if more:
                    keep_q(h + 1)
                if more_v:
                    keep_v(h + 2, (phase + 2) % 4)
            keep_q(0)
            keep_v(0, 0)
            keep_v(1, 1)
            step(0, 0)
            repeat(act, 1, H - 2, 4, step)
            step(H - 2, (H - 2) % 4, True, False)
            step(H - 1, (H - 1) % 4, False, False)

        @block.vector
        def _(dve):
            V = nc.vector

            def keep_k(h):
                dve.wait_ge(k_done, h + 1)
                V.tensor_copy(kT[:], ps[:, K, :]).then_inc(k_kept, 1)

            def maxima(h):
                for b in range(B):
                    dve.wait_ge(scored, 2 * h + b + 1)
                    for half in range(2):
                        at, width = half * P, (half + 1) * P
                        V.tensor_reduce(top[:, b, half:half + 1], ps[:, SC + b, at:at + width], AX.X, ALU.max)\
                            .then_inc(topped, 1)
                for b in range(B):
                    for half in range(2):
                        dve.wait_ge(topped, 4 * h + 2 * b + half + 1)
                        V.tensor_scalar(bias[:, b, half:half + 1], top[:, b, half:half + 1], -SCALE, None, ALU.mult)\
                            .then_inc(biased, 1)

            def normalise(h):
                for b in range(B):
                    dve.wait_ge(exped, 4 * h + 2 * b + 2)
                    V.reciprocal(inv[:, b, :], total[:, b, :]).then_inc(inverted, 1)
                    dve.wait_ge(inverted, 2 * h + b + 1)
                    for half in range(2):
                        at, width = half * P, (half + 1) * P
                        V.tensor_scalar(probs[:, b, at:at + width], probs[:, b, at:at + width],
                                        inv[:, b, half:half + 1], None, ALU.mult).then_inc(scaled, 1)

            def keep_turned(h):
                for b in range(B):
                    dve.wait_ge(turned, 2 * h + b + 1)
                    V.tensor_copy(probsT[:, b, :], ps[:, TR + b, 0:3 * P]).then_inc(turn_kept, 1)

            def keep_mixed(h):
                dve.wait_ge(mixed, h + 1)
                if not static(h) or h >= 1:
                    dve.wait_ge(projected, h)
                V.tensor_copy(mixT[:], ps[:, Q, :]).then_inc(mix_kept, 1)

            def step(h, phase, more=True, more_v=True):
                maxima(h)
                normalise(h)
                if more:
                    keep_k(h + 1)
                keep_turned(h)
                keep_mixed(h)
            keep_k(0)
            step(0, 0)
            repeat(dve, 1, H - 1, 4, step)
            step(H - 1, 3, False, False)
            dve.wait_ge(projected, H)
            for t in range(TT):
                V.tensor_tensor(residual[:, t, :], ps[:, ACC + t // 2, (t % 2) * D:(t % 2 + 1) * D], z[:, t, :],
                                ALU.add).then_inc(added, 1)
            dve.wait_ge(added, TT)



L3_COLS = {"q": (0, 256), "k": (256, 64), "v": (320, 64), "o": (384, 256)}
QB, QEPS = 127.0, 1e-5


def quantise(dve, V, own, y, scale):
    settle(dve, own, V.tensor_scalar(y, y, scale, QB - QEPS, ALU.mult, ALU.min))
    return V.tensor_scalar(y, y, -(QB - QEPS), None, ALU.max)


def l3_projections(nc, c, d, s):
    ps = c.ps
    with ExitStack() as ctx:
        def sb(n, shape, dt=F32):
            return ctx.enter_context(nc.sbuf_tensor("l3p_" + n, shape, dt))

        sem = stage_semaphores(nc, ctx, "l3p")
        sums, minus_mean, ones = sb("sums", [P, 4]), sb("minus_mean", [P, 4]), sb("ones", [P, P])
        w = sb("w", [P, KT, 640])
        yv = sb("yv", [P, CT, 64])
        largest, all_largest, scale = sb("largest", [P, 4]), sb("all_largest", [P, 4]), sb("scale", [P, 4])
        loaded, ones_ready, summed, mean_done, mean_ready, signed = \
            sem("loaded"), sem("ones_ready"), sem("summed"), sem("mean_done"), sem("mean_ready"), sem("signed")
        q_done, k_done, v_done, kept_act, reduced, all_reduced, out = \
            sem("q_done"), sem("k_done"), sem("v_done"), sem("kept_act"), sem("reduced"), sem("all_reduced"), sem("out")
        own = Tally(sem("own"))
        block = ctx.enter_context(nc.Block(no_gpsimd_drain=True))

        @block.sync
        def _(sp):
            sp.dma_start(w[:], d["l3_w"].rearrange("k p n -> p k n")).then_inc(loaded, 16)

        @block.gpsimd
        def _(pool):
            nc.gpsimd.memset(ones[:], 1.0).then_inc(ones_ready, 1)
            nc.gpsimd.memset(s.values[:, :, :, HD:HD + 1], 1.0).then_inc(ones_ready, 1)
            nc.gpsimd.memset(s.values[:, :, :, HD + 1:32], 0.0).then_inc(ones_ready, 1)
            nc.gpsimd.memset(largest[:], 0.0).then_inc(ones_ready, 1)
            pool.wait_ge(reduced, 1)
            nc.gpsimd.partition_all_reduce(all_largest[:], largest[:], P, bass.bass_isa.ReduceOp.max)\
                .then_inc(all_reduced, 1)

        @block.tensor
        def _(pe):
            pe.wait_ge(ones_ready, 1)
            pe.wait_ge(summed, 1)
            nc.tensor.matmul(ps[:, 7, 0:4], ones[:], sums[:], start=True, stop=True).then_inc(mean_done, 1)
            pe.wait_ge(signed, 4)
            for m in range(KT):
                for k in range(KT):
                    last = nc.tensor.matmul(ps[:, m, :], s.w_bin[:, k, m * P:(m + 1) * P], c.hT[:, k, :],
                                            start=k == 0, stop=k == KT - 1)
                last.then_inc(q_done, 1)
            for half in range(2):
                for k in range(KT):
                    last = nc.tensor.matmul(ps[0:64, 2 + half, :], s.w_bin[:, k, 256:320],
                                            c.ctxT[:, k, half * CTX:(half + 1) * CTX], start=k == 0, stop=k == KT - 1)
                last.then_inc(k_done, 1)
            for t in range(CT):
                for k in range(KT):
                    last = nc.tensor.matmul(ps[:, 4, t * 64:(t + 1) * 64], c.ctxT[:, k, t * P:(t + 1) * P],
                                            s.w_bin[:, k, 320:384], start=k == 0, stop=k == KT - 1)
            last.then_inc(v_done, 1)

        def col(n, k, rows=P):
            return c.cols[0:rows, COL[n] + k:COL[n] + k + 1]

        @block.scalar
        def _(act):
            act.wait_ge(mean_ready, 1)
            for i, (at, n) in enumerate(L3_COLS.values()):
                nc.scalar.activation(s.w_bin[:, :, at:at + n], w[:, :, at:at + n], ACT.Sign,
                                     bias=minus_mean[:, i:i + 1]).then_inc(signed, 1)
            for m in range(KT):
                act.wait_ge(q_done, m + 1)
                nc.scalar.activation(s.qT[:, m, :], ps[:, m, :], ACT.Identity, bias=col("q_b", m)).then_inc(kept_act, 1)
            for half in range(2):
                act.wait_ge(k_done, half + 1)
                nc.scalar.activation(s.kT[:, half * CTX:(half + 1) * CTX], ps[0:64, 2 + half, :], ACT.Identity,
                                     bias=col("k_b", 0, 64)).then_inc(kept_act, 1)

        @block.vector
        def _(dve):
            V = nc.vector
            dve.wait_ge(loaded, 16)
            for i, (at, n) in enumerate(L3_COLS.values()):
                last = own.up(V.tensor_reduce(sums[:, i:i + 1], w[:, :, at:at + n], AX.XY, ALU.add))
            dve.wait_ge(own.sem, last)
            V.tensor_copy(minus_mean[:], sums[:]).then_inc(summed, 1)
            dve.wait_ge(mean_done, 1)
            dve.wait_ge(summed, 1)
            for i, (_, n) in enumerate(L3_COLS.values()):
                last = own.up(V.tensor_scalar(minus_mean[:, i:i + 1], ps[:, 7, i:i + 1], -1.0 / (D * n), None, ALU.mult))
            dve.wait_ge(own.sem, last)
            V.tensor_copy(scale[:], minus_mean[:]).then_inc(mean_ready, 1)
            dve.wait_ge(mean_ready, 1)
            vb = c.rows[:, ROW["v_b"]:ROW["v_b"] + 64].unsqueeze(1).broadcast_to([P, CT, 64])
            dve.wait_ge(v_done, 1)
            settle(dve, own, V.tensor_tensor(yv[:], ps[:, 4, :].rearrange("p (t n) -> p t n", t=CT), vb, ALU.add))
            dve.wait_ge(ones_ready, 4)
            own.up(V.tensor_reduce(largest[:, 2:3], yv[:], AX.XY, ALU.max, apply_absolute_value=True))
            dve.wait_ge(kept_act, 4)
            own.up(V.tensor_reduce(largest[:, 0:1], s.qT[:], AX.XY, ALU.max, apply_absolute_value=True))
            last = own.up(V.tensor_reduce(largest[0:64, 1:2], s.kT[:], AX.X, ALU.max, apply_absolute_value=True))
            dve.wait_ge(own.sem, last)
            V.tensor_copy(sums[:], largest[:]).then_inc(reduced, 1)
            dve.wait_ge(all_reduced, 1)
            settle(dve, own, V.tensor_scalar(scale[:], all_largest[:], QEPS, None, ALU.add))
            settle(dve, own, V.reciprocal(scale[:], scale[:]))
            settle(dve, own, V.tensor_scalar(scale[:], scale[:], QB, None, ALU.mult))
            quantise(dve, V, own, s.qT[:], scale[:, 0:1]).then_inc(out, 1)
            quantise(dve, V, own, s.kT[:], scale[0:64, 1:2]).then_inc(out, 1)
            settle(dve, own, V.tensor_scalar(yv[:], yv[:], scale[:, 2:3], QB - QEPS, ALU.mult, ALU.min))
            V.tensor_scalar(s.values[:, :, :, 0:HD], yv[:].rearrange("p t (h e) -> p t h e", h=4),
                            -(QB - QEPS), None, ALU.max).then_inc(out, 1)
            dve.wait_ge(out, 3)


def l3_output(nc, c, d, s):
    ps = c.ps
    with ExitStack() as ctx:
        def sb(n, shape, dt=F32):
            return ctx.enter_context(nc.sbuf_tensor("l3o_" + n, shape, dt))

        sem = stage_semaphores(nc, ctx, "l3o")
        y, largest, all_largest, scale = sb("y", [P, TT, D]), sb("largest", [P, 2]), sb("all", [P, 2]), sb("scale", [P, 2])
        done, reduced, all_reduced, added = sem("done"), sem("reduced"), sem("all_reduced"), sem("added")
        own = Tally(sem("own"))
        block = ctx.enter_context(nc.Block(no_gpsimd_drain=True))

        @block.tensor
        def _(pe):
            for t in range(TT):
                for k in range(KT):
                    last = nc.tensor.matmul(ps[:, t, 0:D], c.hT[:, k, t * P:(t + 1) * P], s.w_bin[:, k, 384:640],
                                            start=k == 0, stop=k == KT - 1)
                last.then_inc(done, 1)

        @block.gpsimd
        def _(pool):
            pool.wait_ge(reduced, 1)
            nc.gpsimd.partition_all_reduce(all_largest[:, 0:1], largest[:, 0:1], P, bass.bass_isa.ReduceOp.max)\
                .then_inc(all_reduced, 1)

        @block.vector
        def _(dve):
            V = nc.vector
            ob = c.rows[:, ROW["o_b"]:ROW["o_b"] + D]
            for t in range(TT):
                dve.wait_ge(done, t + 1)
                last = own.up(V.tensor_tensor(y[:, t, :], ps[:, t, 0:D], ob, ALU.add))
            dve.wait_ge(own.sem, last)
            V.tensor_reduce(largest[:, 0:1], y[:], AX.XY, ALU.max, apply_absolute_value=True).then_inc(reduced, 1)
            dve.wait_ge(all_reduced, 1)
            settle(dve, own, V.tensor_scalar(scale[:, 0:1], all_largest[:, 0:1], QEPS, None, ALU.add))
            settle(dve, own, V.reciprocal(scale[:, 0:1], scale[:, 0:1]))
            settle(dve, own, V.tensor_scalar(scale[:, 0:1], scale[:, 0:1], QB, None, ALU.mult))
            settle(dve, own, quantise(dve, V, own, y[:], scale[:, 0:1]))
            V.scalar_tensor_tensor(out=flat(c.x[:]), in0=flat(y[:]), scalar=c.gate[:, 3:4], in1=flat(c.x[:]),
                                   op0=ALU.mult, op1=ALU.add).then_inc(added, 1)
            dve.wait_ge(added, 1)


def l3_attention(nc, c, d):
    s = Core()
    with ExitStack() as ctx:
        def sb(n, shape, dt=F32):
            return ctx.enter_context(nc.sbuf_tensor("l3x_" + n, shape, dt))
        s.w_bin = sb("w_bin", [P, KT, 640])
        finished = stage_semaphores(nc, ctx, "l3x")("placed")
        with ExitStack() as inner:
            s.qT = inner.enter_context(nc.sbuf_tensor("l3x_qT", [P, KT, T], F32))
            s.kT = inner.enter_context(nc.sbuf_tensor("l3x_kT", [64, B * CTX], F32))
            s.values = inner.enter_context(nc.sbuf_tensor("l3x_values", [P, CT, 4, 32], F32))
            l3_projections(nc, c, d, s)

            def finish(dve, own, t, heads, inv):
                nc.vector.tensor_tensor(c.z[:, t, :].rearrange("p (h e) -> p h e", h=H), heads, inv, ALU.mult)\
                    .then_inc(finished, 1)
                if t == TT - 1:
                    dve.wait_ge(finished, TT)
            small_head_attention(nc, c, "l3x", s.qT, s.kT, s.values, 4, False, None, finish)
        norm_stage(nc, c, "l3x_ln", c.z, c.h, LN_EPS, c.hT, scale="ln_g", shift="ln_b")
        l3_output(nc, c, d, s)


LAYERS = (1, 8)


def make_plan(nc, c, d):
    layers = [
        [lambda: norm_stage(nc, c, "l0x_norm", c.x, c.h, LN_EPS, c.hT),
         lambda: l0_attention(nc, c, d)],
        [lambda: norm_stage(nc, c, "l0f_norm", c.x, c.h, LN_EPS, c.hT, even_odd=True),
         lambda: ffn_stage(nc, c, d, "l0")],
        [lambda: norm_stage(nc, c, "l1x_norm", c.x, c.h, LN_EPS, c.hT),
         lambda: l1_attention(nc, c, d)],
        [lambda: norm_stage(nc, c, "l1f_norm", c.x, c.h, LN_EPS, c.hT, prefetch=load_expert_tiles(nc, c, d, "l1")),
         lambda: router_stage(nc, c, d, "l1"),
         lambda: ffn_stage(nc, c, d, "l1")],
        [lambda: norm_stage(nc, c, "l2x_norm", c.x, c.h, LN_EPS, c.hT),
         lambda: l2_linear_attention(nc, c, d)],
        [lambda: norm_stage(nc, c, "l2z_norm", c.x, c.z, LN_EPS),
         lambda: norm_stage(nc, c, "l2a_norm", c.z, c.h, RMS_EPS, c.hT, rms=True, scale="ln1_w"),
         lambda: l2_self_attention(nc, c, d, c.z, c.z2),
         lambda: norm_stage(nc, c, "l2f_norm", c.z2, c.h, RMS_EPS, c.hT, rms=True, scale="ln2_w",
                            prefetch=load_expert_tiles(nc, c, d, "l2")),
         lambda: router_stage(nc, c, d, "l2"),
         lambda: ffn_stage(nc, c, d, "l2", residual=c.z2)],
        [lambda: norm_stage(nc, c, "l3x_norm", c.x, c.h, LN_EPS, c.hT),
         lambda: l3_attention(nc, c, d)],
        [lambda: norm_stage(nc, c, "l3f_norm", c.x, c.h, LN_EPS, c.hT, prefetch=load_expert_tiles(nc, c, d, "l3")),
         lambda: router_stage(nc, c, d, "l3"),
         lambda: ffn_stage(nc, c, d, "l3")],
    ]
    return [stage for layer in layers[LAYERS[0] - 1:LAYERS[1]] for stage in layer]


def build(nc, d, out, stages=99):
    c = Core()
    with ExitStack() as ctx:
        def sb(name, shape, dt=F32):
            return ctx.enter_context(nc.sbuf_tensor(name, shape, dt))
        c.x, c.h, c.hT = sb("x", [P, TT, D]), sb("h", [P, TT, D]), sb("hT", [P, KT, T])
        c.ctxT, c.ctx = sb("ctxT", [P, KT, B * CTX]), sb("ctx_tok", [P, CT, D])
        c.cols, c.rows, c.gate = sb("cols", [P, N_COLS]), sb("rows", [P, N_ROWS]), sb("gate", [P, 8])
        c.z, c.z2 = sb("z", [P, TT, D]), sb("z2", [P, TT, D])
        c.att_mask = sb("att_mask", [P, CT])
        c.ident, c.ident_bf = sb("ident", [P, P]), sb("ident_bf", [P, P], BF16)
        c.mask_q, c.mask_k = sb("mask_q", [P, P], BF16), sb("mask_k", [P, P], BF16)
        c.zero_bf, c.minus_half = sb("zero_bf", [P, 512], BF16), sb("minus_half", [P, 8])
        c.ps = ctx.enter_context(nc.psum_tensor("ps", [P, 8, 512], F32))
        c.before, c.routers, c.weightT = sb("before", [P, 16, 16]), sb("routers", [P, KT, 32]), sb("weightT", [P, T], BF16)
        c.slots = sb("slots", [P, SLOTS, FW])
        c.slot_loaded = [ctx.enter_context(nc.semaphore(f"slot_loaded{s}")) for s in range(SLOTS)]
        c.slot_loads = [0] * SLOTS
        c.dve_pairs, c.dve_pairs_n = ctx.enter_context(nc.semaphore("tiles_gated")), 0
        setup_stage(nc, c, d)
        plan = make_plan(nc, c, d)
        for step in plan[:stages]:
            step()
        stored = ctx.enter_context(nc.semaphore("stored"))
        with nc.Block(no_gpsimd_drain=True) as block:
            @block.sync
            def _(sp):
                sp.dma_start(out.rearrange("t p n -> p t n"), c.x[:]).then_inc(stored, 16)
                sp.wait_ge(stored, 16)


def layout(i):
    a = {k: np.asarray(v) for k, v in i.items()}
    o = {}

    def cols(v):
        v = v.reshape(-1)
        if v.size < D:
            v = np.concatenate([v, np.zeros(D - v.size, v.dtype)])
        return v.reshape(KT, P).T

    o["x"] = a["x"].reshape(TT, P, D)
    o["ctx"] = a["ctx_2048"].reshape(CT, P, D)
    o["ctx_t"] = a["ctx_2048"].reshape(B * CTX, D).T.reshape(KT, P, B * CTX)
    o["cols"] = np.concatenate([cols(a[n]) for n in (
        "L2_ffn_ln1_w", "L2_ffn_ln2_w", "L3_ffn_router_scale", "L2_xattn_bq", "L2_xattn_bk",
        "L3_xattn_ln_g", "L3_xattn_ln_b", "L3_xattn_q_b", "L3_xattn_k_b")], axis=1)
    o["rows"] = np.concatenate([a[n].reshape(-1) for n in (
        "g_xattn", "g_ffn", "L2_xattn_bv", "L2_xattn_bo", "L3_xattn_o_b", "L3_xattn_v_b",
        "L3_ffn_per_expert_scale")])[None]
    o["att_mask"] = a["mask_BxS2_ff1"].reshape(CT, P).T
    o["l0_w"] = np.stack([a["L0_xattn_" + n].T.reshape(KT, P, D) for n in ("wq", "wk", "wv", "wo")])
    o["l2_w"] = np.stack([a["L2_xattn_" + n].T.reshape(KT, P, D) for n in ("Wq", "Wk", "Wv", "Wo")])
    for name, f in (("fm_q", a["L2_xattn_Wqf"]), ("fm_k", a["L2_xattn_Wkf"])):
        m = np.zeros((P, 512), f.dtype)
        for h in range(8):
            m[16 * h:16 * h + 16, 64 * h:64 * h + 64] = f.T
        o[name] = m

    def fp4_gate(w):
        return w.reshape(8, P, 2, P).transpose(0, 3, 2, 1)
    g, u = fp4_gate(a["L0_ffn_gate_W_packed"]), fp4_gate(a["L0_ffn_up_W_packed"])
    dn = a["L0_ffn_down_W_packed"].reshape(D, 8, P).transpose(1, 2, 0)
    o["fp4_w"] = np.concatenate([np.stack([g, u], 3).reshape(8, P, 512), dn], axis=2)
    gs = a["L0_ffn_gate_scales"].reshape(8, P, 2, 8).transpose(0, 3, 2, 1)
    us = a["L0_ffn_up_scales"].reshape(8, P, 2, 8).transpose(0, 3, 2, 1)
    ds = a["L0_ffn_down_scales"].reshape(D, 8, 8).transpose(1, 2, 0)
    o["fp4_s"] = np.concatenate([np.stack([gs, us], 3).reshape(8, 8, 512), ds], axis=2)

    def tiles(gate, up, down, n):
        pad = n * P - gate.shape[0]
        gate, up, down = (np.concatenate([m, np.zeros((pad, D), m.dtype)]) for m in (gate, up, down))
        gu = np.stack([gate, up]).reshape(2, n, P, KT, P).transpose(1, 4, 3, 0, 2).reshape(n, P, 4 * P)
        return np.concatenate([gu, down.reshape(n, P, D)], axis=2)

    def moe(gw, uw, dw, sg, su, sd, n):
        return tiles(np.concatenate([gw.reshape(-1, D), sg]), np.concatenate([uw.reshape(-1, D), su]),
                     np.concatenate([dw.transpose(0, 2, 1).reshape(-1, D), sd.T]), n)
    l1 = moe(*(a["L1_ffn_" + n] for n in ("gate_w", "up_w", "down_w", "sh_gate_w", "sh_up_w", "sh_down_w")), 14)
    l2 = moe(*(a["L2_ffn_" + n] for n in ("eg_w", "eu_w", "ed_w", "sg_w", "su_w", "sd_w")), 25)
    gu = a["L3_ffn_gate_up"].transpose(0, 2, 1)
    l3 = tiles(gu[:, 0:256].reshape(-1, D), gu[:, 256:512].reshape(-1, D), a["L3_ffn_down"].reshape(-1, D), 16)
    o["moe_w"] = np.concatenate([l1, l2, l3])
    rt = [a["L1_ffn_gate_weight"].T, a["L2_ffn_gate_w"].T, a["L3_ffn_gate_w"]]
    o["routers"] = np.concatenate([r.reshape(KT, P, -1) for r in rt], axis=2)
    sel = np.zeros((P, MOE_TILES * P), np.uint16)
    for name, (n, e, per) in MOE.items():
        unit = np.arange(n * P)
        real = {"l1": 1760, "l2": 3168, "l3": 2048}[name]
        for part in range(3):
            row = np.minimum(unit // per, e) + part * (e + 1)
            sel[row[:real], MOE_AT[name] * P + unit[:real]] = ONE_BF16
    o["sel"] = sel

    def heads(w):
        return w.reshape(KT, P, 8, 256).transpose(2, 1, 0, 3).reshape(8, P, 512)
    wo = a["L2_ffn_wo"].reshape(8, 2, P, D).transpose(0, 2, 1, 3).reshape(8, P, 512)
    o["l2a_w"] = np.concatenate([heads(a["L2_ffn_" + n]) for n in ("wq", "wk", "wv")] + [wo], axis=2)
    o["l3_w"] = np.concatenate([a["L3_xattn_" + n].T.reshape(KT, P, -1) for n in ("q_w", "k_w", "v_w", "o_w")], axis=2)
    return {k: np.ascontiguousarray(v) for k, v in o.items()}


def kernel(**inputs):
    import concourse.bacc as _bacc
    from concourse.bass_utils import run_bass_kernel_spmd as _run

    arrays = layout(inputs)
    nc = _bacc.Bacc("TRN2", target_bir_lowering=False, num_devices=1)
    d = {k: nc.dram_tensor("in_" + k, v.shape, mybir.dt.from_np(v.dtype), kind="ExternalInput").ap()
         for k, v in arrays.items()}
    out = nc.dram_tensor("out_x", (TT, P, D), F32, kind="ExternalOutput").ap()
    build(nc, d, out)
    r = _run(nc, [{"in_" + k: v for k, v in arrays.items()}], core_ids=[0])
    return np.asarray(r.results[0]["out_x"]).reshape(B, S, D)
```

```python
from contextlib import ExitStack

import numpy as np

import concourse.bass as bass
from concourse import mybir

ALU = mybir.AluOpType
ACT = mybir.ActivationFunctionType
AX = mybir.AxisListType
F32 = mybir.dt.float32
F32R = mybir.dt.float32r
F16 = mybir.dt.float16
BF16 = mybir.dt.bfloat16
I32 = mybir.dt.int32
U16 = mybir.dt.uint16

P = 128
B, S, D = 2, 256, 256
CTX = 512
TT = B * S // P
CT = B * CTX // P
KT = D // P
T = B * S
H = 16
HD = D // H
LN_EPS, RMS_EPS = 1e-5, 1e-6
MASKED = -1e30

COLS = ["ln1_w", "ln2_w", "router_scale", "bq", "bk", "ln_g", "ln_b", "q_b", "k_b"]
COL = {n: 2 * i for i, n in enumerate(COLS)}
N_COLS = 2 * len(COLS)
ROWS = [("g_xattn", 4), ("g_ffn", 4), ("bv", D), ("bo", D), ("o_b", D), ("v_b", 64), ("expert_scale", 8)]
ROW, N_ROWS = {}, 0
for _n, _w in ROWS:
    ROW[_n] = N_ROWS
    N_ROWS += _w

FW = 2 * KT * P + D
MOE = {"l1": (14, 8, 176), "l2": (25, 16, 176), "l3": (16, 8, 256)}
MOE_AT = {"l1": 0, "l2": 14, "l3": 39}
MOE_TILES = 55
ONE_BF16 = 0x3F80
SLOTS = 4


class Tally:

    def __init__(self, sem):
        self.sem, self.n = sem, 0

    def up(self, ins):
        ins.then_inc(self.sem, 1)
        self.n += 1
        return self.n


def settle(eng, tally, ins):
    eng.wait_ge(tally.sem, tally.up(ins))


def stage_semaphores(nc, ctx, prefix):
    taken = []

    def sem(name):
        taken.append(nc.alloc_semaphore(name=f"{prefix}_{name}"))
        return taken[-1]

    def give_back():
        nc.clear_and_free_semaphores(taken)
        nc.all_engine_barrier()
    ctx.callback(give_back)
    return sem


class Core:
    pass


def slot_view(c, shape):
    n = int(np.prod(shape))
    names = "abcd"[:len(shape)]
    sizes = {m: s for m, s in zip(names, shape)}
    return c.slots[:].rearrange("p s n -> p (s n)")[:, 0:n].rearrange(
        "p (" + " ".join(names) + ") -> p " + " ".join(names), **sizes)


def flat(ap):
    return ap.rearrange("p a b -> p (a b)")


def setup_stage(nc, c, d):
    with ExitStack() as ctx:
        sem = stage_semaphores(nc, ctx, "setup")
        zeroed, masks = sem("zeroed"), sem("masks")
        block = ctx.enter_context(nc.Block(no_gpsimd_drain=True))

        @block.sync
        def _(sp):
            sp.dma_start(c.x[:], d["x"].rearrange("t p n -> p t n")).then_inc(c.x_loaded, 16)
            sp.dma_start(slot_view(c, [4, KT, D]), d["l0_w"].rearrange("w k p n -> p w k n")).then_inc(c.early.sem, 16)
            c.early.n += 16
            sp.dma_start(c.rows[:], d["rows"].broadcast_to([P, N_ROWS])).then_inc(c.rows_loaded, 16)
            sp.dma_start(c.ctxT[:], d["ctx_t"].rearrange("k p n -> p k n")).then_inc(c.ctxT_loaded, 16)
            sp.wait_ge(c.x_loaded, 16)

        @block.gpsimd
        def _(pool):
            nc.gpsimd.memset(c.ident[:], 0.0).then_inc(zeroed, 1)
            nc.gpsimd.memset(c.ident_bf[:], 0.0).then_inc(zeroed, 1)
            nc.gpsimd.memset(c.mask_q[:], 0.0).then_inc(zeroed, 1)
            nc.gpsimd.memset(c.mask_k[:], 0.0).then_inc(zeroed, 1)
            nc.gpsimd.memset(c.zero_bf[:], 0.0).then_inc(zeroed, 1)
            nc.gpsimd.memset(c.minus_half[:], -0.5).then_inc(zeroed, 1)
            nc.gpsimd.memset(c.weightT[:], 0.0).then_inc(zeroed, 1)
            nc.gpsimd.memset(c.before[:], 1.0).then_inc(zeroed, 1)
            pool.wait_ge(zeroed, 8)
            nc.gpsimd.affine_select(out=c.before[:], in_=c.before[:], compare_op=ALU.is_gt, fill=0.0, base=0,
                                    pattern=[[1, 16], [-1, 16]], channel_multiplier=0).then_inc(masks, 1)
            for m in (c.ident, c.ident_bf):
                nc.gpsimd.affine_select(out=m[:], in_=m[:], compare_op=ALU.not_equal, fill=1.0, base=0,
                                        pattern=[[-1, P]], channel_multiplier=1).then_inc(masks, 1)
            nc.gpsimd.affine_select(out=c.mask_q[:], in_=c.mask_q[:], compare_op=ALU.is_ge, fill=MASKED, base=0,
                                    pattern=[[-1, P]], channel_multiplier=1).then_inc(masks, 1)
            nc.gpsimd.affine_select(out=c.mask_k[:], in_=c.mask_k[:], compare_op=ALU.is_ge, fill=MASKED, base=0,
                                    pattern=[[1, P]], channel_multiplier=-1).then_inc(masks, 1)
            pool.wait_ge(masks, 5)


def load_rest(sp, c, d):
    sp.dma_start(c.ctx[:], d["ctx"].rearrange("t p n -> p t n")).then_inc(c.inputs_loaded, 16)
    sp.dma_start(c.cols[:], d["cols"]).then_inc(c.inputs_loaded, 16)
    sp.dma_start(c.att_mask[:], d["att_mask"]).then_inc(c.inputs_loaded, 16)
    sp.dma_start(c.routers[:], d["routers"].rearrange("k p n -> p k n")).then_inc(c.inputs_loaded, 16)
    sp.dma_start(c.stack_sel[:].rearrange("p h a n -> p (h a n)").bitcast(U16), d["stack_sel"])\
        .then_inc(c.inputs_loaded, 16)
    sp.dma_start(c.fm[:, 0], d["fm_q"]).then_inc(c.kv_w_loaded, 16)
    sp.dma_start(c.fm[:, 1], d["fm_k"]).then_inc(c.kv_w_loaded, 16)
    sp.dma_start(c.kv_w[:], d["l2_w"][1:3].rearrange("w k p n -> p w k n")).then_inc(c.kv_w_loaded, 16)
    sp.dma_start(flat(c.z[:])[:, 0:FW].bitcast(I32), d["fp4_w"][0]).then_inc(c.fp4_loaded, 16)
    sp.dma_start(flat(c.z2[:])[:, 0:FW], d["fp4_s"][0].unsqueeze(1).broadcast_to([8, 16, FW]))\
        .then_inc(c.fp4_loaded, 16)


class Norm:

    def __init__(self, nc, c, ctx, tag, src, dst, eps, features_out=None, even_odd=False, rms=False, scale=None,
                 shift=None, cut=False):
        self.nc, self.c, self.src, self.dst, self.eps = nc, c, src, dst, eps
        self.features_out, self.even_odd, self.rms = features_out, even_odd, rms
        self.scale, self.shift, self.cut = scale, shift, cut
        sem = stage_semaphores(nc, ctx, tag)

        def sb(name, shape):
            return ctx.enter_context(nc.sbuf_tensor(f"{tag}_{name}", shape, F32))
        self.stats, self.moments = sb("stats", [P, TT, 6]), sb("moments", [P, TT, 2])
        self.var, self.rstd = sb("var", [P, TT]), sb("rstd", [P, TT])
        self.square = sb("square", [P, D]) if rms else None
        self.own = Tally(sem("own"))
        self.var_ready, self.rstd_ready, self.normed = sem("var_ready"), sem("rstd_ready"), sem("normed")
        self.turned, self.act_out, self.dve_out = sem("turned"), sem("act_out"), sem("dve_out")
        self.cut_ready = sem("cut_ready") if cut else None

    def ready(self, eng):
        eng.wait_ge(self.act_out, 2 if self.cut else 1)
        eng.wait_ge(self.dve_out, 3 if self.cut else 1)
        if self.cut:
            eng.wait_ge(self.cut_ready, 1)

    def evacuate(self, eng, k):
        c, out, nc = self.c, self.features_out, self.nc

        def col(n):
            return c.cols[:, COL[n] + k:COL[n] + k + 1]
        if self.scale is None:
            return (eng.copy if eng is nc.scalar else eng.tensor_copy)(out[:, k, :], c.ps[:, k, :])
        if eng is nc.scalar:
            bias = 0.0 if self.shift is None else col(self.shift)
            return eng.activation(out[:, k, :], c.ps[:, k, :], ACT.Identity, bias=bias, scale=col(self.scale))
        if self.shift is None:
            return eng.tensor_scalar(out[:, k, :], c.ps[:, k, :], col(self.scale), None, ALU.mult)
        return eng.tensor_scalar(out[:, k, :], c.ps[:, k, :], col(self.scale), col(self.shift), ALU.mult, ALU.add)

    def gpsimd(self, pool, root_only=False):
        pool.wait_ge(self.var_ready, 1)
        self.nc.gpsimd.tensor_tensor(self.rstd[:], self.var[:], self.c.minus_half[:, 0:TT], ALU.pow)\
            .then_inc(self.rstd_ready, 1)
        if self.cut and not root_only:
            self.gpsimd_cut(pool)

    def gpsimd_cut(self, pool):
        if self.cut:
            pool.wait_ge(self.act_out, 2)
            self.nc.gpsimd.tensor_tensor(self.c.h_rest[:, 0, :], self.features_out[:, 0, :], self.c.h_top[:, 0, :],
                                         ALU.subtract).then_inc(self.cut_ready, 1)

    def vector(self, dve):
        V, own, src, dst = self.nc.vector, self.own, self.src, self.dst
        if self.rms:
            for t in range(TT):
                settle(dve, own, V.tensor_tensor_reduce(
                    out=self.square[:], in0=src[:, t, :], in1=src[:, t, :], scale=1.0, scalar=0.0,
                    op0=ALU.mult, op1=ALU.add, accum_out=self.moments[:, t, 1:2]))
            V.tensor_scalar(self.var[:], self.moments[:, :, 1], 1.0 / D, self.eps, ALU.mult, ALU.add)\
                .then_inc(self.var_ready, 1)
        else:
            for t in range(TT):
                last = own.up(V.bn_stats(self.stats[:, t, :], src[:, t, :]))
            dve.wait_ge(own.sem, last)
            for t in range(TT):
                last = own.up(V.bn_aggr(self.moments[:, t, :], self.stats[:, t, :]))
            dve.wait_ge(own.sem, last)
            V.tensor_scalar(self.var[:], self.moments[:, :, 1], self.eps, None, ALU.add).then_inc(self.var_ready, 1)
        dve.wait_ge(self.rstd_ready, 1)
        for t in range(TT):
            if self.rms:
                V.tensor_scalar(dst[:, t, :], src[:, t, :], self.rstd[:, t:t + 1], None, ALU.mult)\
                    .then_inc(self.normed, 1)
            else:
                V.tensor_scalar(dst[:, t, :], src[:, t, :], self.moments[:, t, 0:1], self.rstd[:, t:t + 1],
                                ALU.subtract, ALU.mult).then_inc(self.normed, 1)
        if self.features_out is None:
            dve.wait_ge(self.normed, TT)
            return
        dve.wait_ge(self.turned, 1)
        self.evacuate(V, 1).then_inc(self.dve_out, 1)
        if self.cut:
            h_top, h_rest = self.c.h_top[:, 1, :], self.c.h_rest[:, 1, :]
            dve.wait_ge(self.dve_out, 1)
            V.tensor_copy(h_top, self.features_out[:, 1, :]).then_inc(self.dve_out, 1)
            dve.wait_ge(self.dve_out, 2)
            V.tensor_tensor(h_rest, self.features_out[:, 1, :], h_top, ALU.subtract).then_inc(self.dve_out, 1)

    def tensor(self, pe, wait=True):
        if self.features_out is None:
            return
        for t in range(TT):
            pe.wait_ge(self.normed, t + 1)
            for k in range(KT):
                piece = self.dst[:, t, k::2] if self.even_odd else self.dst[:, t, k * P:(k + 1) * P]
                last = self.nc.tensor.transpose(self.c.ps[:, k, t * P:(t + 1) * P], piece, self.c.ident[:])
        last.then_inc(self.turned, 1)
        if wait:
            self.ready(pe)

    def scalar(self, act):
        if self.features_out is None:
            return
        act.wait_ge(self.turned, 1)
        self.evacuate(self.nc.scalar, 0).then_inc(self.act_out, 1)
        if self.cut:
            act.wait_ge(self.act_out, 1)
            self.nc.scalar.copy(self.c.h_top[:, 0, :], self.features_out[:, 0, :]).then_inc(self.act_out, 1)


def l0_attention(nc, c, d, norm):
    SCALE = D ** -0.5
    KEYS = CTX + S
    NK = KEYS // P
    with ExitStack() as ctx:
        def sb(name, shape, dt=F32):
            return ctx.enter_context(nc.sbuf_tensor("l0x_" + name, shape, dt))

        sem = stage_semaphores(nc, ctx, "l0x")
        w = slot_view(c, [4, KT, D])
        early = c.early.n
        qT, knT, oT = sb("qT", [P, KT, T]), sb("knT", [P, KT, T]), sb("oT", [P, KT, T])
        vn = sb("vn", [P, TT, D])
        probs, probsT = sb("probs", [P, 2, KEYS]), sb("probsT", [P, NK, S])
        top, bias = sb("top", [P, TT]), sb("bias", [P, TT])
        total, inv, factor = sb("total", [P, TT]), sb("inv", [P, TT]), sb("factor", [P, TT])
        projected, act_kept, dve_kept = sem("projected"), sem("act_kept"), sem("dve_kept")
        scored, biased, exped = sem("scored"), sem("biased"), sem("exped")
        turned, mixed, mixed_act, mixed_dve = sem("turned"), sem("mixed"), sem("mixed_act"), sem("mixed_dve")
        turn_act, turn_dve = sem("turn_act"), sem("turn_dve")
        out_ready, added = sem("out_ready"), sem("added")
        own = Tally(sem("own"))
        ps = c.ps
        gates = sem("gates")
        norm = norm(ctx)
        keys = KeySplit(nc, ctx, sem, "l0x", c.ctxT, KT, P)
        block = ctx.enter_context(nc.Block(no_gpsimd_drain=True))

        @block.sync
        def _(sp):
            load_rest(sp, c, d)
            bounce_keys(sp, keys)
            stack_keys(sp, c, keys)
            sp.wait_ge(c.inputs_loaded, 80)

        @block.gpsimd
        def _(pool):
            norm.gpsimd(pool)
            pool.wait_ge(norm.rstd_ready, 1)
            pool.wait_ge(c.ctxT_loaded, 16)
            split_keys(pool, nc.gpsimd, keys)
            pool.wait_ge(keys.split, 1)
            settle(pool, keys.ones, nc.gpsimd.memset(c.k_stack[STACK:P], 1.0))
            settle(pool, keys.ones, nc.gpsimd.memset(c.values[:, :, :, HD:HD + 1], 1.0))
            settle(pool, keys.ones, nc.gpsimd.memset(c.values[:, :, :, HD + 1:32], 0.0))

        @block.tensor
        def _(pe):
            norm.tensor(pe)
            pe.wait_ge(c.early.sem, early)
            for which in range(2):
                for m in range(KT):
                    for k in range(KT):
                        last = nc.tensor.matmul(ps[:, 2 * which + m, :], w[:, which, k, m * P:(m + 1) * P],
                                                c.hT[:, k, :], start=k == 0, stop=k == KT - 1)
                    last.then_inc(projected, 1)
            for t in range(TT):
                for k in range(KT):
                    last = nc.tensor.matmul(ps[:, 4 + t, 0:D], c.hT[:, k, t * P:(t + 1) * P], w[:, 2, k, :],
                                            start=k == 0, stop=k == KT - 1)
                last.then_inc(projected, 1)

            def scores(t):
                b, bank = t // 2, 2 * (t % 2)
                if t < 2:
                    pe.wait_ge(c.ctxT_loaded, 16)
                    pe.wait_ge(act_kept, 2)
                    pe.wait_ge(dve_kept, 2)
                else:
                    pe.wait_ge(exped, t - 1)
                for k in range(KT):
                    nc.tensor.matmul(ps[:, bank, :], qT[:, k, t * P:(t + 1) * P],
                                     c.ctxT[:, k, b * CTX:(b + 1) * CTX], start=k == 0, stop=k == KT - 1)
                for k in range(KT):
                    last = nc.tensor.matmul(ps[:, bank + 1, 0:S], qT[:, k, t * P:(t + 1) * P],
                                            knT[:, k, b * S:(b + 1) * S], start=k == 0, stop=k == KT - 1)
                last.then_inc(scored, 1)

            def turn(t):
                bank = 4 + 2 * (t % 2)
                pe.wait_ge(exped, t + 1)
                if t < 2:
                    pe.wait_ge(act_kept, 4)
                    pe.wait_ge(dve_kept, 4)
                elif t == 2:
                    pe.wait_ge(mixed_act, 1)
                    pe.wait_ge(mixed_dve, 1)
                else:
                    pe.wait_ge(added, 2)
                for j in range(NK):
                    last = nc.tensor.transpose(ps[:, bank + j // 4, (j % 4) * P:(j % 4 + 1) * P],
                                               probs[:, t % 2, j * P:(j + 1) * P], c.ident[:])
                last.then_inc(turned, 1)

            def mix(b):
                pe.wait_ge(c.inputs_loaded, 80)
                pe.wait_ge(turn_act, 2 * b + 2)
                pe.wait_ge(turn_dve, 2 * b + 2)
                for m in range(KT):
                    for j in range(NK):
                        v = c.ctx[:, b * 4 + j, m * P:(m + 1) * P] if j < 4 else \
                            vn[:, b * 2 + j - 4, m * P:(m + 1) * P]
                        last = nc.tensor.matmul(ps[:, 4 + m, 0:S], v, probsT[:, j, :],
                                                start=j == 0, stop=j == NK - 1)
                    last.then_inc(mixed, 1)

            def project_out(t):
                pe.wait_ge(mixed_act, t // 2 + 1)
                pe.wait_ge(mixed_dve, t // 2 + 1)
                for k in range(KT):
                    last = nc.tensor.matmul(ps[:, 6 + t % 2, 0:D], oT[:, k, t * P:(t + 1) * P], w[:, 3, k, :],
                                            start=k == 0, stop=k == KT - 1)
                last.then_inc(out_ready, 1)

            scores(0)
            scores(1)
            turn(0)
            turn(1)
            scores(2)
            scores(3)
            mix(0)
            project_out(0)
            project_out(1)
            turn(2)
            turn(3)
            mix(1)
            project_out(2)
            project_out(3)

        @block.scalar
        def _(act):
            norm.scalar(act)
            act.wait_ge(c.rows_loaded, 16)
            nc.scalar.activation(c.gate[:], c.rows[:, 0:8], ACT.Tanh).then_inc(gates, 1)
            act.wait_ge(projected, 1)
            nc.scalar.copy(qT[:, 0, :], ps[:, 0, :]).then_inc(act_kept, 1)
            act.wait_ge(projected, 3)
            nc.scalar.copy(knT[:, 0, :], ps[:, 2, :]).then_inc(act_kept, 1)
            for t in (0, 2):
                act.wait_ge(projected, 5 + t)
                nc.scalar.copy(vn[:, t, :], ps[:, 4 + t, 0:D]).then_inc(act_kept, 1)

            def exponentials(t):
                bank = 2 * (t % 2)
                act.wait_ge(biased, t + 1)
                if t >= 2:
                    act.wait_ge(turned, t - 1)
                nc.scalar.activation(probs[:, t % 2, :], flat(ps[:, bank:bank + 2, :])[:, 0:KEYS], ACT.Exp,
                                     bias=bias[:, t:t + 1], scale=SCALE, accum_out=total[:, t:t + 1])\
                    .then_inc(exped, 1)

            def keep_turned(t):
                act.wait_ge(turned, t + 1)
                if t == 2:
                    act.wait_ge(mixed, 2)
                nc.scalar.copy(probsT[:, 0:4, (t % 2) * P:(t % 2 + 1) * P],
                               ps[:, 4 + 2 * (t % 2), :].rearrange("p (j n) -> p j n", j=4)).then_inc(turn_act, 1)

            def keep_mixed(b):
                act.wait_ge(mixed, 2 * b + 1)
                nc.scalar.copy(oT[:, 0, b * S:(b + 1) * S], ps[:, 4, 0:S]).then_inc(mixed_act, 1)

            exponentials(0)
            exponentials(1)
            keep_turned(0)
            keep_turned(1)
            exponentials(2)
            exponentials(3)
            keep_mixed(0)
            keep_turned(2)
            keep_turned(3)
            keep_mixed(1)
            act.wait_ge(c.inputs_loaded, 80)
            nc.scalar.copy(c.values[:, :, :, 0:HD], c.ctx[:].rearrange("p t (h e) -> p t h e", h=H))\
                .then_inc(gates, 1)
            act.wait_ge(gates, 2)

        @block.vector
        def _(dve):
            norm.vector(dve)
            dve.wait_ge(projected, 2)
            nc.vector.tensor_copy(qT[:, 1, :], ps[:, 1, :]).then_inc(dve_kept, 1)
            dve.wait_ge(projected, 4)
            nc.vector.tensor_copy(knT[:, 1, :], ps[:, 3, :]).then_inc(dve_kept, 1)
            for t in (1, 3):
                dve.wait_ge(projected, 5 + t)
                nc.vector.tensor_copy(vn[:, t, :], ps[:, 4 + t, 0:D]).then_inc(dve_kept, 1)

            def maximum(t):
                bank = 2 * (t % 2)
                dve.wait_ge(scored, t + 1)
                settle(dve, own, nc.vector.reduce_max(top[:, t:t + 1], flat(ps[:, bank:bank + 2, :])[:, 0:KEYS], AX.X))
                nc.vector.tensor_scalar(bias[:, t:t + 1], top[:, t:t + 1], -SCALE, None, ALU.mult)\
                    .then_inc(biased, 1)

            def keep_turned(t):
                dve.wait_ge(turned, t + 1)
                if t == 2:
                    dve.wait_ge(mixed, 2)
                nc.vector.tensor_copy(probsT[:, 4:6, (t % 2) * P:(t % 2 + 1) * P],
                                      ps[:, 5 + 2 * (t % 2), 0:2 * P].rearrange("p (j n) -> p j n", j=2))\
                    .then_inc(turn_dve, 1)

            def keep_mixed(b):
                dve.wait_ge(mixed, 2 * b + 2)
                nc.vector.tensor_copy(oT[:, 1, b * S:(b + 1) * S], ps[:, 5, 0:S]).then_inc(mixed_dve, 1)

            def add(t):
                dve.wait_ge(exped, t + 1)
                settle(dve, own, nc.vector.reciprocal(inv[:, t:t + 1], total[:, t:t + 1]))
                settle(dve, own, nc.vector.tensor_tensor(factor[:, t:t + 1], inv[:, t:t + 1], c.gate[:, 0:1], ALU.mult))
                dve.wait_ge(out_ready, t + 1)
                nc.vector.scalar_tensor_tensor(out=c.x[:, t, :], in0=ps[:, 6 + t % 2, 0:D], scalar=factor[:, t:t + 1],
                                               in1=c.x[:, t, :], op0=ALU.mult, op1=ALU.add).then_inc(added, 1)

            dve.wait_ge(gates, 1)
            maximum(0)
            maximum(1)
            keep_turned(0)
            keep_turned(1)
            maximum(2)
            maximum(3)
            keep_mixed(0)
            add(0)
            add(1)
            keep_turned(2)
            keep_turned(3)
            keep_mixed(1)
            add(2)
            add(3)
            dve.wait_ge(added, 4)


def repeat(eng, first, end, unroll, body):
    groups = (end - first) // unroll
    if groups > 1:
        with eng.Fori(0, groups) as it:
            for s in range(unroll):
                body(it * unroll + (first + s), (first + s) % unroll)
    else:
        groups = 0
    for j in range(first + groups * unroll, end):
        body(j, j % unroll)


def load_expert_tiles(nc, c, d, name):
    at = MOE_AT[name]

    def start(sp):
        for s in range(SLOTS):
            sp.dma_start(c.slots[:, s, :], d["moe_w"][at + s]).then_inc(c.slot_loaded[s], 16)
    return start


class Router:

    def __init__(self, nc, c, ctx, name):
        E = MOE[name][1]
        self.nc, self.c, self.name, self.E = nc, c, name, E
        self.at = {"l1": 0, "l2": 8, "l3": 24}[name]
        self.R = 3 * (E + 1)
        sem = stage_semaphores(nc, ctx, name + "r")

        def sb(n, shape, dt=F32):
            return ctx.enter_context(nc.sbuf_tensor(f"{name}r_{n}", shape, dt))
        self.centered, self.expd = sb("centered", [P, TT, E]), sb("exp", [P, TT, E])
        self.work = {n: sb(n, [P, TT, E]) for n in ("logits", "prob", "rank", "chosen", "group_masked")}
        self.work.update({n: sb(n, [P, TT]) for n in ("top", "total", "inv", "ms")})
        if name == "l1":
            self.work.update({n: sb(n, [P, TT, E, E]) for n in ("above", "equal")})
        else:
            spare = flat(c.l2_kT[:])[:, 0:2 * TT * E * E].rearrange("p (w t e f) -> p w t e f", w=2, t=TT, e=E)
            self.work.update(above=spare[:, 0], equal=spare[:, 1])
        self.work.update({n: sb(n, [P, TT, E + 1]) for n in ("weight", "rest")})
        self.group_top, self.square = sb("group_top", [P, TT, 4]), sb("square", [P, D])
        self.parts = sb("parts", [P, TT, 3, E + 1], BF16)
        self.rw, self.rms = sb("rw", [P, KT, E]), sb("rms", [P, TT])
        self.scaled, self.scored, self.centred_ready, self.exped = (
            sem(n) for n in ("scaled", "scored", "centred", "exped"))
        self.split, self.turned, self.kept = sem("split"), sem("turned"), sem("kept")
        self.ms_ready, self.rms_ready = sem("ms_ready"), sem("rms_ready")
        self.own = Tally(sem("own"))
        self.scores = c.ps[:, 6, 0:TT * E].rearrange("p (t e) -> p t e", t=TT)
        self.turned_bf = c.ps[:, 7, :].bitcast(BF16)

    def score(self, pe):
        c, E = self.c, self.E
        if self.name == "l3":
            pe.wait_ge(self.scaled, KT)
        for t in range(TT):
            for k in range(KT):
                w = self.rw[:, k, :] if self.name == "l3" else c.routers[:, k, self.at:self.at + E]
                last = self.nc.tensor.matmul(self.scores[:, t, :], c.hT[:, k, t * P:(t + 1) * P], w,
                                             start=k == 0, stop=k == KT - 1)
        last.then_inc(self.scored, 1)

    def turn(self, pe):
        pe.wait_ge(self.split, 1)
        for t in range(TT):
            last = self.nc.tensor.transpose(self.turned_bf[0:self.R, t * P:(t + 1) * P],
                                            self.parts[:, t].rearrange("p a e -> p (a e)"), self.c.ident_bf[:])
        last.then_inc(self.turned, 1)
        pe.wait_ge(self.kept, 1)

    def exponentials(self, act):
        act.wait_ge(self.centred_ready, 1)
        self.nc.scalar.activation(self.expd[:], self.centered[:], ACT.Exp).then_inc(self.exped, 1)

    def keep(self, act):
        act.wait_ge(self.turned, 1)
        self.nc.scalar.copy(self.c.weightT[0:self.R, :], self.turned_bf[0:self.R, 0:T]).then_inc(self.kept, 1)

    def gpsimd(self, pool):
        if self.name == "l3":
            pool.wait_ge(self.ms_ready, 1)
            self.nc.gpsimd.tensor_tensor(self.rms[:], self.work["ms"][:], self.c.minus_half[:, 0:TT], ALU.pow)\
                .then_inc(self.rms_ready, 1)

    def vector(self, dve):
        nc, c, E, name, own, at = self.nc, self.c, self.E, self.name, self.own, self.at
        logits, prob, rank, chosen, group_masked = (
            self.work[n] for n in ("logits", "prob", "rank", "chosen", "group_masked"))
        top, total, inv, ms = (self.work[n] for n in ("top", "total", "inv", "ms"))
        above, equal, weight, rest = (self.work[n] for n in ("above", "equal", "weight", "rest"))
        centered, expd, group_top, square = self.centered, self.expd, self.group_top, self.square
        parts, rw, rms = self.parts, self.rw, self.rms
        scaled, scored, centred_ready, exped = self.scaled, self.scored, self.centred_ready, self.exped
        split, ms_ready, rms_ready = self.split, self.ms_ready, self.rms_ready
        V = nc.vector

        def ranked(score, n, keep):
            shape = [P, TT, n, n]
            other, self_ = score.unsqueeze(2).broadcast_to(shape), score.unsqueeze(3).broadcast_to(shape)
            a, q = above[:, :, 0:n, 0:n], equal[:, :, 0:n, 0:n]
            own.up(V.tensor_tensor(a, other, self_, ALU.is_gt))
            settle(dve, own, V.tensor_tensor(q, other, self_, ALU.is_equal))
            before = c.before[:, 0:n, 0:n].unsqueeze(1).broadcast_to(shape)
            settle(dve, own, V.tensor_tensor(q, q, before, ALU.mult))
            settle(dve, own, V.tensor_tensor(a, a, q, ALU.add))
            settle(dve, own, V.tensor_reduce(rank[:, :, 0:n], a, AX.X, ALU.add))
            settle(dve, own, V.tensor_scalar(chosen[:, :, 0:n], rank[:, :, 0:n], float(keep), None, ALU.is_lt))

        if name == "l3":
            for k in range(KT):
                col = COL["router_scale"] + k
                V.tensor_scalar(rw[:, k, :], c.routers[:, k, at:at + E], c.cols[:, col:col + 1], None, ALU.mult)\
                    .then_inc(scaled, 1)
            for t in range(TT):
                settle(dve, own, V.tensor_tensor_reduce(
                    out=square[:], in0=c.h[:, t, :], in1=c.h[:, t, :], scale=1.0, scalar=0.0,
                    op0=ALU.mult, op1=ALU.add, accum_out=ms[:, t:t + 1]))
            V.tensor_scalar(ms[:], ms[:], 1.0 / D, RMS_EPS, ALU.mult, ALU.add).then_inc(ms_ready, 1)
        dve.wait_ge(scored, 1)
        if name == "l3":
            dve.wait_ge(rms_ready, 1)
            for t in range(TT):
                last = own.up(V.tensor_scalar(logits[:, t, :], self.scores[:, t, :], rms[:, t:t + 1], D ** -0.5,
                                              ALU.mult, ALU.mult))
            dve.wait_ge(own.sem, last)
        else:
            settle(dve, own, V.tensor_copy(logits[:], self.scores))
        settle(dve, own, V.tensor_reduce(top[:], logits[:], AX.X, ALU.max))
        V.tensor_tensor(centered[:], logits[:], top[:].unsqueeze(2).broadcast_to([P, TT, E]), ALU.subtract)\
            .then_inc(centred_ready, 1)
        dve.wait_ge(exped, 1)
        settle(dve, own, V.tensor_reduce(total[:], expd[:], AX.X, ALU.add))
        settle(dve, own, V.reciprocal(inv[:], total[:]))
        settle(dve, own, V.tensor_tensor(prob[:], expd[:], inv[:].unsqueeze(2).broadcast_to([P, TT, E]), ALU.mult))
        if name == "l1":
            pairs = prob[:].rearrange("p t (g e) -> p t g e", g=4)
            settle(dve, own, V.tensor_reduce(group_top[:], pairs, AX.X, ALU.max))
            ranked(group_top[:], 4, 2)
            settle(dve, own, V.tensor_tensor(
                group_masked[:].rearrange("p t (g e) -> p t g e", g=4), pairs,
                chosen[:, :, 0:4].unsqueeze(3).broadcast_to([P, TT, 4, 2]), ALU.mult))
            ranked(group_masked[:], E, 2)
            settle(dve, own, V.tensor_tensor(weight[:, :, 0:E], group_masked[:], chosen[:], ALU.mult))
        else:
            ranked(prob[:], E, 6 if name == "l2" else 2)
            settle(dve, own, V.tensor_tensor(prob[:], prob[:], chosen[:], ALU.mult))
            settle(dve, own, V.tensor_reduce(total[:], prob[:], AX.X, ALU.add))
            if name == "l3":
                settle(dve, own, V.tensor_scalar(total[:], total[:], 1e-12, None, ALU.max))
            settle(dve, own, V.reciprocal(inv[:], total[:]))
            settle(dve, own, V.tensor_tensor(weight[:, :, 0:E], prob[:],
                                             inv[:].unsqueeze(2).broadcast_to([P, TT, E]), ALU.mult))
            if name == "l3":
                es = c.rows[:, ROW["expert_scale"]:ROW["expert_scale"] + E]
                settle(dve, own, V.tensor_tensor(weight[:, :, 0:E], weight[:, :, 0:E],
                                                 es.unsqueeze(1).broadcast_to([P, TT, E]), ALU.mult))
        settle(dve, own, V.memset(weight[:, :, E:E + 1], 1.0))
        settle(dve, own, V.tensor_copy(parts[:, :, 0, :], weight[:]))
        settle(dve, own, V.tensor_tensor(rest[:], weight[:], parts[:, :, 0, :], ALU.subtract))
        settle(dve, own, V.tensor_copy(parts[:, :, 1, :], rest[:]))
        V.tensor_tensor(parts[:, :, 2, :], rest[:], parts[:, :, 1, :], ALU.subtract).then_inc(split, 1)


def ffn_stage(nc, c, d, name, norm, residual=None, also=None, context=None):
    fp4 = name == "l0"
    J = 16 if fp4 else MOE[name][0]
    func = {"l0": ACT.Gelu_apprx_tanh, "l1": ACT.Silu, "l2": ACT.Silu, "l3": ACT.Gelu}[name]
    gate = {"l0": 4, "l1": 5, "l2": 6, "l3": 7}[name]
    unit = 2.0 ** 14 if fp4 else 1.0
    ps = c.ps
    with ExitStack() as ctx:
        def sb(n, shape, dt=F32):
            return ctx.enter_context(nc.sbuf_tensor(f"{name}f_{n}", shape, dt))

        sem = stage_semaphores(nc, ctx, name + "f")
        h_top, h_rest = c.h_top, c.h_rest
        w_top, w_rest = sb("w_top", [P, SLOTS, FW], F32R), sb("w_rest", [P, SLOTS, FW], F32R)
        acted_buf, hidden = sb("acted", [P, 2, T]), sb("hidden", [P, 2, T])
        hid_top, hid_rest = sb("hid_top", [P, 2, T], F32R), sb("hid_rest", [P, 2, T], F32R)
        factor = sb("factor", [P, 1])
        top_ready, rest_ready = sem("top_ready"), sem("rest_ready")
        gated, upped, acted, hidden_ready = sem("gated"), sem("upped"), sem("acted"), sem("hidden_ready")
        downed, added, multiplied = sem("downed"), sem("added"), sem("multiplied")
        own = Tally(sem("own"))
        slots = c.slots
        if fp4:
            words = [flat(c.z[:])[:, 0:FW].bitcast(I32), sb("words", [P, FW], I32)[:]]
            scales = [flat(c.z2[:])[:, 0:FW], sb("scales", [P, FW])[:]]
            spread, sign = sb("spread", [P, FW], I32), sb("sign", [P, FW], I32)
            codes = sb("codes", [P, 2, FW], I32)
            packed_loaded, words_read = [c.fp4_loaded, sem("packed1")], sem("words_read")
            coded, dequantized = sem("coded"), sem("dequantized")
        else:
            loaded, base = c.slot_loaded, list(c.slot_loads)
            for j in range(J):
                c.slot_loads[j % SLOTS] += 1
            start_loads = load_expert_tiles(nc, c, d, name)
            selected = sb("sel", [P, J * P], BF16)
            sel_loaded = sem("sel_loaded")

        def later(j, first):
            return not isinstance(j, int) or j >= first
        norm = norm(ctx)
        router = None if fp4 else Router(nc, c, ctx, name)
        routed = None if fp4 else sem("routed")
        context = context(sem) if context is not None else None
        block = ctx.enter_context(nc.Block(no_gpsimd_drain=True))

        @block.sync
        def _(sp):
            if fp4:
                for i in range(1, 8):
                    if i >= 2:
                        sp.wait_ge(words_read, i - 1)
                        sp.wait_ge(dequantized, i - 1)
                    sp.dma_start(words[i % 2], d["fp4_w"][i]).then_inc(packed_loaded[i % 2], 16)
                    sp.dma_start(scales[i % 2], d["fp4_s"][i].unsqueeze(1).broadcast_to([8, 16, FW]))\
                        .then_inc(packed_loaded[i % 2], 16)
                return
            start_loads(sp)
            sp.dma_start(selected[:].bitcast(U16), d["sel"][:, MOE_AT[name] * P:(MOE_AT[name] + J) * P])\
                .then_inc(sel_loaded, 16)
            if also is not None:
                also(sp)

            def load(j, slot):
                sp.wait_ge(rest_ready, j - SLOTS + 1)
                src = d["moe_w"][bass.ds(j + MOE_AT[name], 1)].rearrange("a p n -> p (a n)")
                sp.dma_start(slots[:, slot, :], src).then_inc(loaded[slot], 16)
            repeat(sp, SLOTS, J, SLOTS, load)

        @block.tensor
        def _(pe):
            if context is not None:
                context.keys(pe)
            norm.tensor(pe, wait=context is None)
            if context is not None:
                context.values(pe)
                norm.ready(pe)
            if not fp4:
                router.score(pe)
            for bank in (4, 5):
                nc.tensor.matmul(ps[:, bank, :], c.zero_bf[:, 0:P], c.zero_bf[:], start=True, stop=True,
                                 skip_group_check=True)

            def routing(j, slot):
                if later(j, 2):
                    pe.wait_ge(hidden_ready, j - 1)
                nc.tensor.matmul(ps[:, 6 + slot % 2, :], selected[:, bass.ds(j * P, P)], c.weightT[:],
                                 start=True, stop=True).then_inc(routed, 1)

            def gate_up(j, slot):
                parity = slot % 2
                if later(j, 2):
                    pe.wait_ge(acted, j - 1)
                    pe.wait_ge(hidden_ready, j - 1)
                pe.wait_ge(rest_ready, j + 1)
                for part, done in ((0, gated), (1, upped)):
                    for k in range(KT):
                        at = k * 2 * P + part * P
                        for a, b in ((w_top, h_top), (w_top, h_rest), (w_rest, h_top)):
                            last = nc.tensor.matmul(ps[:, 2 * parity + part, :], a[:, slot, at:at + P], b[:, k, :],
                                                    start=k == 0 and b is h_top and a is w_top,
                                                    stop=k == KT - 1 and a is w_rest)
                    last.then_inc(done, 1)

            def down(j, slot):
                pe.wait_ge(hidden_ready, j + 1)
                for t in range(TT):
                    for a, b in ((hid_top, w_top), (hid_top, w_rest), (hid_rest, w_top)):
                        last = nc.tensor.matmul(ps[:, 4 + t // 2, (t % 2) * D:(t % 2 + 1) * D],
                                                a[:, slot % 2, t * P:(t + 1) * P], b[:, slot, 4 * P:4 * P + D],
                                                start=False, stop=True, skip_group_check=True)
                last.then_inc(downed, 1)

            def step(j, phase):
                if not fp4:
                    routing(j + 1, (phase + 1) % SLOTS)
                gate_up(j + 1, (phase + 1) % SLOTS)
                down(j, phase)
            gate_up(0, 0)
            if context is not None:
                pe.wait_ge(context.kept, 8)
            gate_up(1, 1)
            if not fp4:
                router.turn(pe)
                pe.wait_ge(sel_loaded, 16)
                routing(0, 0)
                routing(1, 1)
            down(0, 0)
            repeat(pe, 1, J - 1, SLOTS, step)
            down(J - 1, (J - 1) % SLOTS)

        @block.scalar
        def _(act):
            def cut(j, slot):
                if fp4:
                    act.wait_ge(dequantized, j // 2 + 1)
                else:
                    act.wait_ge(loaded[slot], (base[slot] + 1) * 16 + (j - slot) * (16 // SLOTS))
                if later(j, SLOTS):
                    act.wait_ge(downed, j - SLOTS + 1)
                nc.scalar.copy(w_top[:, slot, :], slots[:, slot, :]).then_inc(top_ready, 1)

            def activate(j, phase):
                act.wait_ge(gated, j + 1)
                if later(j, 2):
                    act.wait_ge(hidden_ready, j - 1)
                nc.scalar.activation(acted_buf[:, phase % 2, :], ps[:, 2 * (phase % 2), :], func, scale=unit)\
                    .then_inc(acted, 1)

            def step(j, phase):
                activate(j, phase)
                cut(j + 3, (phase + 3) % SLOTS)
            if context is not None:
                context.keep_keys(act)
            if fp4:
                norm.scalar(act)
            if context is not None:
                context.keep_values(act, 0, 1)
            for j in range(2):
                cut(j, j)
            if context is not None:
                context.keep_values(act, 1, 4)
            if not fp4:
                norm.scalar(act)
                router.exponentials(act)
            activate(0, 0)
            for j in (2, 3):
                cut(j, j)
            activate(1, 1)
            if not fp4:
                router.keep(act)
            cut(4, 0)
            repeat(act, 2, J - 3, SLOTS, step)
            for j in range(J - 3, J):
                activate(j, j % SLOTS)

        @block.gpsimd
        def _(pool):
            def cut(j, slot):
                pool.wait_ge(top_ready, j + 1)
                nc.gpsimd.tensor_tensor(w_rest[:, slot, :], slots[:, slot, :], w_top[:, slot, :], ALU.subtract)\
                    .then_inc(rest_ready, 1)

            def dequantize(i):
                pool.wait_ge(coded, i + 1)
                if i >= 2:
                    pool.wait_ge(rest_ready, 2 * i - 2)
                half = codes[:, i % 2, :].bitcast(F16).rearrange("p (n h) -> p h n", h=2)
                pair = slots[:, 2 * (i % 2):2 * (i % 2) + 2, :]
                sc = scales[i % 2]
                for h in range(2):
                    nc.gpsimd.tensor_tensor(
                        pair[:, :, 256 * h:256 * h + 256],
                        half[:, h, 0:512].rearrange("p (s n) -> p s n", s=2),
                        sc[:, 0:512].rearrange("p (s n) -> p s n", s=2), ALU.mult)
                    last = nc.gpsimd.tensor_tensor(pair[:, h, 512:768], half[:, h, 512:768], sc[:, 512:768],
                                                   ALU.mult)
                last.then_inc(dequantized, 1)
            if fp4:
                norm.gpsimd(pool, root_only=True)
                for i in range(8):
                    dequantize(i)
                    if i == 0:
                        norm.gpsimd_cut(pool)
                    for j in (2 * i, 2 * i + 1):
                        cut(j, j % SLOTS)
            else:
                norm.gpsimd(pool)
                router.gpsimd(pool)
                for j in range(2):
                    cut(j, j)
                repeat(pool, 2, J, SLOTS, cut)

        @block.vector
        def _(dve):
            V = nc.vector

            def decode(i):
                dve.wait_ge(packed_loaded[i % 2], 32 * (i // 2 + 1))
                w = words[i % 2]
                V.tensor_scalar(spread[:], w, 255, None, ALU.bitwise_and).then_inc(words_read, 1)
                dve.wait_ge(words_read, i + 1)
                settle(dve, own, V.scalar_tensor_tensor(out=spread[:], in0=spread[:], scalar=12, in1=spread[:],
                                                        op0=ALU.logical_shift_left, op1=ALU.bitwise_or))
                if i >= 2:
                    dve.wait_ge(dequantized, i - 1)
                own.up(V.tensor_scalar(codes[:, i % 2, :], spread[:], 9, 0x0E000E00, ALU.logical_shift_left,
                                       ALU.bitwise_and))
                last = own.up(V.tensor_scalar(sign[:], spread[:], 12, 0x80008000 - (1 << 32),
                                              ALU.logical_shift_left, ALU.bitwise_and))
                dve.wait_ge(own.sem, last)
                V.tensor_tensor(codes[:, i % 2, :], codes[:, i % 2, :], sign[:], ALU.bitwise_or).then_inc(coded, 1)

            def combine(j, phase):
                p = phase % 2
                dve.wait_ge(acted, j + 1)
                dve.wait_ge(upped, j + 1)
                if later(j, 2):
                    dve.wait_ge(downed, j - 1)
                product = hidden if fp4 else acted_buf
                V.tensor_tensor(product[:, p, :], acted_buf[:, p, :], ps[:, 2 * p + 1, :], ALU.mult)\
                    .then_inc(multiplied, 1)
                dve.wait_ge(multiplied, j * 3 + 1)
                if not fp4:
                    dve.wait_ge(routed, j + 1)
                    V.tensor_tensor(hidden[:, p, :], acted_buf[:, p, :], ps[:, 6 + p, :], ALU.mult)\
                        .then_inc(multiplied, 1)
                    dve.wait_ge(multiplied, j * 3 + 2)
                V.tensor_copy(hid_top[:, p, :], hidden[:, p, :]).then_inc(multiplied, 2 if fp4 else 1)
                dve.wait_ge(multiplied, j * 3 + 3)
                V.tensor_tensor(hid_rest[:, p, :], hidden[:, p, :], hid_top[:, p, :], ALU.subtract)\
                    .then_inc(hidden_ready, 1)

            settle(dve, own, V.tensor_scalar(factor[:], c.gate[:, gate:gate + 1], unit * unit, None, ALU.mult))
            if fp4:
                decode(0)
                norm.vector(dve)
                decode(1)
                combine(0, 0)
                decode(2)
                for j in range(1, J):
                    combine(j, j % 2)
                    if j % 2 and j // 2 + 3 < 8:
                        decode(j // 2 + 3)
            else:
                norm.vector(dve)
                norm.ready(dve)
                router.vector(dve)
                for j in range(2):
                    combine(j, j)
                repeat(dve, 2, J, 2, combine)
            if residual is not None:
                settle(dve, own, V.scalar_tensor_tensor(out=flat(c.x[:]), in0=flat(residual[:]), scalar=factor[:],
                                                        in1=flat(c.x[:]), op0=ALU.mult, op1=ALU.add))
            dve.wait_ge(downed, J)
            for t in range(TT):
                V.scalar_tensor_tensor(out=c.x[:, t, :], in0=ps[:, 4 + t // 2, (t % 2) * D:(t % 2 + 1) * D],
                                       scalar=factor[:], in1=c.x[:, t, :], op0=ALU.mult, op1=ALU.add)\
                    .then_inc(added, 1)
            dve.wait_ge(added, TT)


Q_PARTS = (0, 0, 1, 1, 0, 2)
K_PARTS = (0, 1, 0, 1, 2, 0)
STACK = 6 * HD
STACK_M = STACK + 3


def split_parts(dve, V, own, src, parts, rest):
    settle(dve, own, V.tensor_copy(parts[0], src))
    settle(dve, own, V.tensor_tensor(rest, src, parts[0], ALU.subtract))
    settle(dve, own, V.tensor_copy(parts[1], rest))
    return V.tensor_tensor(parts[2], rest, parts[1], ALU.subtract)


class KeySplit:

    def __init__(self, nc, ctx, sem, name, kT, k_tiles, k_rows):
        self.kT, self.k_tiles, self.k_rows = kT, k_tiles, k_rows
        self.parts = ctx.enter_context(nc.sbuf_tensor(f"{name}_k_parts", [k_rows, 3, k_tiles, B * CTX], BF16))
        self.rest = ctx.enter_context(nc.sbuf_tensor(f"{name}_k_rest", [k_rows, k_tiles, B * CTX], F32))
        self.own, self.ones = Tally(sem("k_own")), Tally(sem("ones"))
        self.split, self.bounced = sem("k_split"), sem("k_bounced")
        self.bounce = nc.dram_tensor(f"{name}_k_bounce", [3 * k_tiles, k_rows, B * CTX], BF16, kind="Internal").ap()


def split_keys(eng, V, keys):
    split_parts(eng, V, keys.own, keys.kT[:], [keys.parts[:, i] for i in range(3)], keys.rest[:])\
        .then_inc(keys.split, 1)


def bounce_keys(sp, keys):
    sp.wait_ge(keys.split, 1)
    sp.dma_start(keys.bounce.rearrange("c p n -> p c n"), keys.parts[:].rearrange("p c k n -> p (c k) n"))\
        .then_inc(keys.bounced, 16)
    sp.wait_ge(keys.bounced, 16)


def stack_keys(sp, c, keys):
    per = H // KT if keys.k_tiles == KT else keys.k_rows // HD
    by_head = keys.bounce.rearrange("(c k) (h d) n -> c d k h n", c=3, d=HD)
    for row, part in enumerate(K_PARTS):
        for a in range(keys.k_tiles):
            sp.dma_start(c.k_stack[row * HD:(row + 1) * HD, a * per:(a + 1) * per, :], by_head[part, :, a])\
                .then_inc(c.stacked.sem, 16)
            c.stacked.n += 16


def small_head_attention(nc, c, name, qT, values, kv_heads, causal, finish, norm=None, beside=None):
    G = 4
    KTILES = CTX // P
    ps = c.ps
    with ExitStack() as ctx:
        def sb(n, shape, dt=F32):
            return ctx.enter_context(nc.sbuf_tensor(f"{name}_{n}", shape, dt))

        sem = stage_semaphores(nc, ctx, name)
        stacked, k_stack = c.stacked.n, c.k_stack
        q_parts = sb("q_parts", [P, 3, KT, T], BF16)
        rest = flat(c.z[:]).rearrange("p (k n) -> p k n", k=KT)
        q_stack = sb("q_stack", [P, H, T], BF16)
        top = sb("top", [P, TT, H])
        m_rest, m_parts = sb("m_rest", [P, TT, H]), sb("m_parts", [P, TT, 3, H], BF16)
        m_turned = sb("m_turned", [3 * H, T], BF16)
        probsT = sb("probsT", [P, 3, 4 * S])
        outT, inv = sb("outT", [P, G, T]), sb("inv", [P, TT, H])
        q_split, head_stacked, q_kept = sem("q_split"), sem("head_stacked"), sem("q_kept")
        scored, maxed = sem("scored"), sem("maxed")
        m_split, m_transposed, m_kept = sem("m_split"), sem("m_transposed"), sem("m_kept")
        m_stacked = [sem("m_stacked0"), sem("m_stacked1")]
        scoredT, exped, mixed = sem("scoredT"), sem("exped"), sem("mixed")
        kept, turned = sem("kept"), sem("turned")
        own = Tally(sem("own"))
        m_bf = ps[:, 6, :].bitcast(BF16)
        PAIRS, FIRST = H, 8
        STEPS = PAIRS + 2 * H
        EACH = 3
        LAST = (2 * H - FIRST) // EACH
        between = {n: range(PAIRS + FIRST + EACH * n, PAIRS + FIRST + EACH * (n + 1)) for n in range(LAST)}

        def plain_step(n):
            if n < PAIRS:
                return 0, n % 2, 2 * (n // 2), 2, 2 * (n % 2)
            return 1, (n - PAIRS) // H, (n - PAIRS) % H, 1, 6 + n % 2
        units = [(b, g, kt) for b in range(B) for g in range(G) for kt in range(KTILES)]
        norm = norm(ctx) if norm is not None else None
        beside = beside(ctx) if beside is not None else None
        block = ctx.enter_context(nc.Block(no_gpsimd_drain=True))

        if norm is not None:
            @block.gpsimd
            def _(pool):
                norm.gpsimd(pool)
                if beside is not None:
                    beside.gpsimd(pool)

        def span(kt):
            return (P, P) if causal and kt == KTILES - 1 else (0, S)

        @block.sync
        def _(sp):
            if beside is not None:
                beside.load(sp)
            for b in range(B):
                sp.wait_ge(m_kept, b + 1)
                for part in range(3):
                    sp.dma_start(q_stack[STACK + part:STACK + part + 1, :, b * S:(b + 1) * S],
                                 m_turned[part * H:(part + 1) * H, b * S:(b + 1) * S]).then_inc(m_stacked[b], 16)
            if beside is not None:
                beside.bounce(sp)

        @block.tensor
        def _(pe):
            if norm is not None:
                norm.tensor(pe)
            if beside is not None:
                beside.tensor(pe)
            pe.wait_ge(c.stacked.sem, stacked)

            def stack(h):
                pe.wait_ge(q_split, h // 8 + 1)
                if h >= 2:
                    pe.wait_ge(q_kept, h - 1)
                for part in range(3):
                    last = nc.tensor.matmul(ps[0:STACK, 4 + h % 2, :], c.stack_sel[:, h % 8, part, :],
                                            q_parts[:, part, h // 8, :], start=part == 0, stop=part == 2)
                last.then_inc(head_stacked, 1)

            def plain_scores(n):
                b, half, h0, heads, bank = plain_step(n)
                if n < PAIRS:
                    pe.wait_ge(q_kept, h0 + heads)
                if n >= PAIRS:
                    pe.wait_ge(m_kept, 1)
                if n >= 2 and n - PAIRS not in (0, 1):
                    pe.wait_ge(maxed, n - 1)
                width = 3 * P if causal and half == 0 else CTX
                q0 = b * S + half * P
                for i in range(heads):
                    h = h0 + i
                    last = nc.tensor.matmul(ps[:, bank + i, 0:width], q_stack[0:STACK, h, q0:q0 + P],
                                            k_stack[0:STACK, h * kv_heads // H, b * CTX:b * CTX + width],
                                            start=True, stop=not causal)
                    if causal:
                        last = nc.tensor.matmul(ps[:, bank + i, width - P:width], c.ident_bf[:], c.mask_q[:],
                                                start=False, stop=True)
                last.then_inc(scored, 1)

            def turn_maxima(b):
                pe.wait_ge(m_split, b + 1)
                pe.wait_ge(maxed, (PAIRS, STEPS)[b])
                for t in (2 * b, 2 * b + 1):
                    last = nc.tensor.transpose(m_bf[0:3 * H, (t % 2) * P:(t % 2 + 1) * P],
                                               m_parts[:, t].rearrange("p a h -> p (a h)"), c.ident_bf[:])
                last.then_inc(m_transposed, 1)

            def turned_scores(n):
                b, g, kt = units[n]
                if n < 2:
                    pe.wait_ge(maxed, PAIRS)
                else:
                    pe.wait_ge(exped, n - 1)
                if n % 16 == 0:
                    pe.wait_ge(m_stacked[b], 48)
                q0, nq = span(kt)
                for r in range(4):
                    h = 4 * g + r
                    bank, at = 2 * (n % 2) + r // 2, (r % 2) * S
                    diagonal = causal and kt >= 2
                    last = nc.tensor.matmul(ps[:, bank, at:at + nq],
                                            k_stack[0:STACK_M, h * kv_heads // H,
                                                    b * CTX + kt * P:b * CTX + (kt + 1) * P],
                                            q_stack[0:STACK_M, h, b * S + q0:b * S + q0 + nq],
                                            start=True, stop=not diagonal)
                    if diagonal:
                        last = nc.tensor.matmul(ps[:, bank, at:at + P], c.ident_bf[:], c.mask_k[:],
                                                start=False, stop=True)
                last.then_inc(scoredT, 1)

            def mix(n):
                b, g, kt = units[n]
                pe.wait_ge(exped, n + 1)
                if kt == 0 and n >= 2 * KTILES:
                    pe.wait_ge(kept, n // KTILES - 1)
                q0, nq = span(kt)
                for r in range(4):
                    h = 4 * g + r
                    last = nc.tensor.matmul(ps[32 * r:32 * r + 32, 4 + g % 2, q0:q0 + nq],
                                            values[:, b * KTILES + kt, h * kv_heads // H, :],
                                            probsT[:, n % 3, r * S:r * S + nq],
                                            start=kt == 0, stop=kt == KTILES - 1)
                last.then_inc(mixed, 1)

            for h in range(3):
                stack(h)
            for n in range(PAIRS):
                plain_scores(n)
                if n + 3 < H:
                    stack(n + 3)
            pe.wait_ge(q_kept, H)
            turn_maxima(0)
            for n in range(PAIRS, PAIRS + FIRST):
                plain_scores(n)
            turned_scores(0)
            for n in range(len(units)):
                plain = between.get(n, ())
                if n + 1 < len(units):
                    turned_scores(n + 1)
                for p in plain[0:1]:
                    plain_scores(p)
                mix(n)
                for p in plain[1:]:
                    plain_scores(p)
                if n == LAST:
                    turn_maxima(1)
            for t in range(TT):
                pe.wait_ge(kept, len(units) // KTILES)
                for g in range(G):
                    last = nc.tensor.transpose(ps[:, t, g * P:(g + 1) * P], outT[:, g, t * P:(t + 1) * P], c.ident[:])
                last.then_inc(turned, 1)

        @block.scalar
        def _(act):
            if norm is not None:
                norm.scalar(act)
            if beside is not None:
                beside.scalar(act)
            for h in range(H):
                act.wait_ge(head_stacked, h + 1)
                nc.scalar.copy(q_stack[0:STACK, h, :], ps[0:STACK, 4 + h % 2, :]).then_inc(q_kept, 1)

            def keep_maxima(b):
                act.wait_ge(m_transposed, b + 1)
                nc.scalar.copy(m_turned[:, b * S:(b + 1) * S], m_bf[0:3 * H, 0:S]).then_inc(m_kept, 1)
            keep_maxima(0)
            for n, (b, g, kt) in enumerate(units):
                _, nq = span(kt)
                if n == LAST + 3:
                    keep_maxima(1)
                act.wait_ge(scoredT, n + 1)
                if n >= 3:
                    act.wait_ge(mixed, n - 2)
                scores = flat(ps[:, 2 * (n % 2):2 * (n % 2) + 2, :]).rearrange("p (r q) -> p r q", r=4)[:, :, 0:nq]
                probs = probsT[:, n % 3, :].rearrange("p (r q) -> p r q", r=4)[:, :, 0:nq]
                nc.scalar.activation(probs, scores, ACT.Exp, scale=HD ** -0.5).then_inc(exped, 1)

        @block.vector
        def _(dve):
            V = nc.vector
            if norm is not None:
                norm.vector(dve)
                norm.ready(dve)
            if beside is not None:
                beside.means(dve)
            for k in range(KT):
                split_parts(dve, V, own, qT[:, k, :], [q_parts[:, i, k, :] for i in range(3)], rest[:, k, :])\
                    .then_inc(q_split, 1)
            if beside is not None:
                beside.vector(dve)
            def maxima(n):
                b, half, h0, heads, bank = plain_step(n)
                width = 3 * P if causal and half == 0 else CTX
                dve.wait_ge(scored, n + 1)
                V.tensor_reduce(top[:, 2 * b + half, h0:h0 + heads], ps[:, bank:bank + heads, 0:width], AX.X, ALU.max)\
                    .then_inc(maxed, 1)

            def split_maxima(b):
                dve.wait_ge(maxed, (PAIRS, STEPS)[b])
                ts = slice(2 * b, 2 * b + 2)
                settle(dve, own, V.tensor_scalar(m_parts[:, ts, 0, :], top[:, ts, :], -1.0, None, ALU.mult))
                settle(dve, own, V.scalar_tensor_tensor(out=m_rest[:, ts, :], in0=top[:, ts, :], scalar=-1.0,
                                                        in1=m_parts[:, ts, 0, :], op0=ALU.mult, op1=ALU.subtract))
                settle(dve, own, V.tensor_copy(m_parts[:, ts, 1, :], m_rest[:, ts, :]))
                V.tensor_tensor(m_parts[:, ts, 2, :], m_rest[:, ts, :], m_parts[:, ts, 1, :], ALU.subtract)\
                    .then_inc(m_split, 1)

            for n in range(PAIRS):
                maxima(n)
            split_maxima(0)
            for n in range(PAIRS, PAIRS + FIRST):
                maxima(n)
            for n, (b, g, kt) in enumerate(units):
                for p in between.get(n, ()):
                    maxima(p)
                if n == LAST - 1:
                    split_maxima(1)
                if kt == KTILES - 1:
                    dve.wait_ge(mixed, n + 1)
                    V.tensor_copy(outT[:, g, b * S:(b + 1) * S], ps[:, 4 + g % 2, 0:S]).then_inc(kept, 1)
            for t in range(TT):
                dve.wait_ge(turned, t + 1)
                heads = ps[:, t, :].rearrange("p (h e) -> p h e", h=H)
                settle(dve, own, V.reciprocal(inv[:, t, :], heads[:, :, HD]))
                finish(dve, own, t, heads[:, :, 0:HD], inv[:, t, :].unsqueeze(2).broadcast_to([P, H, HD]))


def l1_attention(nc, c, d, norm, beside):
    with ExitStack() as ctx:
        normed = c.z2
        added = stage_semaphores(nc, ctx, "l1xv")("added")

        def finish(dve, own, t, heads, inv):
            out = normed[:, t, :].rearrange("p (h e) -> p h e", h=H)
            settle(dve, own, nc.vector.tensor_tensor(out, heads, inv, ALU.mult))
            nc.vector.scalar_tensor_tensor(out=c.x[:, t, :], in0=normed[:, t, :], scalar=c.gate[:, 1:2],
                                           in1=c.x[:, t, :], op0=ALU.mult, op1=ALU.add).then_inc(added, 1)
            if t == TT - 1:
                dve.wait_ge(added, TT)
        small_head_attention(nc, c, "l1x", c.hT, c.values, H, True, finish, norm, beside)


class L2Context:

    def __init__(self, nc, c, sem):
        self.nc, self.c = nc, c
        self.k_done, self.v_done, self.kept = sem("k_done"), sem("v_done"), sem("kv_kept")

    def keys(self, pe):
        c = self.c
        pe.wait_ge(c.kv_w_loaded, 48)
        for m in range(KT):
            for half in range(2):
                for k in range(KT):
                    last = self.nc.tensor.matmul(c.ps[:, 2 + 2 * m + half, :], c.kv_w[:, 0, k, m * P:(m + 1) * P],
                                                 c.ctxT[:, k, half * CTX:(half + 1) * CTX],
                                                 start=k == 0, stop=k == KT - 1)
                last.then_inc(self.k_done, 1)

    def values(self, pe):
        c = self.c
        for i, bank in enumerate((6, 7, 2, 3)):
            if i >= 2:
                pe.wait_ge(self.kept, 4)
            for s in range(2):
                t = 2 * i + s
                for k in range(KT):
                    last = self.nc.tensor.matmul(c.ps[:, bank, s * D:(s + 1) * D], c.ctxT[:, k, t * P:(t + 1) * P],
                                                 c.kv_w[:, 1, k, :], start=k == 0, stop=k == KT - 1)
            last.then_inc(self.v_done, 1)

    def keep_keys(self, act):
        for i in range(4):
            m, half = i // 2, i % 2
            act.wait_ge(self.k_done, i + 1)
            self.nc.scalar.activation(self.c.l2_kT[:, m, half * CTX:(half + 1) * CTX], self.c.ps[:, 2 + i, :],
                                      ACT.Identity, bias=self.c.cols[:, COL["bk"] + m:COL["bk"] + m + 1])\
                .then_inc(self.kept, 1)

    def keep_values(self, act, first, end):
        for i, bank in list(enumerate((6, 7, 2, 3)))[first:end]:
            act.wait_ge(self.v_done, i + 1)
            self.nc.scalar.copy(self.c.l2_values[:, 2 * i:2 * i + 2, :, 0:HD],
                                self.c.ps[:, bank, :].rearrange("p (t h e) -> p t h e", t=2, h=H))\
                .then_inc(self.kept, 1)


def load_l2_weights(c, d):
    def start(sp):
        w = slot_view(c, [4, KT, D])
        sp.dma_start(w[:, 0], d["l2_w"][0].rearrange("k p n -> p k n")).then_inc(c.early.sem, 16)
        sp.dma_start(w[:, 3], d["l2_w"][3].rearrange("k p n -> p k n")).then_inc(c.early.sem, 16)
        c.early.n += 32
    return start


def l2_linear_attention(nc, c, d, norm):
    F = 64
    PAIRS = H // 2
    ps = c.ps
    with ExitStack() as ctx:
        def sb(n, shape, dt=F32):
            return ctx.enter_context(nc.sbuf_tensor("l2x_" + n, shape, dt))

        sem = stage_semaphores(nc, ctx, "l2x")
        w, fm_q, fm_k, early = slot_view(c, [4, KT, D]), c.fm[:, 0], c.fm[:, 1], c.early.n + 32
        qT, kT, values = sb("qT", [P, KT, T]), c.l2_kT, c.l2_values
        q_feat, k_feat = sb("q_feat", [P, PAIRS, T]), sb("k_feat", [P, CT, H * F])
        kv = sb("kv", [P, B, PAIRS, 64])
        outT, inv, normed = flat(c.ctxT[:]).rearrange("p (g n) -> p g n", g=4), sb("inv", [P, TT, H]), c.z
        mixedT, biased = flat(c.ctx[:])[:, 0:KT * T].rearrange("p (k n) -> p k n", k=KT), c.z2
        filled = sem("filled")
        q_done = sem("q_done")
        kept_act, kept_dve, v_kept = sem("kept_act"), sem("kept_dve"), sem("v_kept")
        qf_done, kf_done, qf_kept, kf_kept = sem("qf_done"), sem("kf_done"), sem("qf_kept"), sem("kf_kept")
        kv_done, kv_kept, out_done, out_kept = sem("kv_done"), sem("kv_kept"), sem("out_done"), sem("out_kept")
        turned, normalised, back, back_act, back_dve = \
            sem("turned"), sem("normalised"), sem("back"), sem("back_act"), sem("back_dve")
        projected, added = sem("projected"), sem("added")
        own = Tally(sem("own"))
        KF_BANKS = (6, 7, 0, 1)
        start_loads = load_l2_weights(c, d)
        norm = norm(ctx)
        block = ctx.enter_context(nc.Block(no_gpsimd_drain=True))

        @block.sync
        def _(sp):
            start_loads(sp)

        @block.gpsimd
        def _(pool):
            nc.gpsimd.memset(kv[:], 0.0).then_inc(filled, 1)
            nc.gpsimd.memset(values[:, :, :, HD:HD + 1], 1.0).then_inc(filled, 1)
            bv = c.rows[:, ROW["bv"]:ROW["bv"] + D].rearrange("p (h e) -> p h e", h=H)
            nc.gpsimd.tensor_tensor(values[:, :, :, 0:HD], values[:, :, :, 0:HD],
                                    bv.unsqueeze(1).broadcast_to([P, CT, H, HD]), ALU.add).then_inc(v_kept, 1)
            norm.gpsimd(pool)

        @block.tensor
        def _(pe):
            for n in range(2 * CT):
                if n >= 4:
                    pe.wait_ge(kf_kept, n - 3)
                nc.tensor.matmul(ps[:, KF_BANKS[n % 4], :], kT[:, n % 2, (n // 2) * P:(n // 2 + 1) * P], fm_k,
                                 start=True, stop=True).then_inc(kf_done, 1)
            pe.wait_ge(filled, 2)
            pe.wait_ge(v_kept, 1)
            for b in range(B):
                pe.wait_ge(kf_kept, CT * (b + 1))
                for j in range(PAIRS):
                    for t in range(4):
                        last = nc.tensor.matmul(ps[:, 2 + b, j * 34:(j + 1) * 34],
                                                k_feat[:, b * 4 + t, j * P:(j + 1) * P],
                                                values[:, b * 4 + t, 2 * j:2 * j + 2, :], start=t == 0, stop=t == 3)
                last.then_inc(kv_done, 1)
                if b == 0:
                    pe.wait_ge(kf_kept, 2 * CT)
                    norm.tensor(pe, wait=False)
            norm.ready(pe)
            pe.wait_ge(c.early.sem, early)
            for m in range(KT):
                for k in range(KT):
                    last = nc.tensor.matmul(ps[:, m, :], w[:, 0, k, m * P:(m + 1) * P], c.hT[:, k, :],
                                            start=k == 0, stop=k == KT - 1)
                last.then_inc(q_done, 1)
            pe.wait_ge(kept_act, 1)
            pe.wait_ge(kept_dve, 1)
            for j in range(PAIRS):
                if j >= 4:
                    pe.wait_ge(qf_kept, j - 3)
                nc.tensor.matmul(ps[:, 4 + j % 4, :], fm_q[:, (j % 4) * P:(j % 4 + 1) * P], qT[:, j // 4, :],
                                 start=True, stop=True).then_inc(qf_done, 1)
            pe.wait_ge(qf_kept, PAIRS)
            for b in range(B):
                pe.wait_ge(kv_kept, 2 * (b + 1))
                for j in range(PAIRS):
                    row = 64 * (j % 2)
                    last = nc.tensor.matmul(ps[row:row + 64, 4 + j // 2, b * S:(b + 1) * S], kv[:, b, j, :],
                                            q_feat[:, j, b * S:(b + 1) * S], start=True, stop=True)
                last.then_inc(out_done, 1)
            pe.wait_ge(out_kept, 4)
            for t in range(TT):
                for g in range(4):
                    last = nc.tensor.transpose(ps[:, t, g * P:(g + 1) * P], outT[:, g, t * P:(t + 1) * P], c.ident[:])
                last.then_inc(turned, 1)
            for t in range(TT):
                pe.wait_ge(normalised, t + 1)
                for k in range(KT):
                    last = nc.tensor.transpose(ps[:, 4 + k, t * P:(t + 1) * P], normed[:, t, k * P:(k + 1) * P],
                                               c.ident[:])
            last.then_inc(back, 1)
            pe.wait_ge(back_act, 1)
            pe.wait_ge(back_dve, 1)
            for t in range(TT):
                for k in range(KT):
                    last = nc.tensor.matmul(ps[:, 6 + t // 2, (t % 2) * D:(t % 2 + 1) * D],
                                            mixedT[:, k, t * P:(t + 1) * P], w[:, 3, k, :],
                                            start=k == 0, stop=k == KT - 1)
                last.then_inc(projected, 1)

        def bias(name, m):
            return c.cols[:, COL[name] + m:COL[name] + m + 1]

        @block.scalar
        def _(act):
            norm.scalar(act)
            act.wait_ge(q_done, 1)
            nc.scalar.activation(qT[:, 0, :], ps[:, 0, :], ACT.Identity, bias=bias("bq", 0)).then_inc(kept_act, 1)
            for j in range(PAIRS):
                act.wait_ge(qf_done, j + 1)
                nc.scalar.activation(q_feat[:, j, :], ps[:, 4 + j % 4, :], ACT.Relu).then_inc(qf_kept, 1)
            act.wait_ge(out_done, 2)
            for g in range(4):
                nc.scalar.copy(outT[:, g, :], ps[:, 4 + g, :]).then_inc(out_kept, 1)
            act.wait_ge(back, 1)
            nc.scalar.copy(mixedT[:, 0, :], ps[:, 4, :]).then_inc(back_act, 1)

        @block.vector
        def _(dve):
            V = nc.vector
            for n in range(2 * CT):
                dve.wait_ge(kf_done, n + 1)
                V.tensor_scalar(k_feat[:, n // 2, (n % 2) * 512:(n % 2 + 1) * 512], ps[:, KF_BANKS[n % 4], :], 0.0,
                                c.att_mask[:, n // 2:n // 2 + 1], ALU.max, ALU.mult).then_inc(kf_kept, 1)
            norm.vector(dve)
            dve.wait_ge(filled, 2)
            for b in range(B):
                dve.wait_ge(kv_done, b + 1)
                for head in range(2):
                    rows = slice(64 * head, 64 * head + 64)
                    src = ps[rows, 2 + b, 0:PAIRS * 34].rearrange("p (j e) -> p j e", j=PAIRS)
                    V.tensor_copy(kv[rows, b, :, 32 * head:32 * head + HD + 1],
                                  src[:, :, 17 * head:17 * head + 17]).then_inc(kv_kept, 1)
            dve.wait_ge(q_done, 2)
            V.tensor_scalar(qT[:, 1, :], ps[:, 1, :], bias("bq", 1), None, ALU.add).then_inc(kept_dve, 1)
            for t in range(TT):
                dve.wait_ge(turned, t + 1)
                heads = ps[:, t, :].rearrange("p (h e) -> p h e", h=H)
                settle(dve, own, V.tensor_scalar(inv[:, t, :], heads[:, :, HD], 1e-8, None, ALU.add))
                settle(dve, own, V.reciprocal(inv[:, t, :], inv[:, t, :]))
                V.tensor_tensor(normed[:, t, :].rearrange("p (h e) -> p h e", h=H), heads[:, :, 0:HD],
                                inv[:, t, :].unsqueeze(2).broadcast_to([P, H, HD]), ALU.mult).then_inc(normalised, 1)
            dve.wait_ge(back, 1)
            V.tensor_copy(mixedT[:, 1, :], ps[:, 5, :]).then_inc(back_dve, 1)
            bo = c.rows[:, ROW["bo"]:ROW["bo"] + D]
            for t in range(TT):
                dve.wait_ge(projected, 2 * (t // 2) + 2)
                settle(dve, own, V.tensor_tensor(biased[:, t, :], ps[:, 6 + t // 2, (t % 2) * D:(t % 2 + 1) * D], bo,
                                                 ALU.add))
                V.scalar_tensor_tensor(out=c.x[:, t, :], in0=biased[:, t, :], scalar=c.gate[:, 2:3],
                                       in1=c.x[:, t, :], op0=ALU.mult, op1=ALU.add).then_inc(added, 1)
            dve.wait_ge(added, TT)


def l2_self_attention(nc, c, d, z, residual, norms):
    SCALE = 1.0 / float(np.sqrt(np.float32(P)))
    PW = 3 * 2 * KT * P + 2 * D
    QKV = 3 * 2 * KT * P
    PAIRS = H // 2
    ps = c.ps
    Q, K, SC, TR, ACC = 0, 1, 2, 4, 6
    with ExitStack() as ctx:
        def sb(n, shape, dt=F32):
            return ctx.enter_context(nc.sbuf_tensor("l2a_" + n, shape, dt))

        sem = stage_semaphores(nc, ctx, "l2a")
        w = sb("w", [P, 2, PW])
        w_top, w_rest = sb("w_top", [P, 2, PW], F32R), sb("w_rest", [P, 2, PW], F32R)
        qT, kT, v = sb("qT", [P, T]), sb("kT", [P, T]), \
            flat(c.ctx[:]).rearrange("p (s t n) -> p s t n", s=2, t=TT)
        spare = flat(c.l2_kT[:])[:, 0:2 * B * 3 * P].rearrange("p (w b n) -> p w b n", w=2, b=B)
        probs, probsT = spare[:, 0], spare[:, 1]
        mix_top, mix_rest = sb("mix_top", [P, T], F32R), sb("mix_rest", [P, T], F32R)
        top, bias = sb("top", [P, B, 2]), sb("bias", [P, B, 2])
        total, inv = sb("total", [P, B, 2]), sb("inv", [P, B, 2])
        loaded, wo_loaded = [sem("loaded0"), sem("loaded1")], [sem("wo_loaded0"), sem("wo_loaded1")]
        q_done, k_done, v_done, scored = sem("q_done"), sem("k_done"), sem("v_done"), sem("scored")
        q_kept, k_kept, v_kept = sem("q_kept"), sem("k_kept"), sem("v_kept")
        topped, biased, exped, scaled = sem("topped"), sem("biased"), sem("exped"), sem("scaled")
        inverted = sem("inverted")
        turned, turn_kept, mixed, mix_kept = sem("turned"), sem("turn_kept"), sem("mixed"), sem("mix_kept")
        projected, added = sem("projected"), sem("added")
        qkv_top, qkv_cut, wo_top, wo_cut = sem("qkv_top"), sem("qkv_cut"), sem("wo_top"), sem("wo_cut")
        mix_topped = sem("mix_topped")
        norms = [norm(ctx) for norm in norms]
        block = ctx.enter_context(nc.Block(no_gpsimd_drain=True))

        def static(h):
            return isinstance(h, int)

        @block.sync
        def _(sp):
            for s in range(2):
                sp.dma_start(w[:, s, 0:QKV], d["l2a_w"][s, :, 0:QKV]).then_inc(loaded[s], 16)
                sp.dma_start(w[:, s, QKV:PW], d["l2a_w"][s, :, QKV:PW]).then_inc(wo_loaded[s], 16)

            def load(pair, slot):
                src = d["l2a_w"][bass.ds(pair, 1)].rearrange("a p n -> p (a n)")
                sp.wait_ge(qkv_cut, 2 * pair - 2)
                sp.dma_start(w[:, slot, 0:QKV], src[:, 0:QKV]).then_inc(loaded[slot], 16)
                sp.wait_ge(wo_cut, 2 * pair - 2)
                sp.dma_start(w[:, slot, QKV:PW], src[:, QKV:PW]).then_inc(wo_loaded[slot], 16)
            repeat(sp, 2, PAIRS, 2, load)

        @block.tensor
        def _(pe):
            for norm in norms:
                norm.tensor(pe)
            for i in range(2):
                nc.tensor.matmul(ps[:, ACC + i, :], c.zero_bf[:, 0:P], c.zero_bf[:], start=True, stop=True,
                                 skip_group_check=True)

            def product(to, lefts, rights, slices, first, last_one):
                (lt, lr), (rt, rr), (ls, rs) = lefts, rights, slices
                nc.tensor.matmul(to, lt[ls], rt[rs], start=first, stop=False)
                nc.tensor.matmul(to, lt[ls], rr[rs], start=False, stop=False)
                return nc.tensor.matmul(to, lr[ls], rt[rs], start=False, stop=last_one)
            W, HT, ALL = (w_top, w_rest), (c.h_top, c.h_rest), slice(None)

            def head_weights(phase, which, k):
                at = which * 512 + k * 256 + (phase % 2) * P
                return ALL, phase // 2 % 2, slice(at, at + P)

            def queries(h, phase):
                pe.wait_ge(qkv_cut, h - phase % 2 + 2)
                if not static(h) or h >= 2:
                    pe.wait_ge(mix_kept, h - 1)
                for k in range(KT):
                    last = product(ps[:, Q, :], W, HT, (head_weights(phase, 0, k), (ALL, k)), k == 0, k == KT - 1)
                last.then_inc(q_done, 1)

            def keys(h, phase):
                pe.wait_ge(qkv_cut, h - phase % 2 + 2)
                if not static(h) or h >= 1:
                    pe.wait_ge(v_kept, h + 1)
                for k in range(KT):
                    last = product(ps[:, K, :], W, HT, (head_weights(phase, 1, k), (ALL, k)), k == 0, k == KT - 1)
                last.then_inc(k_done, 1)

            def values(n, phase, k_ready):
                slot = phase // 2 % 2
                pe.wait_ge(qkv_cut, n - phase % 2 + 2)
                pe.wait_ge(k_kept, k_ready)
                for i in range(2):
                    t = 2 * (phase % 2) + i
                    for k in range(KT):
                        last = product(ps[:, K, i * D:(i + 1) * D], HT, W,
                                       ((ALL, k, slice(t * P, (t + 1) * P)),
                                        (ALL, slot, slice(1024 + k * 256, 1280 + k * 256))), k == 0, k == KT - 1)
                last.then_inc(v_done, 1)

            def scores(h):
                pe.wait_ge(q_kept, h + 1)
                pe.wait_ge(k_kept, h + 1)
                for b in range(B):
                    if not static(h) or h >= 1:
                        pe.wait_ge(exped, 4 * h - 2 + 2 * b)
                    for half in range(2):
                        to = ps[:, SC + b, half * P:half * P + (half + 1) * P]
                        q0 = b * S + half * P
                        nc.tensor.matmul(to, qT[:, q0:q0 + P], kT[:, b * S:b * S + (half + 1) * P],
                                         start=True, stop=False)
                        last = nc.tensor.matmul(to[:, half * P:(half + 1) * P], c.ident_bf[:], c.mask_q[:],
                                                start=False, stop=True)
                    last.then_inc(scored, 1)

            def turn(h):
                for b in range(B):
                    pe.wait_ge(scaled, 4 * h + 2 * b + 2)
                    if not static(h) or h >= 1:
                        pe.wait_ge(turn_kept, 2 * h + b - 1)
                    for i in range(3):
                        last = nc.tensor.transpose(ps[:, TR + b, i * P:(i + 1) * P], probs[:, b, i * P:(i + 1) * P],
                                                   c.ident[:])
                    last.then_inc(turned, 1)

            def mix(h, phase, more):
                pair_slot = phase // 2 % 2
                pe.wait_ge(q_kept, h + 2 if more else h + 1)
                pe.wait_ge(v_kept, h + 2 - phase % 2)
                for b in range(B):
                    pe.wait_ge(turn_kept, 2 * h + b + 1)
                    for half in range(2):
                        at = b * S + half * P
                        src = probsT[:, b, 0:2 * P] if half == 0 else probsT[:, b, 2 * P:3 * P]
                        last = nc.tensor.matmul(ps[:, Q, at:(b + 1) * S],
                                                v[:, pair_slot, 2 * b + half, (phase % 2) * P:(phase % 2 + 1) * P],
                                                src, start=half == 0, stop=half == 1)
                last.then_inc(mixed, 1)

            def project(h, phase):
                pe.wait_ge(mix_kept, h + 1)
                pe.wait_ge(wo_cut, h - phase % 2 + 2)
                at = 1536 + (phase % 2) * D
                for t in range(TT):
                    for a, b in ((mix_top, w_top), (mix_top, w_rest), (mix_rest, w_top)):
                        last = nc.tensor.matmul(ps[:, ACC + t // 2, (t % 2) * D:(t % 2 + 1) * D],
                                                a[:, t * P:(t + 1) * P], b[:, phase // 2 % 2, at:at + D],
                                                start=False, stop=True, skip_group_check=True)
                last.then_inc(projected, 1)

            def step(h, phase, more=True, more_v=True):
                if more:
                    keys(h + 1, (phase + 1) % 4)
                if not static(h) or h >= 1:
                    project(h - 1, (phase - 1) % 4)
                if more:
                    queries(h + 1, (phase + 1) % 4)
                if more_v:
                    values(h + 2, (phase + 2) % 4, h + 2)
                turn(h)
                if more:
                    scores(h + 1)
                mix(h, phase, more)

            queries(0, 0)
            keys(0, 0)
            values(0, 0, 1)
            scores(0)
            pe.wait_ge(v_kept, 1)
            values(1, 1, 1)
            for h in range(2):
                step(h, h)
            repeat(pe, 2, H - 2, 4, step)
            step(H - 2, (H - 2) % 4, True, False)
            step(H - 1, (H - 1) % 4, False, False)
            project(H - 1, (H - 1) % 4)

        @block.gpsimd
        def _(pool):
            def rest(pair, slot, lo, hi, top, cut):
                pool.wait_ge(top, 2 * pair + 2)
                nc.gpsimd.tensor_tensor(w_rest[:, slot, lo:hi], w[:, slot, lo:hi], w_top[:, slot, lo:hi],
                                        ALU.subtract).then_inc(cut, 2)

            def step(pair, slot):
                rest(pair - 1, (slot + 1) % 2, QKV, PW, wo_top, wo_cut)
                rest(pair, slot, 0, QKV, qkv_top, qkv_cut)
            norms[0].gpsimd(pool)
            norms[1].gpsimd(pool, root_only=True)
            rest(0, 0, 0, QKV, qkv_top, qkv_cut)
            norms[1].gpsimd_cut(pool)
            step(1, 1)
            repeat(pool, 2, PAIRS, 2, step)
            rest(PAIRS - 1, 1, QKV, PW, wo_top, wo_cut)

        @block.scalar
        def _(act):
            def top_qkv(done, slot, bytes_in):
                act.wait_ge(loaded[slot], bytes_in)
                if not static(done) or done > 0:
                    act.wait_ge(q_done, done)
                nc.scalar.copy(w_top[:, slot, 0:QKV], w[:, slot, 0:QKV]).then_inc(qkv_top, 2)

            def top_wo(done, slot, bytes_in):
                act.wait_ge(wo_loaded[slot], bytes_in)
                if not static(done) or done > 0:
                    act.wait_ge(projected, done)
                nc.scalar.copy(w_top[:, slot, QKV:PW], w[:, slot, QKV:PW]).then_inc(wo_top, 2)

            def keep_q(h):
                act.wait_ge(q_done, h + 1)
                nc.scalar.copy(qT[:], ps[:, Q, :]).then_inc(q_kept, 1)

            def keep_v(n, phase):
                act.wait_ge(v_done, n + 1)
                if not static(n) or n >= 4:
                    act.wait_ge(mixed, n - phase % 2 - 2)
                nc.scalar.copy(v[:, phase // 2 % 2, 2 * (phase % 2):2 * (phase % 2) + 2, :],
                               ps[:, K, :].rearrange("p (t n) -> p t n", t=2)).then_inc(v_kept, 1)

            def exponentials(h):
                for b in range(B):
                    for half in range(2):
                        at, width = half * P, (half + 1) * P
                        act.wait_ge(biased, 4 * h + 2 * b + half + 1)
                        if not static(h) or h >= 1:
                            act.wait_ge(turned, 2 * h + b - 1)
                        nc.scalar.activation(probs[:, b, at:at + width], ps[:, SC + b, at:at + width], ACT.Exp,
                                             bias=bias[:, b, half:half + 1], scale=SCALE,
                                             accum_out=total[:, b, half:half + 1]).then_inc(exped, 1)

            def step(h, phase, more=True, more_v=True):
                exponentials(h)
                if more:
                    keep_q(h + 1)
                if more_v:
                    keep_v(h + 2, (phase + 2) % 4)
                if phase % 2 and more:
                    top_wo(h - 1, (phase + 1) // 2 % 2, (h - phase) * 4 + (16 if phase == 1 else 32))
                    if not static(h) or (h + 3) // 2 < PAIRS:
                        top_qkv(h + 1, (phase + 3) // 2 % 2, (h - phase) * 4 + 32)
            top_qkv(0, 0, 16)
            for norm in norms:
                norm.scalar(act)
            top_wo(0, 0, 16)
            top_qkv(0, 1, 16)
            keep_q(0)
            keep_v(0, 0)
            keep_v(1, 1)
            for h in range(2):
                step(h, h)
            repeat(act, 2, H - 4, 4, step)
            for h in (H - 4, H - 3):
                step(h, h % 4)
            step(H - 2, (H - 2) % 4, True, False)
            step(H - 1, (H - 1) % 4, False, False)

        @block.vector
        def _(dve):
            V = nc.vector

            def keep_k(h):
                dve.wait_ge(k_done, h + 1)
                V.tensor_copy(kT[:], ps[:, K, :]).then_inc(k_kept, 1)

            def maxima(h):
                for b in range(B):
                    dve.wait_ge(scored, 2 * h + b + 1)
                    for half in range(2):
                        at, width = half * P, (half + 1) * P
                        V.tensor_reduce(top[:, b, half:half + 1], ps[:, SC + b, at:at + width], AX.X, ALU.max)\
                            .then_inc(topped, 1)
                for b in range(B):
                    for half in range(2):
                        dve.wait_ge(topped, 4 * h + 2 * b + half + 1)
                        V.tensor_scalar(bias[:, b, half:half + 1], top[:, b, half:half + 1], -SCALE, None, ALU.mult)\
                            .then_inc(biased, 1)

            def normalise(h):
                for b in range(B):
                    dve.wait_ge(exped, 4 * h + 2 * b + 2)
                    V.reciprocal(inv[:, b, :], total[:, b, :]).then_inc(inverted, 1)
                    dve.wait_ge(inverted, 2 * h + b + 1)
                    for half in range(2):
                        at, width = half * P, (half + 1) * P
                        V.tensor_scalar(probs[:, b, at:at + width], probs[:, b, at:at + width],
                                        inv[:, b, half:half + 1], None, ALU.mult).then_inc(scaled, 1)

            def keep_turned(h):
                for b in range(B):
                    dve.wait_ge(turned, 2 * h + b + 1)
                    V.tensor_copy(probsT[:, b, :], ps[:, TR + b, 0:3 * P]).then_inc(turn_kept, 1)

            def keep_mixed(h):
                dve.wait_ge(mixed, h + 1)
                if not static(h) or h >= 1:
                    dve.wait_ge(projected, h)
                V.tensor_copy(mix_top[:], ps[:, Q, :]).then_inc(mix_topped, 1)
                dve.wait_ge(mix_topped, h + 1)
                V.tensor_tensor(mix_rest[:], ps[:, Q, :], mix_top[:], ALU.subtract).then_inc(mix_kept, 1)

            def step(h, phase, more=True, more_v=True):
                maxima(h)
                if not static(h) or h >= 1:
                    keep_mixed(h - 1)
                if more:
                    keep_k(h + 1)
                normalise(h)
                keep_turned(h)
            for norm in norms:
                norm.vector(dve)
            keep_k(0)
            for h in range(2):
                step(h, h)
            repeat(dve, 2, H - 1, 4, step)
            step(H - 1, 3, False, False)
            keep_mixed(H - 1)
            dve.wait_ge(projected, H)
            for t in range(TT):
                V.tensor_tensor(residual[:, t, :], ps[:, ACC + t // 2, (t % 2) * D:(t % 2 + 1) * D], z[:, t, :],
                                ALU.add).then_inc(added, 1)
            dve.wait_ge(added, TT)


L3_COLS = {"q": (0, 256), "k": (256, 64), "v": (320, 64), "o": (384, 256)}
QB, QEPS = 127.0, 1e-5


def quantise(dve, V, own, y, scale):
    settle(dve, own, V.tensor_scalar(y, y, scale, QB - QEPS, ALU.mult, ALU.min))
    return V.tensor_scalar(y, y, -(QB - QEPS), None, ALU.max)


class L3Context:

    def __init__(self, nc, c, d, ctx):
        self.nc, self.c, self.d = nc, c, d
        sem = stage_semaphores(nc, ctx, "l3p")

        def sb(n, shape, dt=F32):
            return ctx.enter_context(nc.sbuf_tensor("l3p_" + n, shape, dt))
        self.sums, self.minus_mean, self.ones = sb("sums", [P, 4]), sb("minus_mean", [P, 4]), sb("ones", [P, P])
        self.largest, self.all_largest, self.scale = (sb(n, [P, 2]) for n in ("largest", "all_largest", "scale"))
        self.kT = sb("kT", [64, 1, B * CTX])
        self.loaded, self.filled, self.summed, self.mean_done, self.mean_ready, self.signed = (
            sem(n) for n in ("loaded", "filled", "summed", "mean_done", "mean_ready", "signed"))
        self.k_done, self.v_done, self.kept, self.reduced, self.all_reduced, self.scaled = (
            sem(n) for n in ("k_done", "v_done", "kept", "reduced", "all_reduced", "scaled"))
        self.own, self.pool_own = Tally(sem("own")), Tally(sem("pool_own"))
        self.w = slot_view(c, [KT, 640])
        self.keys = KeySplit(nc, ctx, sem, "l3x", self.kT, 1, 64)
        c.l3_keys = self.keys

    def load(self, sp):
        sp.dma_start(self.w, self.d["l3_w"].rearrange("k p n -> p k n")).then_inc(self.loaded, 16)

    def bounce(self, sp):
        bounce_keys(sp, self.keys)

    def gpsimd(self, pool):
        G, own, c = self.nc.gpsimd, self.pool_own, self.c
        G.memset(self.ones[:], 1.0).then_inc(self.filled, 1)
        G.memset(self.largest[:], 0.0).then_inc(self.filled, 1)
        pool.wait_ge(self.reduced, 1)
        G.partition_all_reduce(self.all_largest[:], self.largest[:], P, bass.bass_isa.ReduceOp.max)\
            .then_inc(self.all_reduced, 1)
        pool.wait_ge(self.scaled, 1)
        pool.wait_ge(self.all_reduced, 1)
        for y, s in ((c.v3[:], self.scale[:, 1:2]), (self.kT[:], self.scale[0:64, 0:1])):
            settle(pool, own, G.tensor_scalar(y, y, s, QB - QEPS, ALU.mult, ALU.min))
            settle(pool, own, G.tensor_scalar(y, y, -(QB - QEPS), None, ALU.max))
        split_keys(pool, G, self.keys)

    def tensor(self, pe):
        c, ps, T_ = self.c, self.c.ps, self.nc.tensor
        pe.wait_ge(self.filled, 2)
        pe.wait_ge(self.summed, 1)
        T_.matmul(ps[:, 7, 0:4], self.ones[:], self.sums[:], start=True, stop=True).then_inc(self.mean_done, 1)
        pe.wait_ge(self.signed, 4)
        for half in range(2):
            for k in range(KT):
                last = T_.matmul(ps[0:64, 2 + half, :], c.w_bin[:, k, 256:320].bitcast(F32),
                                 c.ctxT[:, k, half * CTX:(half + 1) * CTX], start=k == 0, stop=k == KT - 1)
            last.then_inc(self.k_done, 1)
        for t in range(CT):
            for k in range(KT):
                last = T_.matmul(ps[:, 4, t * 64:(t + 1) * 64], c.ctxT[:, k, t * P:(t + 1) * P],
                                 c.w_bin[:, k, 320:384].bitcast(F32), start=k == 0, stop=k == KT - 1)
        last.then_inc(self.v_done, 1)
        pe.wait_ge(self.kept, 3)

    def scalar(self, act):
        act.wait_ge(self.mean_ready, 4)
        for i, (at, n) in enumerate(L3_COLS.values()):
            self.nc.scalar.activation(self.c.w_bin[:, :, at:at + n], self.w[:, :, at:at + n], ACT.Sign,
                                      bias=self.minus_mean[:, i:i + 1]).then_inc(self.signed, 1)

    def means(self, dve):
        V, ps, own = self.nc.vector, self.c.ps, self.own
        dve.wait_ge(self.loaded, 16)
        for i, (at, n) in enumerate(L3_COLS.values()):
            last = own.up(V.tensor_reduce(self.minus_mean[:, i:i + 1], self.w[:, :, at:at + n], AX.XY, ALU.add))
        dve.wait_ge(own.sem, last)
        V.tensor_copy(self.sums[:], self.minus_mean[:]).then_inc(self.summed, 1)
        dve.wait_ge(self.mean_done, 1)
        dve.wait_ge(self.summed, 1)
        for i, (_, n) in enumerate(L3_COLS.values()):
            V.tensor_scalar(self.minus_mean[:, i:i + 1], ps[:, 7, i:i + 1], -1.0 / (D * n), None, ALU.mult)\
                .then_inc(self.mean_ready, 1)

    def vector(self, dve):
        V, c, ps, own = self.nc.vector, self.c, self.c.ps, self.own
        kb = c.cols[0:64, COL["k_b"]:COL["k_b"] + 1]
        for half in range(2):
            dve.wait_ge(self.k_done, half + 1)
            V.tensor_scalar(self.kT[:, 0, half * CTX:(half + 1) * CTX], ps[0:64, 2 + half, :], kb, None, ALU.add)\
                .then_inc(self.kept, 1)
        vb = c.rows[:, ROW["v_b"]:ROW["v_b"] + 64].unsqueeze(1).broadcast_to([P, CT, 64])
        dve.wait_ge(self.v_done, 1)
        V.tensor_tensor(c.v3[:], ps[:, 4, :].rearrange("p (t n) -> p t n", t=CT), vb, ALU.add).then_inc(self.kept, 1)
        dve.wait_ge(self.filled, 2)
        dve.wait_ge(self.kept, 3)
        own.up(V.tensor_reduce(self.largest[0:64, 0:1], self.kT[:], AX.XY, ALU.max, apply_absolute_value=True))
        last = own.up(V.tensor_reduce(self.largest[:, 1:2], c.v3[:], AX.XY, ALU.max, apply_absolute_value=True))
        dve.wait_ge(own.sem, last)
        V.tensor_copy(self.sums[:, 0:2], self.largest[:]).then_inc(self.reduced, 1)
        dve.wait_ge(self.all_reduced, 1)
        settle(dve, own, V.tensor_scalar(self.scale[:], self.all_largest[:], QEPS, None, ALU.add))
        settle(dve, own, V.reciprocal(self.scale[:], self.scale[:]))
        V.tensor_scalar(self.scale[:], self.scale[:], QB, None, ALU.mult).then_inc(self.scaled, 1)


def l3_queries(nc, c, d, s, norm):
    ps = c.ps
    with ExitStack() as ctx:
        sem = stage_semaphores(nc, ctx, "l3q")
        largest, all_largest, scale = (ctx.enter_context(nc.sbuf_tensor("l3q_" + n, [P, 1], F32))
                                       for n in ("largest", "all_largest", "scale"))
        q_done, kept, reduced, all_reduced = sem("q_done"), sem("kept"), sem("reduced"), sem("all_reduced")
        placed, out = sem("placed"), sem("out")
        own = Tally(sem("own"))
        norm = norm(ctx)
        block = ctx.enter_context(nc.Block(no_gpsimd_drain=True))

        @block.gpsimd
        def _(pool):
            norm.gpsimd(pool)
            nc.gpsimd.tensor_copy(c.values[:, :, 0:4, 0:HD], c.v3[:].rearrange("p t (h e) -> p t h e", h=4))\
                .then_inc(placed, 1)
            pool.wait_ge(reduced, 1)
            pool.wait_ge(placed, 1)
            nc.gpsimd.partition_all_reduce(all_largest[:], largest[:], P, bass.bass_isa.ReduceOp.max)\
                .then_inc(all_reduced, 1)

        @block.tensor
        def _(pe):
            norm.tensor(pe)
            for m in range(KT):
                for k in range(KT):
                    last = nc.tensor.matmul(ps[:, 2 + m, :], c.w_bin[:, k, m * P:(m + 1) * P].bitcast(F32),
                                            c.hT[:, k, :], start=k == 0, stop=k == KT - 1)
                last.then_inc(q_done, 1)

        def bias(m):
            return c.cols[:, COL["q_b"] + m:COL["q_b"] + m + 1]

        @block.scalar
        def _(act):
            norm.scalar(act)
            act.wait_ge(q_done, 1)
            nc.scalar.activation(s.qT[:, 0, :], ps[:, 2, :], ACT.Identity, bias=bias(0)).then_inc(kept, 1)

        @block.vector
        def _(dve):
            V = nc.vector
            norm.vector(dve)
            dve.wait_ge(q_done, 2)
            settle(dve, own, V.tensor_scalar(s.qT[:, 1, :], ps[:, 3, :], bias(1), None, ALU.add))
            dve.wait_ge(kept, 1)
            V.tensor_reduce(largest[:], s.qT[:], AX.XY, ALU.max, apply_absolute_value=True).then_inc(reduced, 1)
            dve.wait_ge(all_reduced, 1)
            settle(dve, own, V.tensor_scalar(scale[:], all_largest[:], QEPS, None, ALU.add))
            settle(dve, own, V.reciprocal(scale[:], scale[:]))
            settle(dve, own, V.tensor_scalar(scale[:], scale[:], QB, None, ALU.mult))
            quantise(dve, V, own, s.qT[:], scale[:]).then_inc(out, 1)
            dve.wait_ge(out, 1)


def l3_output(nc, c, d, s, norm):
    ps = c.ps
    with ExitStack() as ctx:
        def sb(n, shape, dt=F32):
            return ctx.enter_context(nc.sbuf_tensor("l3o_" + n, shape, dt))

        sem = stage_semaphores(nc, ctx, "l3o")
        y, largest = sb("y", [P, TT, D]), sb("largest", [P, 2])
        all_largest, scale = sb("all", [P, 2]), sb("scale", [P, 2])
        done, reduced, all_reduced, added = sem("done"), sem("reduced"), sem("all_reduced"), sem("added")
        own = Tally(sem("own"))
        norm = norm(ctx)
        block = ctx.enter_context(nc.Block(no_gpsimd_drain=True))

        @block.scalar
        def _(act):
            norm.scalar(act)

        @block.tensor
        def _(pe):
            norm.tensor(pe)
            for t in range(TT):
                for k in range(KT):
                    for a in (c.h_top, c.h_rest):
                        last = nc.tensor.matmul(ps[:, t, 0:D], a[:, k, t * P:(t + 1) * P], c.w_bin[:, k, 384:640],
                                                start=k == 0 and a is c.h_top, stop=k == KT - 1 and a is c.h_rest)
                last.then_inc(done, 1)

        @block.gpsimd
        def _(pool):
            norm.gpsimd(pool)
            pool.wait_ge(reduced, 1)
            nc.gpsimd.partition_all_reduce(all_largest[:, 0:1], largest[:, 0:1], P, bass.bass_isa.ReduceOp.max)\
                .then_inc(all_reduced, 1)

        @block.vector
        def _(dve):
            V = nc.vector
            norm.vector(dve)
            ob = c.rows[:, ROW["o_b"]:ROW["o_b"] + D]
            for t in range(TT):
                dve.wait_ge(done, t + 1)
                last = own.up(V.tensor_tensor(y[:, t, :], ps[:, t, 0:D], ob, ALU.add))
            dve.wait_ge(own.sem, last)
            V.tensor_reduce(largest[:, 0:1], y[:], AX.XY, ALU.max, apply_absolute_value=True).then_inc(reduced, 1)
            dve.wait_ge(all_reduced, 1)
            settle(dve, own, V.tensor_scalar(scale[:, 0:1], all_largest[:, 0:1], QEPS, None, ALU.add))
            settle(dve, own, V.reciprocal(scale[:, 0:1], scale[:, 0:1]))
            settle(dve, own, V.tensor_scalar(scale[:, 0:1], scale[:, 0:1], QB, None, ALU.mult))
            settle(dve, own, quantise(dve, V, own, y[:], scale[:, 0:1]))
            V.scalar_tensor_tensor(out=flat(c.x[:]), in0=flat(y[:]), scalar=c.gate[:, 3:4], in1=flat(c.x[:]),
                                   op0=ALU.mult, op1=ALU.add).then_inc(added, 1)
            dve.wait_ge(added, 1)


def l3_attention(nc, c, d, norm):
    s = Core()
    with ExitStack() as ctx:
        finished = stage_semaphores(nc, ctx, "l3x")("placed")
        with ExitStack() as inner:
            s.qT = inner.enter_context(nc.sbuf_tensor("l3x_qT", [P, KT, T], F32))
            l3_queries(nc, c, d, s, norm)

            def finish(dve, own, t, heads, inv):
                nc.vector.tensor_tensor(c.z[:, t, :].rearrange("p (h e) -> p h e", h=H), heads, inv, ALU.mult)\
                    .then_inc(finished, 1)
                if t == TT - 1:
                    dve.wait_ge(finished, TT)
            small_head_attention(nc, c, "l3x", s.qT, c.values[:, :, 0:4, :], 4, False, finish)
        l3_output(nc, c, d, s, lambda ctx: Norm(nc, c, ctx, "l3x_ln", c.z, c.h, LN_EPS, c.hT,
                                                scale="ln_g", shift="ln_b", cut=True))


def make_plan(nc, c, d):
    def norm(tag, src=c.x, dst=c.h, eps=LN_EPS, out=c.hT, **more):
        return lambda ctx: Norm(nc, c, ctx, tag, src, dst, eps, out, **more)

    return [
        [lambda: l0_attention(nc, c, d, norm("l0x_norm"))],
        [lambda: ffn_stage(nc, c, d, "l0", norm("l0f_norm", even_odd=True, cut=True),
                           context=lambda sem: L2Context(nc, c, sem))],
        [lambda: l1_attention(nc, c, d, norm("l1x_norm"), lambda ctx: L3Context(nc, c, d, ctx))],
        [lambda: ffn_stage(nc, c, d, "l1", norm("l1f_norm", cut=True),
                           also=lambda sp: stack_keys(sp, c, c.l3_keys))],
        [lambda: l2_linear_attention(nc, c, d, norm("l2x_norm"))],
        [lambda: l2_self_attention(nc, c, d, c.z, c.z2, [
            norm("l2z_norm", dst=c.z, out=None),
            norm("l2a_norm", src=c.z, eps=RMS_EPS, rms=True, scale="ln1_w", cut=True)]),
         lambda: ffn_stage(nc, c, d, "l2", norm("l2f_norm", src=c.z2, eps=RMS_EPS, rms=True, scale="ln2_w", cut=True),
                           residual=c.z2)],
        [lambda: l3_attention(nc, c, d, norm("l3x_norm"))],
        [lambda: ffn_stage(nc, c, d, "l3", norm("l3f_norm", cut=True))],
    ]


def build(nc, d, out):
    c = Core()
    with ExitStack() as ctx:
        def sb(name, shape, dt=F32):
            return ctx.enter_context(nc.sbuf_tensor(name, shape, dt))
        c.x, c.h, c.hT = sb("x", [P, TT, D]), sb("h", [P, TT, D]), sb("hT", [P, KT, T])
        c.h_top, c.h_rest = sb("h_top", [P, KT, T], F32R), sb("h_rest", [P, KT, T], F32R)
        c.ctxT, c.ctx = sb("ctxT", [P, KT, B * CTX]), sb("ctx_tok", [P, CT, D])
        c.cols, c.rows, c.gate = sb("cols", [P, N_COLS]), sb("rows", [P, N_ROWS]), sb("gate", [P, 8])
        c.z, c.z2 = sb("z", [P, TT, D]), sb("z2", [P, TT, D])
        c.att_mask = sb("att_mask", [P, CT])
        c.ident, c.ident_bf = sb("ident", [P, P]), sb("ident_bf", [P, P], BF16)
        c.mask_q, c.mask_k = sb("mask_q", [P, P], BF16), sb("mask_k", [P, P], BF16)
        c.zero_bf, c.minus_half = sb("zero_bf", [P, 512], BF16), sb("minus_half", [P, 8])
        c.ps = ctx.enter_context(nc.psum_tensor("ps", [P, 8, 512], F32))
        c.before, c.routers, c.weightT = sb("before", [P, 16, 16]), sb("routers", [P, KT, 32]), sb("weightT", [P, T], BF16)
        c.slots = sb("slots", [P, SLOTS, FW])
        c.slot_loaded = [ctx.enter_context(nc.semaphore(f"slot_loaded{s}")) for s in range(SLOTS)]
        c.slot_loads = [0] * SLOTS
        c.x_loaded, c.rows_loaded, c.ctxT_loaded, c.inputs_loaded, c.fp4_loaded = \
            (ctx.enter_context(nc.semaphore(n))
             for n in ("x_loaded", "rows_loaded", "ctxT_loaded", "inputs_loaded", "fp4_loaded"))
        c.early = Tally(ctx.enter_context(nc.semaphore("early_loads")))
        c.stacked = Tally(ctx.enter_context(nc.semaphore("keys_stacked")))
        c.k_stack = sb("k_stack", [P, H, B * CTX], BF16)
        c.w_bin, c.v3 = sb("w_bin", [P, KT, 640], F32R), sb("v3", [P, CT, 64])
        c.l2_kT, c.l2_values = sb("l2_kT", [P, KT, B * CTX]), sb("l2_values", [P, CT, H, HD + 1])
        c.stack_sel = sb("stack_sel", [P, 8, 3, STACK], BF16)
        c.fm = sb("feature_maps", [P, 2, 512])
        c.kv_w = sb("kv_w", [P, 2, KT, D])
        c.kv_w_loaded = ctx.enter_context(nc.semaphore("kv_w_loaded"))
        c.values = sb("values", [P, CT, H, 32])
        setup_stage(nc, c, d)
        for layer in make_plan(nc, c, d):
            for stage in layer:
                stage()
        stored = ctx.enter_context(nc.semaphore("stored"))
        with nc.Block(no_gpsimd_drain=True) as block:
            @block.sync
            def _(sp):
                sp.dma_start(out.rearrange("t p n -> p t n"), c.x[:]).then_inc(stored, 16)
                sp.wait_ge(stored, 16)


def layout(i):
    a = {k: np.asarray(v) for k, v in i.items()}
    o = {}

    def cols(v):
        v = v.reshape(-1)
        if v.size < D:
            v = np.concatenate([v, np.zeros(D - v.size, v.dtype)])
        return v.reshape(KT, P).T

    o["x"] = a["x"].reshape(TT, P, D)
    o["ctx"] = a["ctx_2048"].reshape(CT, P, D)
    o["ctx_t"] = a["ctx_2048"].reshape(B * CTX, D).T.reshape(KT, P, B * CTX)
    o["cols"] = np.concatenate([cols(a[n]) for n in (
        "L2_ffn_ln1_w", "L2_ffn_ln2_w", "L3_ffn_router_scale", "L2_xattn_bq", "L2_xattn_bk",
        "L3_xattn_ln_g", "L3_xattn_ln_b", "L3_xattn_q_b", "L3_xattn_k_b")], axis=1)
    o["rows"] = np.concatenate([a[n].reshape(-1) for n in (
        "g_xattn", "g_ffn", "L2_xattn_bv", "L2_xattn_bo", "L3_xattn_o_b", "L3_xattn_v_b",
        "L3_ffn_per_expert_scale")])[None]
    o["att_mask"] = a["mask_BxS2_ff1"].reshape(CT, P).T
    o["l0_w"] = np.stack([a["L0_xattn_" + n].T.reshape(KT, P, D) for n in ("wq", "wk", "wv", "wo")])
    o["l2_w"] = np.stack([a["L2_xattn_" + n].T.reshape(KT, P, D) for n in ("Wq", "Wk", "Wv", "Wo")])
    for name, f in (("fm_q", a["L2_xattn_Wqf"]), ("fm_k", a["L2_xattn_Wkf"])):
        m = np.zeros((P, 512), f.dtype)
        for h in range(8):
            m[16 * h:16 * h + 16, 64 * h:64 * h + 64] = f.T
        o[name] = m

    def fp4_gate(w):
        return w.reshape(8, P, 2, P).transpose(0, 3, 2, 1)
    g, u = fp4_gate(a["L0_ffn_gate_W_packed"]), fp4_gate(a["L0_ffn_up_W_packed"])
    dn = a["L0_ffn_down_W_packed"].reshape(D, 8, P).transpose(1, 2, 0)
    o["fp4_w"] = np.concatenate([np.stack([g, u], 3).reshape(8, P, 512), dn], axis=2)
    gs = a["L0_ffn_gate_scales"].reshape(8, P, 2, 8).transpose(0, 3, 2, 1)
    us = a["L0_ffn_up_scales"].reshape(8, P, 2, 8).transpose(0, 3, 2, 1)
    ds = a["L0_ffn_down_scales"].reshape(D, 8, 8).transpose(1, 2, 0)
    o["fp4_s"] = np.concatenate([np.stack([gs, us], 3).reshape(8, 8, 512), ds], axis=2)

    def tiles(gate, up, down, n):
        pad = n * P - gate.shape[0]
        gate, up, down = (np.concatenate([m, np.zeros((pad, D), m.dtype)]) for m in (gate, up, down))
        gu = np.stack([gate, up]).reshape(2, n, P, KT, P).transpose(1, 4, 3, 0, 2).reshape(n, P, 4 * P)
        return np.concatenate([gu, down.reshape(n, P, D)], axis=2)

    def moe(gw, uw, dw, sg, su, sd, n):
        return tiles(np.concatenate([gw.reshape(-1, D), sg]), np.concatenate([uw.reshape(-1, D), su]),
                     np.concatenate([dw.transpose(0, 2, 1).reshape(-1, D), sd.T]), n)
    l1 = moe(*(a["L1_ffn_" + n] for n in ("gate_w", "up_w", "down_w", "sh_gate_w", "sh_up_w", "sh_down_w")), 14)
    l2 = moe(*(a["L2_ffn_" + n] for n in ("eg_w", "eu_w", "ed_w", "sg_w", "su_w", "sd_w")), 25)
    gu = a["L3_ffn_gate_up"].transpose(0, 2, 1)
    l3 = tiles(gu[:, 0:256].reshape(-1, D), gu[:, 256:512].reshape(-1, D), a["L3_ffn_down"].reshape(-1, D), 16)
    o["moe_w"] = np.concatenate([l1, l2, l3])
    rt = [a["L1_ffn_gate_weight"].T, a["L2_ffn_gate_w"].T, a["L3_ffn_gate_w"]]
    o["routers"] = np.concatenate([r.reshape(KT, P, -1) for r in rt], axis=2)
    sel = np.zeros((P, MOE_TILES * P), np.uint16)
    for name, (n, e, per) in MOE.items():
        unit = np.arange(n * P)
        real = {"l1": 1760, "l2": 3168, "l3": 2048}[name]
        for part in range(3):
            row = np.minimum(unit // per, e) + part * (e + 1)
            sel[row[:real], MOE_AT[name] * P + unit[:real]] = ONE_BF16
    o["sel"] = sel
    stack = np.zeros((P, 8, 3, 6, HD), np.uint16)
    for row, part in enumerate(Q_PARTS):
        for unit in range(P):
            stack[unit, unit // HD, part, row, unit % HD] = ONE_BF16
    o["stack_sel"] = stack.reshape(P, 8 * 3 * STACK)

    def heads(w):
        return w.reshape(KT, P, 8, 256).transpose(2, 1, 0, 3).reshape(8, P, 512)
    wo = a["L2_ffn_wo"].reshape(8, 2, P, D).transpose(0, 2, 1, 3).reshape(8, P, 512)
    o["l2a_w"] = np.concatenate([heads(a["L2_ffn_" + n]) for n in ("wq", "wk", "wv")] + [wo], axis=2)
    o["l3_w"] = np.concatenate([a["L3_xattn_" + n].T.reshape(KT, P, -1) for n in ("q_w", "k_w", "v_w", "o_w")], axis=2)
    return {k: np.ascontiguousarray(v) for k, v in o.items()}


def kernel(**inputs):
    import concourse.bacc as _bacc
    from concourse.bass_utils import run_bass_kernel_spmd as _run

    arrays = layout(inputs)
    nc = _bacc.Bacc("TRN2", target_bir_lowering=False, num_devices=1)
    d = {k: nc.dram_tensor("in_" + k, v.shape, mybir.dt.from_np(v.dtype), kind="ExternalInput").ap()
         for k, v in arrays.items()}
    out = nc.dram_tensor("out_x", (TT, P, D), F32, kind="ExternalOutput").ap()
    build(nc, d, out)
    r = _run(nc, [{"in_" + k: v for k, v in arrays.items()}], core_ids=[0])
    return np.asarray(r.results[0]["out_x"]).reshape(B, S, D)
```
